# Optimizing a Trainium2 kernel written in Bass

```python
import numpy as np
import jax
import jax.numpy as jnp

def _softmax(x, axis=-1):
    return jax.nn.softmax(x, axis=axis)

def _gelu(x):
    return jax.nn.gelu(x, approximate=True)

def _silu(x):
    return jax.nn.silu(x)

def _sigmoid(x):
    return jax.nn.sigmoid(x)

def _layernorm(x, axis=-1, eps=1e-05):
    m = jnp.mean(x, axis=axis, keepdims=True)
    v = jnp.var(x, axis=axis, keepdims=True)
    return (x - m) / jnp.sqrt(v + eps)

def _scatter_add(tgt, idx, src, axis=0):
    return tgt.at[idx].add(src)

def _segment_sum(src, seg, n):
    return jax.ops.segment_sum(src, seg, n)
kernel_name = 'mk_xattn_ffn_d2_seqx_r4_f485ff'

def setup_inputs(seed: int=0):
    np.random.seed(seed)
    _w = jnp.asarray

    def _rec_inputs():
        import jax
        import jax.numpy as jnp
        _rk = jax.random.key(seed)
        x = -0.0002928 + 1 * jax.random.normal(jax.random.fold_in(_rk, 1), (2, 1024, 256), jnp.float32)
        _lenS = 1024 - jax.random.randint(jax.random.fold_in(_rk, 7), (2,), 0, max(1, 1024 // 4) + 1, jnp.int32)
        _lenS2 = 154 - jax.random.randint(jax.random.fold_in(_rk, 8), (2,), 0, max(1, 154 // 4) + 1, jnp.int32)
        _ctx_1024P = jax.random.normal(jax.random.fold_in(_rk, 11), (2, 16, 256), jnp.float32)
        _ctx_1024c = jax.random.dirichlet(jax.random.fold_in(_rk, 511), 0.3 * jnp.ones((16,), jnp.float32), (2, 154))
        _ctx_1024t = jnp.einsum('bsk,bkd->bsd', _ctx_1024c, _ctx_1024P)
        _ctx_1024t = _ctx_1024t * jax.lax.rsqrt(jnp.mean(jnp.square(_ctx_1024t)) + 1e-12) * 0.953939
        ctx_1024 = -1.39393e-06 + 0.999914 * (_ctx_1024t + 0.3 * jax.random.normal(jax.random.fold_in(_rk, 611), (2, 154, 256), jnp.float32))
        return (x, ctx_1024)
    x, ctx_1024 = _rec_inputs()

    def _L0_xattn_setup():
        import jax, jax.numpy as jnp
        import numpy as np
        EMBED = 256
        HEADS = 16
        HEAD_DIM = EMBED // HEADS
        key = jax.random.key(seed)
        ks = jax.random.split(key, 11)
        B, S = (2, 512)
        scale = 1.0 / np.sqrt(EMBED)
        inp = {'Q': jax.random.normal(ks[0], (B, S, EMBED), jnp.float32), 'K': jax.random.normal(ks[1], (B, S, EMBED), jnp.float32), 'V': jax.random.normal(ks[2], (B, S, EMBED), jnp.float32), 'Wq': jax.random.normal(ks[3], (EMBED, EMBED), jnp.float32) * scale, 'bq': jnp.zeros((EMBED,), jnp.float32), 'Wk': jax.random.normal(ks[4], (EMBED, EMBED), jnp.float32) * scale, 'bk': jnp.zeros((EMBED,), jnp.float32), 'Wv': jax.random.normal(ks[5], (EMBED, EMBED), jnp.float32) * scale, 'bv': jnp.zeros((EMBED,), jnp.float32), 'Wo': jax.random.normal(ks[6], (EMBED, EMBED), jnp.float32) * scale, 'bo': jnp.zeros((EMBED,), jnp.float32)}
        return inp
    _L0_xattn_all = _L0_xattn_setup()
    _L0_xattn_in = {k: v for k, v in _L0_xattn_all.items() if k in ('Wq', 'bq', 'Wk', 'bk', 'Wv', 'bv', 'Wo', 'bo')}
    del _L0_xattn_all

    def _L0_ffn_setup():
        import jax, jax.numpy as jnp
        import numpy as np
        B, S, H, F, E = (4, 512, 256, 1024, 8)
        key = jax.random.key(seed)
        ks = jax.random.split(key, 8)
        s = 1.0 / np.sqrt(H)
        sf = 1.0 / np.sqrt(F)
        return {'x': jax.random.normal(ks[0], (B, S, H), jnp.float32), 'wr': jax.random.uniform(ks[1], (H, E), jnp.float32, -s, s), 'br': jax.random.uniform(ks[2], (E,), jnp.float32, -s, s), 'w1': jax.random.uniform(ks[3], (E, H, F), jnp.float32, -s, s), 'b1': jax.random.uniform(ks[4], (E, F), jnp.float32, -s, s), 'w2': jax.random.uniform(ks[5], (E, F, H), jnp.float32, -sf, sf), 'b2': jax.random.uniform(ks[6], (E, H), jnp.float32, -sf, sf)}
    _L0_ffn_all = _L0_ffn_setup()
    _L0_ffn_in = {k: v for k, v in _L0_ffn_all.items() if k in ('wr', 'br', 'w1', 'b1', 'w2', 'b2')}
    del _L0_ffn_all

    def _L1_xattn_setup():
        import jax, jax.numpy as jnp
        import numpy as np
        DIM = 256
        HEADS = 16
        DIM_HEAD = 64
        INNER = HEADS * DIM_HEAD
        MLP = 1024
        EPS = 1e-05

        def _layernorm(x, g, b):
            mu = jnp.mean(x, axis=-1, keepdims=True)
            var = jnp.mean(jnp.square(x - mu), axis=-1, keepdims=True)
            return (x - mu) * jax.lax.rsqrt(var + EPS) * g + b

        def _l2norm(x):
            n = jnp.sqrt(jnp.sum(jnp.square(x), axis=-1, keepdims=True))
            return x / jnp.maximum(n, 1e-12)

        def _split_heads(x, B, N):
            return x.reshape(B, N, HEADS, DIM_HEAD).transpose(0, 2, 1, 3)
        key = jax.random.key(seed)
        ks = jax.random.split(key, 16)
        B, N = (4, 512)
        s = 0.02
        return {'Q': jax.random.normal(ks[0], (B, N, DIM), jnp.float32), 'K': jax.random.normal(ks[1], (B, N, DIM), jnp.float32), 'V': jax.random.normal(ks[2], (B, N, DIM), jnp.float32), 'wq': jax.random.normal(ks[3], (DIM, INNER), jnp.float32) * s, 'wk': jax.random.normal(ks[4], (DIM, INNER), jnp.float32) * s, 'wv': jax.random.normal(ks[5], (DIM, INNER), jnp.float32) * s, 'wo': jax.random.normal(ks[6], (INNER, DIM), jnp.float32) * s, 'bo': jnp.zeros((DIM,), jnp.float32), 'w1': jax.random.normal(ks[7], (DIM, MLP), jnp.float32) * s, 'b1': jnp.zeros((MLP,), jnp.float32), 'w2': jax.random.normal(ks[8], (MLP, DIM), jnp.float32) * s, 'b2': jnp.zeros((DIM,), jnp.float32), 'ln1_g': jnp.ones((DIM,), jnp.float32), 'ln1_b': jnp.zeros((DIM,), jnp.float32), 'ln2_g': jnp.ones((DIM,), jnp.float32), 'ln2_b': jnp.zeros((DIM,), jnp.float32)}
    _L1_xattn_all = _L1_xattn_setup()
    _L1_xattn_in = {k: v for k, v in _L1_xattn_all.items() if k in ('wq', 'wk', 'wv', 'wo', 'bo', 'w1', 'b1', 'w2', 'b2', 'ln1_g', 'ln1_b', 'ln2_g', 'ln2_b')}
    del _L1_xattn_all

    def _L1_ffn_setup():
        import math
        import jax, jax.numpy as jnp
        import numpy as np
        B, S, H = (4, 1024, 256)
        FFN = 1024
        E = 16
        N_ZERO, N_COPY, N_CONST = (1, 1, 2)
        MLP_START = N_ZERO + N_COPY + N_CONST
        E_MLP = E - MLP_START
        TOP_K = 2
        CAP_FACTOR = 1.0
        EPS = 1e-05

        def _rmsnorm(x, w, eps):
            return x * jax.lax.rsqrt(jnp.mean(x * x, axis=-1, keepdims=True) + eps) * w
        key = jax.random.key(seed)
        ks = jax.random.split(key, 6)
        std = jnp.float32(0.02)
        return {'x': jax.random.normal(ks[0], (B, S, H), jnp.float32), 'norm_weight': jnp.ones((H,), jnp.float32), 'router_weight': jax.random.normal(ks[1], (E, H), jnp.float32) * std, 'router_bias': jnp.zeros((E,), jnp.float32), 'fc1_weight': jax.random.normal(ks[2], (E_MLP, FFN, H), jnp.float32) * std, 'fc1_bias': jnp.zeros((E_MLP, FFN), jnp.float32), 'fc2_weight': jax.random.normal(ks[3], (E_MLP, H, FFN), jnp.float32) * std, 'fc2_bias': jnp.zeros((E_MLP, H), jnp.float32), 'constant_vectors': jax.random.normal(ks[4], (N_CONST, H), jnp.float32) * std}
    _L1_ffn_all = _L1_ffn_setup()
    _L1_ffn_in = {k: v for k, v in _L1_ffn_all.items() if k in ('norm_weight', 'router_weight', 'router_bias', 'fc1_weight', 'fc1_bias', 'fc2_weight', 'fc2_bias', 'constant_vectors')}
    del _L1_ffn_all
    return {'x': x, 'ctx_1024': ctx_1024, 'L0_xattn_Wq': _L0_xattn_in['Wq'], 'L0_xattn_bq': _L0_xattn_in['bq'], 'L0_xattn_Wk': _L0_xattn_in['Wk'], 'L0_xattn_bk': _L0_xattn_in['bk'], 'L0_xattn_Wv': _L0_xattn_in['Wv'], 'L0_xattn_bv': _L0_xattn_in['bv'], 'L0_xattn_Wo': _L0_xattn_in['Wo'], 'L0_xattn_bo': _L0_xattn_in['bo'], 'L0_ffn_wr': _L0_ffn_in['wr'], 'L0_ffn_br': _L0_ffn_in['br'], 'L0_ffn_w1': _L0_ffn_in['w1'], 'L0_ffn_b1': _L0_ffn_in['b1'], 'L0_ffn_w2': _L0_ffn_in['w2'], 'L0_ffn_b2': _L0_ffn_in['b2'], 'L1_xattn_wq': _L1_xattn_in['wq'], 'L1_xattn_wk': _L1_xattn_in['wk'], 'L1_xattn_wv': _L1_xattn_in['wv'], 'L1_xattn_wo': _L1_xattn_in['wo'], 'L1_xattn_bo': _L1_xattn_in['bo'], 'L1_xattn_w1': _L1_xattn_in['w1'], 'L1_xattn_b1': _L1_xattn_in['b1'], 'L1_xattn_w2': _L1_xattn_in['w2'], 'L1_xattn_b2': _L1_xattn_in['b2'], 'L1_xattn_ln1_g': _L1_xattn_in['ln1_g'], 'L1_xattn_ln1_b': _L1_xattn_in['ln1_b'], 'L1_xattn_ln2_g': _L1_xattn_in['ln2_g'], 'L1_xattn_ln2_b': _L1_xattn_in['ln2_b'], 'L1_ffn_norm_weight': _L1_ffn_in['norm_weight'], 'L1_ffn_router_weight': _L1_ffn_in['router_weight'], 'L1_ffn_router_bias': _L1_ffn_in['router_bias'], 'L1_ffn_fc1_weight': _L1_ffn_in['fc1_weight'], 'L1_ffn_fc1_bias': _L1_ffn_in['fc1_bias'], 'L1_ffn_fc2_weight': _L1_ffn_in['fc2_weight'], 'L1_ffn_fc2_bias': _L1_ffn_in['fc2_bias'], 'L1_ffn_constant_vectors': _L1_ffn_in['constant_vectors']}

def reference(x, ctx_1024, L0_xattn_Wq, L0_xattn_bq, L0_xattn_Wk, L0_xattn_bk, L0_xattn_Wv, L0_xattn_bv, L0_xattn_Wo, L0_xattn_bo, L0_ffn_wr, L0_ffn_br, L0_ffn_w1, L0_ffn_b1, L0_ffn_w2, L0_ffn_b2, L1_xattn_wq, L1_xattn_wk, L1_xattn_wv, L1_xattn_wo, L1_xattn_bo, L1_xattn_w1, L1_xattn_b1, L1_xattn_w2, L1_xattn_b2, L1_xattn_ln1_g, L1_xattn_ln1_b, L1_xattn_ln2_g, L1_xattn_ln2_b, L1_ffn_norm_weight, L1_ffn_router_weight, L1_ffn_router_bias, L1_ffn_fc1_weight, L1_ffn_fc1_bias, L1_ffn_fc2_weight, L1_ffn_fc2_bias, L1_ffn_constant_vectors):
    import jax
    import jax.numpy as jnp

    def _L0_xattn_ref(Q, K, V, Wq, bq, Wk, bk, Wv, bv, Wo, bo):
        import jax, jax.numpy as jnp
        import numpy as np
        EMBED = 256
        HEADS = 16
        HEAD_DIM = EMBED // HEADS
        B, Sq, _ = Q.shape
        Sk = K.shape[1]
        q = Q @ Wq + bq
        k = K @ Wk + bk
        v = V @ Wv + bv
        q = q.reshape(B, Sq, HEADS, HEAD_DIM).transpose(0, 2, 1, 3)
        k = k.reshape(B, Sk, HEADS, HEAD_DIM).transpose(0, 2, 1, 3)
        v = v.reshape(B, Sk, HEADS, HEAD_DIM).transpose(0, 2, 1, 3)
        scores = jnp.einsum('bhqd,bhkd->bhqk', q, k) / jnp.sqrt(jnp.float32(HEAD_DIM))
        attn = jax.nn.softmax(scores, axis=-1)
        out = jnp.einsum('bhqk,bhkd->bhqd', attn, v)
        out = out.transpose(0, 2, 1, 3).reshape(B, Sq, EMBED)
        return out @ Wo + bo

    def _L0_ffn_ref(x, wr, br, w1, b1, w2, b2):
        import jax, jax.numpy as jnp
        import numpy as np
        B, S, H, F, E = (4, 512, 256, 1024, 8)
        scores = jnp.einsum('bsh,he->bse', x, wr) + br
        expert_id = jnp.argmax(scores, axis=-1)
        h = jnp.einsum('bsh,ehf->ebsf', x, w1) + b1[:, None, None, :]
        h = jax.nn.gelu(h, approximate=False)
        y = jnp.einsum('ebsf,efh->ebsh', h, w2) + b2[:, None, None, :]
        one_hot = jax.nn.one_hot(expert_id, E, dtype=x.dtype)
        out = jnp.einsum('ebsh,bse->bsh', y, one_hot)
        return out

    def _L1_xattn_ref(Q, K, V, wq, wk, wv, wo, bo, w1, b1, w2, b2, ln1_g, ln1_b, ln2_g, ln2_b):
        import jax, jax.numpy as jnp
        import numpy as np
        DIM = 256
        HEADS = 16
        DIM_HEAD = 64
        INNER = HEADS * DIM_HEAD
        MLP = 1024
        EPS = 1e-05

        def _layernorm(x, g, b):
            mu = jnp.mean(x, axis=-1, keepdims=True)
            var = jnp.mean(jnp.square(x - mu), axis=-1, keepdims=True)
            return (x - mu) * jax.lax.rsqrt(var + EPS) * g + b

        def _l2norm(x):
            n = jnp.sqrt(jnp.sum(jnp.square(x), axis=-1, keepdims=True))
            return x / jnp.maximum(n, 1e-12)

        def _split_heads(x, B, N):
            return x.reshape(B, N, HEADS, DIM_HEAD).transpose(0, 2, 1, 3)
        B, Nq, _ = Q.shape
        Nk = K.shape[1]
        Qn = _layernorm(Q, ln1_g, ln1_b)
        Kn = _layernorm(K, ln1_g, ln1_b)
        Vn = _layernorm(V, ln1_g, ln1_b)
        q = _split_heads(Qn @ wq, B, Nq)
        k = _split_heads(Kn @ wk, B, Nk)
        v = _split_heads(Vn @ wv, B, Nk)
        qn = _l2norm(q)
        kn = _l2norm(k)
        attn = jnp.einsum('bhqd,bhkd->bhqk', qn, kn)
        out = jnp.einsum('bhqk,bhkd->bhqd', attn, v)
        out = out.transpose(0, 2, 1, 3).reshape(B, Nq, INNER)
        x = Q + out @ wo + bo
        xn = _layernorm(x, ln2_g, ln2_b)
        h = jax.nn.gelu(xn @ w1 + b1, approximate=False)
        return x + h @ w2 + b2

    def _L1_ffn_ref(x, norm_weight, router_weight, router_bias, fc1_weight, fc1_bias, fc2_weight, fc2_bias, constant_vectors):
        import math
        import jax, jax.numpy as jnp
        import numpy as np
        B, S, H = (4, 1024, 256)
        FFN = 1024
        E = 16
        N_ZERO, N_COPY, N_CONST = (1, 1, 2)
        MLP_START = N_ZERO + N_COPY + N_CONST
        E_MLP = E - MLP_START
        TOP_K = 2
        CAP_FACTOR = 1.0
        EPS = 1e-05

        def _rmsnorm(x, w, eps):
            return x * jax.lax.rsqrt(jnp.mean(x * x, axis=-1, keepdims=True) + eps) * w
        Bsz, Sl, Hd = x.shape
        N = Bsz * Sl
        CAP = int(math.ceil(CAP_FACTOR * N * TOP_K / E))
        x_flat = x.reshape(N, Hd)
        xn = _rmsnorm(x_flat, norm_weight, EPS)
        logits = xn @ router_weight.T + router_bias
        probs = jax.nn.softmax(logits, axis=-1)
        gate_vals, expert_idx = jax.lax.top_k(probs, TOP_K)
        e_flat = expert_idx.reshape(-1)
        g_flat = gate_vals.reshape(-1)
        oh = jax.nn.one_hot(e_flat, E, dtype=jnp.int32)
        pos = jnp.sum(jnp.cumsum(oh, axis=0) * oh, axis=-1) - 1
        keep = pos < CAP
        slot = jnp.clip(pos, 0, CAP - 1)
        tok = jnp.repeat(jnp.arange(N), TOP_K)
        contrib = xn[tok] * keep[:, None].astype(x.dtype)
        dispatch = jnp.zeros((E, CAP, Hd), x.dtype).at[e_flat, slot].add(contrib)
        out_zero = jnp.zeros((N_ZERO, CAP, Hd), x.dtype)
        out_copy = dispatch[N_ZERO:N_ZERO + N_COPY]
        out_const = jnp.broadcast_to(constant_vectors[:, None, :], (N_CONST, CAP, Hd))
        dm = dispatch[MLP_START:]
        h = jnp.einsum('ech,efh->ecf', dm, fc1_weight) + fc1_bias[:, None, :]
        h = jax.nn.gelu(h, approximate=False)
        out_mlp = jnp.einsum('ecf,ehf->ech', h, fc2_weight) + fc2_bias[:, None, :]
        expert_out = jnp.concatenate([out_zero, out_copy, out_const, out_mlp], axis=0)
        gathered = expert_out[e_flat, slot]
        w = g_flat * keep.astype(g_flat.dtype)
        combined = (gathered * w[:, None]).reshape(N, TOP_K, Hd).sum(axis=1)
        gate_sums = w.reshape(N, TOP_K).sum(axis=1, keepdims=True)
        out = combined / jnp.where(gate_sums > 0, gate_sums, 1.0)
        return out.reshape(Bsz, Sl, Hd)
    x = x + _L0_xattn_ref(_layernorm(x, axis=-1), ctx_1024, ctx_1024, L0_xattn_Wq, L0_xattn_bq, L0_xattn_Wk, L0_xattn_bk, L0_xattn_Wv, L0_xattn_bv, L0_xattn_Wo, L0_xattn_bo)
    x = x + _L0_ffn_ref(_layernorm(x, axis=-1), L0_ffn_wr, L0_ffn_br, L0_ffn_w1, L0_ffn_b1, L0_ffn_w2, L0_ffn_b2)
    x = x + _L1_xattn_ref(_layernorm(x, axis=-1), ctx_1024, ctx_1024, L1_xattn_wq, L1_xattn_wk, L1_xattn_wv, L1_xattn_wo, L1_xattn_bo, L1_xattn_w1, L1_xattn_b1, L1_xattn_w2, L1_xattn_b2, L1_xattn_ln1_g, L1_xattn_ln1_b, L1_xattn_ln2_g, L1_xattn_ln2_b)
    x = x + _L1_ffn_ref(_layernorm(x, axis=-1), L1_ffn_norm_weight, L1_ffn_router_weight, L1_ffn_router_bias, L1_ffn_fc1_weight, L1_ffn_fc1_bias, L1_ffn_fc2_weight, L1_ffn_fc2_bias, L1_ffn_constant_vectors)
    return x

_drawn_inputs = setup_inputs


def setup_inputs(seed=0):
    import zlib

    import numpy as np

    out = dict(_drawn_inputs(seed))
    spreads = {'L0_xattn_bq': (0.0, 0.1),
     'L0_xattn_bk': (0.0, 2.0),
     'L0_xattn_bv': (0.0, 0.1),
     'L0_xattn_bo': (0.0, 0.1),
     'L1_xattn_bo': (0.0, 0.1),
     'L1_xattn_b1': (0.0, 0.413),
     'L1_xattn_b2': (0.0, 0.1),
     'L1_xattn_ln1_g': (1.0, 0.2),
     'L1_xattn_ln1_b': (0.0, 0.1),
     'L1_xattn_ln2_g': (1.0, 0.6),
     'L1_xattn_ln2_b': (0.0, 0.8),
     'L1_ffn_norm_weight': (1.0, 0.2),
     'L1_ffn_router_bias': (0.0, 0.1),
     'L1_ffn_fc1_bias': (0.0, 0.8),
     'L1_ffn_fc2_bias': (0.0, 0.301)}
    factors = {'L0_ffn_b1': 3.868, 'L0_ffn_b2': 2.894, 'L1_ffn_constant_vectors': 25.168}
    for name, (base, spread) in spreads.items():
        noise = np.random.default_rng([zlib.crc32(name.encode()), seed]).standard_normal(out[name].shape)
        drawn = base * np.exp(spread * noise) if base else spread * noise
        out[name] = jnp.asarray(drawn.astype(out[name].dtype))
    for name, factor in factors.items():
        out[name] = (out[name] * factor).astype(out[name].dtype)
    return out
```

```python
from contextlib import ExitStack

import concourse.bass as bass
from concourse import mybir

F32 = mybir.dt.float32
I32 = mybir.dt.int32
U32 = mybir.dt.uint32
ACT = mybir.ActivationFunctionType
ALU = mybir.AluOpType
X_AXIS = mybir.AxisListType.X

P = 128
D = 256
KC = D // P
BATCH, SEQ, CTX = 2, 1024, 154
N = BATCH * SEQ
TILES = N // P
TPB = SEQ // P
CTX_SPLIT = ((0, P), (P, CTX - P))
EPS = 1e-5

H0, HD0 = 16, 16
HALF_HEADS = P // HD0
HALVES = H0 // HALF_HEADS
GROUP = 4
GROUPS = H0 // GROUP
GW = GROUP * CTX
ROWS = HALF_HEADS * CTX
CHUNKS = -(-ROWS // P)
PADDED = CHUNKS * P
FILLS = ((0, 4), (4, 4), (8, CHUNKS - 8))
NF = len(FILLS)
VW = HD0 + 1
PAIR0 = [min(P * c // CTX, HALF_HEADS - 2) for c in range(CHUNKS)]

E0, F = 8, 1024
FC = F // P
SLOT_TILES0 = N // P + E0
ROWS0 = SLOT_TILES0 * P

H1, HD1 = 16, 64
INNER = H1 * HD1
IC = INNER // P

E1, PLAIN = 16, 4
MLPS = E1 - PLAIN
CAP = N * 2 // E1
ROWS1 = MLPS * CAP
ZM = 4
SKIP = 1 << 20

SMALL = (
    ("bq0", (P, KC)), ("bk0", (P, KC)), ("bvg0", (P, HALVES, CHUNKS, 2 * HD0)),
    ("bo0", (P, D)), ("vmask", (P, CHUNKS, 2)), ("headmask", (P, HALF_HEADS)),
    ("pairmask", (P, P)), ("g1", (P, KC)), ("be1", (P, KC)), ("g2", (P, KC)),
    ("be2", (P, KC)), ("bo1", (P, D)), ("mb1", (P, FC)), ("mb2", (P, D)),
    ("wr0", (P, KC, E0)), ("br0", (P, E0)), ("wr1", (P, KC, E1)), ("br1", (P, E1)),
    ("nw", (P, D)), ("cv", (P, 2, D)), ("tri", (P, P)), ("ones", (P, P)), ("ident", (P, P)),
    ("order0", (P, E0)), ("order1", (P, E1)), ("thresh0", (P, TILES)),
    ("before0", (P, E0, E0)), ("tile_no", (P, SLOT_TILES0)), ("base1", (P, E1)),
)
BROADCAST = {"bo0", "bo1", "mb2", "br0", "br1", "nw", "cv", "bvg0", "order0", "order1", "thresh0",
             "before0", "tile_no", "base1"}


class Own:

    def __init__(self, eng, sem):
        self.eng, self.sem, self.done, self.ahead = eng, sem, 0, 0

    def then(self, ins):
        ins.then_inc(self.sem, 1)
        self.done += 1
        self.eng.wait_ge(self.sem, self.ahead + self.done)

    def enter(self, i, first, per):
        self.base, self.per = self.done, per
        self.ahead = (i - first) * per

    def leave(self, turns):
        assert self.done - self.base == self.per, (self.done - self.base, self.per)
        self.done = self.base + turns * self.per
        self.ahead = 0


class Core:
    pass


def at_least(eng, sem, value):
    if not isinstance(value, int) or value > 0:
        eng.wait_ge(sem, value)


def normalise_vector(k, dve, own, sums, powers, each=None):
    nc = k.nc
    for t in range(TILES):
        last = nc.vector.bn_stats(k.stats[:, t, :], k.X[:, t, :])
    own.then(last)
    for t in range(TILES):
        last = nc.vector.bn_aggr(k.mv[:, t, :], k.stats[:, t, :])
    own.then(last)
    nc.vector.tensor_scalar(k.rstd[:, :], k.mv[:, :, 1], EPS, None, ALU.add).then_inc(sums, 1)
    dve.wait_ge(powers, 1)
    for t in range(TILES):
        last = nc.vector.tensor_scalar(k.XN[:, t, :], k.X[:, t, :], k.mv[:, t, 0:1],
                                       k.rstd[:, t:t + 1], ALU.subtract, ALU.mult)
        if each is not None:
            last.then_inc(each, 1)
    return last


def inverse_roots(k, pool, sums, powers):
    pool.wait_ge(sums, 1)
    k.nc.gpsimd.tensor_tensor(k.rstd[:, :], k.rstd[:, :], k.half_neg[:, 0:TILES],
                              ALU.pow).then_inc(powers, 1)


def context_stage(k):
    nc = k.nc
    with ExitStack() as own_memory:
        def sb(name, shape, dt=F32):
            return own_memory.enter_context(nc.sbuf_tensor(name, shape, dt))

        def sem(name):
            return own_memory.enter_context(nc.semaphore(name))

        ctxT = sb("ctxT", [P, KC, BATCH, CTX])
        ctxTr = sb("ctxTr", [P, KC, BATCH, PADDED])
        C = sb("C", [P, BATCH, 2, D])
        wk0 = sb("wk0", [P, KC, D])
        wvg0 = sb("wvg0", [P, KC, HALVES, CHUNKS, 2 * HD0])
        wk1 = sb("wk1", [P, KC, INNER])
        wv1 = sb("wv1", [P, KC, INNER])
        wo1 = sb("wo1", [P, IC, D])
        kT = sb("kT", [P, BATCH, HALVES, CTX])
        vtmp = sb("vtmp", [P, BATCH, HALVES, CHUNKS, 2 * HD0])
        cst = sb("cst", [P, BATCH, 2, 6])
        cmv = sb("cmv", [P, BATCH, 2, 2])
        crs = sb("crs", [P, BATCH, 2])
        cnT = sb("cnT", [P, KC, BATCH, CTX])
        kn = sb("kn", [P, BATCH, 2, INNER])
        vn = sb("vn", [P, BATCH, 2, INNER])
        sq = sb("sq", [P, INNER])
        kvT = sq[:, :].rearrange("p (n k) -> p n k", k=P)
        ss = sb("ss", [P, BATCH, 2, H1])

        small_in, ctx_in, wctx_in, x_in = sem("small_in"), sem("ctx_in"), sem("wctx_in"), sem("x_in")
        dve_own = sem("dve_own")
        zero_set, zeroed, consts_set = sem("zero_set"), sem("zeroed"), sem("consts_set")
        k0_made, v0_made, ctx_sums, ctx_roots = sem("k0_made"), sem("v0_made"), sem("ctx_sums"), sem("ctx_roots")
        c_ready, cT_made, cT_ready = sem("c_ready"), sem("cT_made"), sem("cT_ready")
        kv_made, kv_taken, sq_made, sq_used = sem("kv_made"), sem("kv_taken"), sem("sq_made"), sem("sq_used")
        k_sums, k_roots, kn_ready = sem("k_sums"), sem("k_roots"), sem("kn_ready")
        kvT_made, kvT_ready, m_made, m_taken = sem("kvT_made"), sem("kvT_ready"), sem("m_made"), sem("m_taken")
        x_sums, x_roots, x_kept, xb = sem("x_sums"), sem("x_roots"), sem("x_kept"), sem("xb")
        zeros = sb("zeros", [P, ZM * D])

        with nc.Block() as block:
            @block.sync
            def _(sp):
                sp.dma_start(ctxT[:, :, :, :], k.ap["ctxT"]).then_inc(ctx_in, 16)
                sp.dma_start(wk0[:, :, :], k.ap["wk0"]).then_inc(ctx_in, 16)
                sp.dma_start(C[:, :, :, :], k.ap["ctx"]).then_inc(ctx_in, 16)
                sp.dma_start(k.X[:, :, :], k.ap["x"].rearrange("(t p) d -> p t d", p=P)).then_inc(x_in, 16)
                sp.dma_start(ctxTr[:, :, :, :], k.ap["ctxTr"]).then_inc(ctx_in, 16)
                sp.dma_start(wvg0[:, :, :, :, :], k.ap["wvg0"]).then_inc(ctx_in, 16)
                sp.dma_start(wk1[:, :, :], k.ap["wk1"]).then_inc(wctx_in, 16)
                sp.dma_start(wv1[:, :, :], k.ap["wv1"]).then_inc(wctx_in, 16)
                sp.dma_start(wo1[:, :, :], k.ap["wo1"]).then_inc(wctx_in, 16)
                sp.dma_start(k.wq0[:, :, :], k.ap["wq0"]).then_inc(k.w0_in, 16)
                sp.dma_start(k.wo0[:, :, :], k.ap["wo0"]).then_inc(k.w0_in, 16)
                sp.wait_ge(zero_set, 1)
                for rows, buffer in ((ROWS0, k.slots0), (ROWS1, k.slots1)):
                    for a in range(0, rows, ZM * P):
                        m = min(ZM, (rows - a) // P)
                        sp.dma_start(buffer[a:a + m * P, :].rearrange("(p m) d -> p (m d)", m=m),
                                     zeros[:, 0:m * D]).then_inc(zeroed, 16)
                sp.wait_ge(zeroed, 16 * -(-ROWS0 // (ZM * P)) + 16 * -(-ROWS1 // (ZM * P)))
                sp.wait_ge(k.w0_in, 32)

            @block.scalar
            def _(act):
                for name, shape in SMALL:
                    to = k.small[name][(slice(None),) * len(shape)]
                    if len(shape) > 2:
                        to = to.rearrange({3: "p a b -> p (a b)", 4: "p a b c -> p (a b c)"}[len(shape)])
                    src = k.ap[name]
                    if name in BROADCAST:
                        src = src.to_broadcast((P, src.shape[1]))
                    act.dma_start(to, src).then_inc(small_in, 16)
                for n in range(4):
                    b, j = divmod(n, 2)
                    rows = CTX_SPLIT[j][1]
                    act.wait_ge(kv_made, 2 * n + 1)
                    at_least(act, sq_used, n)
                    nc.scalar.activation(sq[0:rows, :], k.PS[0:rows, 0:2, :], ACT.Square).then_inc(sq_made, 1)
                    act.wait_ge(kv_made, 2 * n + 2)
                    nc.scalar.activation(vn[0:rows, b, j, :], k.PS[0:rows, 2:4, :],
                                         ACT.Copy).then_inc(kv_taken, 1)
                act.wait_ge(small_in, 16 * len(SMALL))

            @block.gpsimd
            def _(pool):
                nc.gpsimd.memset(zeros[:, :], 0.0).then_inc(zero_set, 1)
                pool.wait_ge(consts_set, 2)
                inverse_roots(k, pool, x_sums, x_roots)
                pool.wait_ge(ctx_sums, 1)
                nc.gpsimd.tensor_tensor(crs[:, :, :], crs[:, :, :],
                                        k.half_neg[:, 0:4].rearrange("p (b j) -> p b j", b=2),
                                        ALU.pow).then_inc(ctx_roots, 1)
                pool.wait_ge(k_sums, 1)
                nc.gpsimd.tensor_tensor(ss[:, :, :, :], ss[:, :, :, :],
                                        k.half_pos[:, 0:4 * H1].rearrange("p (b j h) -> p b j h", b=2, j=2),
                                        ALU.pow).then_inc(k_roots, 1)
                pool.wait_ge(small_in, 16 * len(SMALL))
                pool.wait_ge(x_kept, 1)
                nc.gpsimd.tensor_tensor(k.X[:, :, :], k.X[:, :, :],
                                        k.small["bo0"][:, :].rearrange("p (a d) -> p a d", a=1)
                                        .to_broadcast((P, TILES, D)), ALU.add).then_inc(xb, 1)

            @block.tensor
            def _(pe):
                pe.wait_ge(ctx_in, 16 * 5)
                for n in range(4):
                    b, h = divmod(n, 2)
                    for c in range(KC):
                        last = nc.tensor.matmul(k.PS[:, 4 + n // 2, (n % 2) * CTX:(n % 2 + 1) * CTX],
                                                wk0[:, c, h * P:(h + 1) * P], ctxT[:, c, b, :],
                                                start=c == 0, stop=c == KC - 1)
                last.then_inc(k0_made, 1)
                for n in range(4):
                    b, h = divmod(n, 2)
                    for i in range(CHUNKS):
                        for c in range(KC):
                            last = nc.tensor.matmul(k.PS[:, n, i * 2 * HD0:(i + 1) * 2 * HD0],
                                                    ctxTr[:, c, b, i * P:(i + 1) * P], wvg0[:, c, h, i, :],
                                                    start=c == 0, stop=c == KC - 1)
                    last.then_inc(v0_made, 1)
                pe.wait_ge(small_in, 16 * len(SMALL))
                pe.wait_ge(c_ready, 1)
                for b in range(BATCH):
                    for j, (a, rows) in enumerate(CTX_SPLIT):
                        for c in range(KC):
                            at = (b * KC + c) * CTX + a
                            last = nc.tensor.transpose(
                                k.PS[:, 6 + b, c * CTX + a:c * CTX + a + rows],
                                C[0:rows, b, j, c * P:(c + 1) * P], k.ident[0:rows, 0:rows])
                last.then_inc(cT_made, 1)
                pe.wait_ge(cT_ready, 1)
                pe.wait_ge(wctx_in, 48)
                pe.wait_ge(k.v0_taken, 4)
                for n in range(4):
                    b, j = divmod(n, 2)
                    a, rows = CTX_SPLIT[j]
                    for w, (weights, taken) in enumerate(((wk1, kn_ready), (wv1, kv_taken))):
                        at_least(pe, taken, n)
                        for q in range(2):
                            for c in range(KC):
                                last = nc.tensor.matmul(k.PS[0:rows, 2 * w + q, :], cnT[:, c, b, a:a + rows],
                                                        weights[:, c, q * 512:(q + 1) * 512],
                                                        start=c == 0, stop=c == KC - 1)
                        last.then_inc(kv_made, 1)
                pe.wait_ge(kn_ready, 5)
                pe.wait_ge(kv_taken, 4)
                def pair_product(n):
                    b, i = divmod(n, IC)
                    at_least(pe, kvT_ready, n - 1)
                    for j, (a, rows) in enumerate(CTX_SPLIT):
                        last = nc.tensor.matmul(k.PS[:, n % 2, 0:P], vn[0:rows, b, j, i * P:(i + 1) * P],
                                                kn[0:rows, b, j, i * P:(i + 1) * P], start=j == 0, stop=j == 1)
                    last.then_inc(kvT_made, 1)

                pair_product(0)
                for n in range(BATCH * IC):
                    if n + 1 < BATCH * IC:
                        pair_product(n + 1)
                    pe.wait_ge(kvT_ready, n + 1)
                    at_least(pe, m_taken, n - 1)
                    nc.tensor.matmul(k.PS[:, 2 + n % 2, 0:D], kvT[:, n % IC, :], wo1[:, n % IC, :],
                                     start=True, stop=True).then_inc(m_made, 1)

            @block.vector
            def _(dve):
                own = Own(dve, dve_own)

                def keep_product(n):
                    b, i = divmod(n, IC)
                    dve.wait_ge(m_made, n + 1)
                    nc.vector.tensor_copy(k.keyval1[:, b, i, :], k.PS[:, 2 + n % 2, 0:D]).then_inc(m_taken, 1)

                nc.vector.memset(k.half_neg[:, :], -0.5).then_inc(consts_set, 1)
                nc.vector.memset(k.half_pos[:, :], 0.5).then_inc(consts_set, 1)
                for h in range(HALVES):
                    nc.vector.memset(k.probs[:, h, ROWS:PADDED], 0.0)
                own.then(nc.vector.memset(crs[:, :, :], 1.0))
                own.then(nc.vector.memset(ss[:, :, :, :], 1.0))
                dve.wait_ge(ctx_in, 16 * 5)
                for b in range(BATCH):
                    for j, (a, rows) in enumerate(CTX_SPLIT):
                        last = nc.vector.bn_stats(cst[0:rows, b, j, :], C[0:rows, b, j, :])
                own.then(last)
                for b in range(BATCH):
                    for j, (a, rows) in enumerate(CTX_SPLIT):
                        last = nc.vector.bn_aggr(cmv[0:rows, b, j, :], cst[0:rows, b, j, :])
                own.then(last)
                for j, (a, rows) in enumerate(CTX_SPLIT):
                    last = nc.vector.tensor_scalar(crs[0:rows, :, j], cmv[0:rows, :, j, 1], EPS, None, ALU.add)
                last.then_inc(ctx_sums, 1)
                dve.wait_ge(x_in, 16)
                dve.wait_ge(small_in, 16 * len(SMALL))
                normalise_vector(k, dve, own, x_sums, x_roots).then_inc(x_kept, 1)
                dve.wait_ge(ctx_roots, 1)
                for b in range(BATCH):
                    for j, (a, rows) in enumerate(CTX_SPLIT):
                        last = nc.vector.tensor_scalar(C[0:rows, b, j, :], C[0:rows, b, j, :],
                                                       cmv[0:rows, b, j, 0:1], crs[0:rows, b, j:j + 1],
                                                       ALU.subtract, ALU.mult)
                last.then_inc(c_ready, 1)
                dve.wait_ge(k0_made, 1)
                for n in range(4):
                    b, h = divmod(n, 2)
                    last = nc.vector.tensor_scalar(kT[:, b, h, :],
                                                   k.PS[:, 4 + n // 2, (n % 2) * CTX:(n % 2 + 1) * CTX],
                                                   k.small["bk0"][:, h:h + 1], None, ALU.add)
                own.then(last)
                for n in range(4):
                    b, h = divmod(n, 2)
                    nc.vector.tensor_tensor(
                        k.keys0[:, b, h, :, :],
                        kT[:, b, h, :].rearrange("p (a k) -> p a k", a=1).to_broadcast((P, HALF_HEADS, CTX)),
                        k.small["headmask"][:, :].rearrange("p (h a) -> p h a", a=1)
                        .to_broadcast((P, HALF_HEADS, CTX)), ALU.mult)
                for n in range(4):
                    b, h = divmod(n, 2)
                    dve.wait_ge(v0_made, n + 1)
                    own.then(nc.vector.tensor_tensor(
                        vtmp[:, b, h, :, :],
                        k.PS[:, n, 0:CHUNKS * 2 * HD0].rearrange("p (i d) -> p i d", i=CHUNKS),
                        k.small["bvg0"][:, h, :, :], ALU.add))
                    dve.sem_inc(k.v0_taken, 1)
                    for w in range(2):
                        mask = k.small["vmask"][:, :, w:w + 1]
                        nc.vector.tensor_tensor(k.values0[:, b, h, :, w, 0:HD0],
                                                vtmp[:, b, h, :, w * HD0:(w + 1) * HD0],
                                                mask.to_broadcast((P, CHUNKS, HD0)), ALU.mult)
                        last = nc.vector.tensor_copy(k.values0[:, b, h, :, w, HD0:VW], mask)
                own.then(last)
                dve.wait_ge(cT_made, 1)
                for b in range(BATCH):
                    for c in range(KC):
                        last = nc.vector.tensor_scalar(cnT[:, c, b, :], k.PS[:, 6 + b, c * CTX:(c + 1) * CTX],
                                                       k.small["g1"][:, c:c + 1], k.small["be1"][:, c:c + 1],
                                                       ALU.mult, ALU.add)
                last.then_inc(cT_ready, 1)
                for n in range(4):
                    b, j = divmod(n, 2)
                    rows = CTX_SPLIT[j][1]
                    dve.wait_ge(sq_made, n + 1)
                    nc.vector.tensor_reduce(ss[0:rows, b, j, :],
                                            sq[0:rows, :].rearrange("p (h d) -> p h d", h=H1),
                                            X_AXIS, ALU.add).then_inc(sq_used, 1)
                    nc.vector.tensor_copy(kn[0:rows, b, j, :], k.PS[0:rows, 0:2, :]).then_inc(kn_ready, 1)
                dve.wait_ge(sq_used, 4)
                dve.wait_ge(kn_ready, 4)
                nc.vector.tensor_scalar(ss[:, :, :, :], ss[:, :, :, :], 0.0, None, ALU.add).then_inc(k_sums, 1)
                dve.wait_ge(k_roots, 1)
                own.then(nc.vector.tensor_scalar(ss[:, :, :, :], ss[:, :, :, :], 1e-12, None, ALU.max))
                own.then(nc.vector.reciprocal(ss[:, :, :, :], ss[:, :, :, :]))
                for n in range(4):
                    b, j = divmod(n, 2)
                    rows = CTX_SPLIT[j][1]
                    view = kn[0:rows, b, j, :].rearrange("p (h d) -> p h d", h=H1)
                    last = nc.vector.tensor_tensor(
                        view, view, ss[0:rows, b, j, :].rearrange("p (h a) -> p h a", a=1)
                        .to_broadcast((rows, H1, HD1)), ALU.mult)
                last.then_inc(kn_ready, 1)
                for n in range(BATCH * IC):
                    dve.wait_ge(kvT_made, n + 1)
                    at_least(dve, m_made, n - IC + 1)
                    nc.vector.tensor_tensor(kvT[:, n % IC, :], k.PS[:, n % 2, 0:P], k.small["pairmask"][:, :],
                                            ALU.mult).then_inc(kvT_ready, 1)
                    if n:
                        keep_product(n - 1)
                keep_product(BATCH * IC - 1)


def attention0_stage(k):
    nc = k.nc
    with ExitStack() as own_memory:
        def sb(name, shape, dt=F32):
            return own_memory.enter_context(nc.sbuf_tensor(name, shape, dt))

        def sem(name):
            return own_memory.enter_context(nc.semaphore(name))

        xT = sb("xT", [P, KC, P])
        qT = sb("qT", [P, HALVES, P])
        peak = sb("peak", [P, GROUPS, GROUP])
        pT = sb("pT", [P, HALVES, CHUNKS, P])
        inv = sb("inv", [P, H0])
        O = sb("O", [P, H0, HD0])
        oT = sb("oT", [P, KC, P])

        scored = sem("scored")
        shifted = sem("shifted")
        raised = sem("raised")
        turned = sem("turned")
        turned_kept = sem("turned_kept")
        summed = sem("summed")
        divided = sem("divided")
        x_turned, xT_ready = sem("x_turned"), sem("xT_ready")
        q_made, qT_ready = sem("q_made"), sem("qT_ready")
        o_turned, oT_ready = sem("o_turned"), sem("oT_ready")
        o_made, x_added = sem("o_made"), sem("x_added")
        x_in_ready = sem("x_in_ready")
        xin = sb("xin", [P, D])
        dve_own = sem("dve_own")
        BANK_T, BANK_V, BANK_M = 4, 6, 7
        M = k.PS[:, BANK_M, :]

        def group_bank(g):
            return 2 * (g % 2)

        with nc.Block() as block:
            @block.tensor
            def _(pe):
                def turn_x(t):
                    at_least(pe, x_added, t - 2)
                    for c in range(KC):
                        last = nc.tensor.transpose(M[:, c * P:(c + 1) * P], xin[:, c * P:(c + 1) * P], k.ident)
                    last.then_inc(x_turned, 1)

                def project_q(t):
                    pe.wait_ge(xT_ready, t + 1)
                    for h in range(HALVES):
                        for c in range(KC):
                            last = nc.tensor.matmul(M[:, h * P:(h + 1) * P], k.wq0[:, c, h * P:(h + 1) * P],
                                                    xT[:, c, :], start=c == 0, stop=c == KC - 1)
                    last.then_inc(q_made, 1)

                def score(t, h, b):
                    if h == 0:
                        pe.wait_ge(qT_ready, t + 1)
                    for g in (2 * h, 2 * h + 1):
                        at_least(pe, shifted, 4 * t + g - 1)
                        for q in range(2):
                            a = (g % 2) * GROUP + q * 2
                            last = nc.tensor.matmul(
                                k.PS[:, group_bank(g) + q, 0:2 * CTX], qT[:, h, :],
                                k.keys0[:, b, h, a:a + 2, :], start=True, stop=True)
                        last.then_inc(scored, 1)

                def turn(t, h):
                    pe.wait_ge(raised, 4 * t + 2 * h + 2)
                    for f, (c0, m) in enumerate(FILLS):
                        n = 2 * NF * t + NF * h + f
                        at_least(pe, turned_kept, n - 1)
                        for c in range(m):
                            last = nc.tensor.transpose(
                                k.PS[:, BANK_T + (NF * h + f) % 2, c * P:(c + 1) * P],
                                k.probs[:, h, (c0 + c) * P:(c0 + c + 1) * P], k.ident)
                        last.then_inc(turned, 1)

                def weigh(t, h, b):
                    at_least(pe, divided, 2 * t + h)
                    for f, (c0, m) in enumerate(FILLS):
                        pe.wait_ge(turned_kept, 2 * NF * t + NF * h + f + 1)
                        for c in range(c0, c0 + m):
                            a = PAIR0[c] * VW
                            last = nc.tensor.matmul(
                                k.PS[:, BANK_V, a:a + 2 * VW], pT[:, h, c, :],
                                k.values0[:, b, h, c, :, :], start=c == 0, stop=c == CHUNKS - 1,
                                skip_group_check=True)
                    last.then_inc(summed, 1)

                def turn_o(t, prepared):
                    pe.wait_ge(qT_ready, prepared)
                    pe.wait_ge(divided, 2 * t + 2)
                    flat = O[:, :, :].rearrange("p h d -> p (h d)")
                    for c in range(KC):
                        last = nc.tensor.transpose(M[:, c * P:(c + 1) * P], flat[:, c * P:(c + 1) * P], k.ident)
                    last.then_inc(o_turned, 1)

                def project_o(t):
                    pe.wait_ge(oT_ready, t + 1)
                    for c in range(KC):
                        last = nc.tensor.matmul(M[:, 0:D], oT[:, c, :], k.wo0[:, c, :],
                                                start=c == 0, stop=c == KC - 1)
                    last.then_inc(o_made, 1)

                def tile(t, b, before, after):
                    score(t, 0, b)
                    if after:
                        pe.wait_ge(x_in_ready, t + 2)
                        turn_x(t + 1)
                    if before:
                        turn(t - 1, 1)
                        weigh(t - 1, 1, b_before(t, b))
                    score(t, 1, b)
                    if after:
                        project_q(t + 1)
                    turn(t, 0)
                    if before:
                        turn_o(t - 1, t + 2 if after else TILES)
                    weigh(t, 0, b)
                    if before:
                        project_o(t - 1)

                def b_before(t, b):
                    return 0 if isinstance(t, int) and t == TPB else b

                pe.wait_ge(x_in_ready, 1)
                turn_x(0)
                project_q(0)
                tile(0, 0, False, True)
                tile(1, 0, True, True)
                with pe.Fori(2, TPB) as t:
                    tile(t, 0, True, True)
                tile(TPB, 1, True, True)
                with pe.Fori(TPB + 1, TILES - 1) as t:
                    tile(t, 1, True, True)
                tile(TILES - 1, 1, True, False)
                turn(TILES - 1, 1)
                weigh(TILES - 1, 1, 1)
                turn_o(TILES - 1, TILES)
                project_o(TILES - 1)

            @block.gpsimd
            def _(pool):
                def stage_in(t):
                    at_least(pool, x_turned, t)
                    nc.gpsimd.tensor_copy(xin[:, :], k.XN[:, t, :]).then_inc(x_in_ready, 1)

                stage_in(0)
                with pool.Fori(1, TILES) as t:
                    stage_in(t)

            @block.scalar
            def _(act):
                def raise_scores(t, h):
                    for g in (2 * h, 2 * h + 1):
                        act.wait_ge(shifted, 4 * t + g + 1)
                        part = k.probs[:, h, (g % 2) * GW:(g % 2 + 1) * GW]
                        nc.scalar.activation(part, part, ACT.Exp, scale=HD0 ** -0.5).then_inc(raised, 1)

                def keep_turned(t, h):
                    at_least(act, summed, 2 * t + h - 1)
                    for f, (c0, m) in enumerate(FILLS):
                        act.wait_ge(turned, 2 * NF * t + NF * h + f + 1)
                        nc.scalar.activation(
                            pT[:, h, c0:c0 + m, :],
                            k.PS[:, BANK_T + (NF * h + f) % 2, 0:m * P].rearrange("p (c q) -> p c q", c=m),
                            ACT.Copy).then_inc(turned_kept, 1)

                def keep_o(t):
                    act.wait_ge(o_turned, t + 1)
                    nc.scalar.activation(oT[:, :, :], M[:, 0:D].rearrange("p (c q) -> p c q", c=KC),
                                         ACT.Copy).then_inc(oT_ready, 1)

                def tile(t, before):
                    if before:
                        keep_turned(t - 1, 1)
                    raise_scores(t, 0)
                    keep_turned(t, 0)
                    if before:
                        keep_o(t - 1)
                    raise_scores(t, 1)

                tile(0, False)
                tile(1, True)
                with act.Fori(2, TILES) as t:
                    tile(t, True)
                keep_turned(TILES - 1, 1)
                keep_o(TILES - 1)

            @block.vector
            def _(dve):
                own = Own(dve, dve_own)

                def shift(t, g):
                    h = g // 2
                    scores = k.PS[:, group_bank(g):group_bank(g) + 2, 0:2 * CTX].rearrange(
                        "p q (h k) -> p q h k", h=2)
                    top = peak[:, g, :].rearrange("p (q h) -> p q h", q=2)
                    dve.wait_ge(scored, 4 * t + g + 1)
                    own.then(nc.vector.tensor_reduce(top, scores, X_AXIS, ALU.max))
                    at_least(dve, turned, 2 * NF * (t - 1) + NF * (h + 1))
                    for q in range(2):
                        a = (g % 2) * GW + q * 2 * CTX
                        last = nc.vector.tensor_tensor(
                            k.probs[:, h, a:a + 2 * CTX].rearrange("p (h k) -> p h k", h=2),
                            scores[:, q, :, :],
                            peak[:, g, 2 * q:2 * q + 2].rearrange("p (h a) -> p h a", a=1)
                            .to_broadcast((P, 2, CTX)), ALU.subtract)
                    last.then_inc(shifted, 1)

                def keep_x(t):
                    dve.wait_ge(x_turned, t + 1)
                    nc.vector.tensor_copy(xT[:, :, :], M[:, 0:D].rearrange("p (c q) -> p c q", c=KC))\
                        .then_inc(xT_ready, 1)

                def keep_q(t):
                    dve.wait_ge(q_made, t + 1)
                    for h in range(HALVES):
                        last = nc.vector.tensor_scalar(qT[:, h, :], M[:, h * P:(h + 1) * P],
                                                       k.small["bq0"][:, h:h + 1], None, ALU.add)
                    last.then_inc(qT_ready, 1)

                def divide(t, h):
                    out = k.PS[:, BANK_V, 0:HALF_HEADS * VW].rearrange("p (h v) -> p h v", v=VW)
                    part = inv[:, h * HALF_HEADS:(h + 1) * HALF_HEADS].rearrange("p (h a) -> p h a", a=1)
                    dve.wait_ge(summed, 2 * t + h + 1)
                    own.then(nc.vector.reciprocal(part, out[:, :, HD0:VW]))
                    at_least(dve, o_turned, t)
                    nc.vector.tensor_tensor(O[:, h * HALF_HEADS:(h + 1) * HALF_HEADS, :], out[:, :, 0:HD0],
                                            part.to_broadcast((P, HALF_HEADS, HD0)),
                                            ALU.mult).then_inc(divided, 1)

                def add_x(t):
                    dve.wait_ge(o_made, t + 1)
                    nc.vector.tensor_tensor(k.X[:, t, :], M[:, 0:D], k.X[:, t, :], ALU.add)\
                        .then_inc(x_added, 1)

                def tile(t, before, after):
                    shift(t, 0)
                    shift(t, 1)
                    if after:
                        keep_x(t + 1)
                    if before:
                        divide(t - 1, 1)
                    shift(t, 2)
                    shift(t, 3)
                    if after:
                        keep_q(t + 1)
                    divide(t, 0)
                    if before:
                        add_x(t - 1)

                keep_x(0)
                keep_q(0)
                tile(0, False, True)
                tile(1, True, True)
                with dve.Fori(2, TILES - 1) as t:
                    own.enter(t, 2, GROUPS + HALVES)
                    tile(t, True, True)
                own.leave(TILES - 3)
                tile(TILES - 1, True, False)
                divide(TILES - 1, 1)
                add_x(TILES - 1)


def experts_stage(k, layer, count, blocks, slots, made, expert_of):
    nc = k.nc
    w1, w2, b1, b2 = (k.ap[f"{layer}{w}"] for w in ("w1", "w2", "b1", "b2"))
    W = blocks * P
    HB = W * FC // 512
    CPB = FC // HB
    BANK_X, BANK_Y = 4, 5
    with ExitStack() as own_memory:
        def sb(name, shape, dt=F32):
            return own_memory.enter_context(nc.sbuf_tensor(f"{layer}_{name}", shape, dt))

        def sem(name):
            return own_memory.enter_context(nc.semaphore(f"{layer}_{name}"))

        rows = sb("rows", [P, 2, blocks, D])
        xT = sb("rowsT", [P, 2, KC, W])
        hT = sb("hT", [P, 2, FC, W])
        w1_sb = sb("w1_sb", [P, 2, KC, F])
        w2_sb = sb("w2_sb", [P, 2, FC, D])
        b1_sb = sb("b1_sb", [P, 2, FC])
        b2_sb = sb("b2_sb", [P, 2, D])
        y = sb("y", [P, 2, blocks, D])
        rows_in = [sem(f"rows_in{r}") for r in range(2)]
        w1_in = [sem(f"w1_in{r}") for r in range(2)]
        w2_in = [sem(f"w2_in{r}") for r in range(2)]
        b1_in = [sem(f"b1_in{r}") for r in range(2)]
        b2_in = [sem(f"b2_in{r}") for r in range(2)]
        stored = [sem(f"stored{r}") for r in range(2)]
        turned, xT_ready = sem("rows_turned"), sem("rowsT_ready")
        upped = sem("upped")
        bent = sem("bent")
        downed, y_ready = sem("downed"), sem("y_ready")

        def after(i, back=0):
            j, r = i
            return 2 * j + r + 1 - back

        def pairs(eng, one):
            one((0, 0), True, False)
            one((0, 1), False, False)
            one((1, 0), False, False)
            with eng.Fori(1, count // 2 - 1) as j:
                one((j, 1), False, False)
                one((j + 1, 0), False, False)
            one((count // 2 - 1, 1), False, True)

        def before(i):
            j, r = i
            return (j, 0) if r else (j - 1, 1)

        def behind(i):
            j, r = i
            return (j + 1, 0) if r else (j, 1)

        def load_second(eng, i):
            j, r = i
            e = expert_of(eng, 2 * j + r)
            eng.dma_start(b2_sb[:, r, :], b2[bass.ds(e, 1), :].to_broadcast((P, D))).then_inc(b2_in[r], 16)
            eng.dma_start(w2_sb[:, r, :, :], w2[bass.ds(e, 1), :, :, :]
                          .rearrange("a p c d -> p (a c) d")).then_inc(w2_in[r], 16)

        with nc.Block() as block:
            @block.sync
            def _(sp):
                def load(i):
                    j, r = i
                    tile = 2 * j + r
                    e = expert_of(sp, tile)
                    at_least(sp, turned, after(i, 2))
                    sp.dma_start(rows[:, r, :, :],
                                 slots.rearrange("(i n p) d -> i p n d", p=P, n=blocks)[bass.ds(tile, 1), :, :, :]
                                 .rearrange("a p n d -> p (a n) d")).then_inc(rows_in[r], 16)
                    at_least(sp, upped, HB * after(i, 2))
                    sp.dma_start(w1_sb[:, r, :, :], w1[bass.ds(e, 1), :, :, :]
                                 .rearrange("a p c f -> p (a c) f")).then_inc(w1_in[r], 16)
                    at_least(sp, bent, HB * after(i, 2))
                    sp.dma_start(b1_sb[:, r, :], b1[bass.ds(e, 1), :, :].rearrange("a p f -> p (a f)"))\
                        .then_inc(b1_in[r], 16)

                load((0, 0))
                load_second(sp, (0, 0))
                load((0, 1))
                load_second(sp, (0, 1))
                with sp.Fori(1, count // 2) as j:
                    load((j, 0))
                    load((j, 1))

            @block.tensor
            def _(pe):
                def turn(i):
                    j, r = i
                    pe.wait_ge(rows_in[r], 16 * (j + 1))
                    at_least(pe, xT_ready, after(i, 1))
                    for n in range(blocks):
                        for c in range(KC):
                            last = nc.tensor.transpose(k.PS[:, BANK_X, c * W + n * P:c * W + (n + 1) * P],
                                                       rows[:, r, n, c * P:(c + 1) * P], k.ident)
                    last.then_inc(turned, 1)

                def up(i, first):
                    j, r = i
                    pe.wait_ge(w1_in[r], 16 * (j + 1))
                    pe.wait_ge(xT_ready, after(i))
                    for q in range(HB):
                        if not first:
                            at_least(pe, bent, HB * after(i, 2) + q + 1)
                        for f in range(q * CPB, (q + 1) * CPB):
                            for c in range(KC):
                                last = nc.tensor.matmul(
                                    k.PS[:, q, (f - q * CPB) * W:(f - q * CPB + 1) * W],
                                    w1_sb[:, r, c, f * P:(f + 1) * P], xT[:, r, c, :],
                                    start=c == 0, stop=c == KC - 1)
                        last.then_inc(upped, 1)

                def down(i):
                    j, r = i
                    pe.wait_ge(w2_in[r], 16 * (j + 1))
                    pe.wait_ge(bent, HB * after(i))
                    at_least(pe, y_ready, after(i, 2))
                    for n in range(blocks):
                        for f in range(FC):
                            last = nc.tensor.matmul(k.PS[:, BANK_Y + r, n * D:(n + 1) * D],
                                                    hT[:, r, f, n * P:(n + 1) * P], w2_sb[:, r, f, :],
                                                    start=f == 0, stop=f == FC - 1)
                    last.then_inc(downed, 1)

                def tile(i, first, last):
                    up(i, first)
                    if not last:
                        turn(behind(i))
                    if not first:
                        down(before(i))

                turn((0, 0))
                pairs(pe, tile)
                down((count // 2 - 1, 1))

            @block.scalar
            def _(act):
                def bend(i):
                    j, r = i
                    act.wait_ge(b1_in[r], 16 * (j + 1))
                    at_least(act, downed, after(i, 2))
                    for q in range(HB):
                        act.wait_ge(upped, HB * after(i, 1) + q + 1)
                        for f in range(q * CPB, (q + 1) * CPB):
                            last = nc.scalar.activation(
                                hT[:, r, f, :], k.PS[:, q, (f - q * CPB) * W:(f - q * CPB + 1) * W],
                                ACT.Gelu, bias=b1_sb[:, r, f:f + 1])
                        last.then_inc(bent, 1)

                def store(i):
                    j, r = i
                    act.wait_ge(y_ready, after(i))
                    act.dma_start(made.rearrange("(i n p) d -> i p n d", p=P, n=blocks)[bass.ds(2 * j + r, 1), :, :, :]
                                  .rearrange("a p n d -> p (a n) d"), y[:, r, :, :]).then_inc(stored[r], 16)

                def tile(i, first, last):
                    bend(i)
                    if not first:
                        store(before(i))
                        if not last:
                            load_second(act, behind(i))

                pairs(act, tile)
                store((count // 2 - 1, 1))
                for r in range(2):
                    act.wait_ge(stored[r], 16 * (count // 2))

            @block.vector
            def _(dve):
                def keep_x(i):
                    j, r = i
                    dve.wait_ge(turned, after(i))
                    at_least(dve, upped, HB * after(i, 2))
                    nc.vector.tensor_copy(xT[:, r, :, :],
                                          k.PS[:, BANK_X, 0:KC * W].rearrange("p (c w) -> p c w", c=KC))\
                        .then_inc(xT_ready, 1)

                def keep_y(i):
                    j, r = i
                    dve.wait_ge(b2_in[r], 16 * (j + 1))
                    dve.wait_ge(downed, after(i))
                    at_least(dve, stored[r], 16 * j)
                    nc.vector.tensor_tensor(
                        y[:, r, :, :], k.PS[:, BANK_Y + r, 0:blocks * D].rearrange("p (n d) -> p n d", n=blocks),
                        b2_sb[:, r:r + 1, :].to_broadcast((P, blocks, D)), ALU.add).then_inc(y_ready, 1)

                def tile(i, first, last):
                    if not last:
                        keep_x(behind(i))
                    if not first:
                        keep_y(before(i))

                keep_x((0, 0))
                pairs(dve, tile)
                keep_y((count // 2 - 1, 1))


def wide(ap2, shape, axis):
    return ap2.rearrange("p (e a) -> p e a" if axis == 2 else "p (a e) -> p a e", a=1).to_broadcast(shape)


def router_tensor(k, pe, experts, weights, xn_ready, turned, hT, hT_ready, scored):
    nc = k.nc
    for t in range(TILES + 1):
        if t < TILES:
            pe.wait_ge(xn_ready, t + 1)
            at_least(pe, hT_ready, t - 1)
            for c in range(KC):
                last = nc.tensor.transpose(k.PS[:, t % 2, c * P:(c + 1) * P], k.XN[:, t, c * P:(c + 1) * P],
                                           k.ident)
            last.then_inc(turned, 1)
        if t > 0:
            pe.wait_ge(hT_ready, t)
            for c in range(KC):
                last = nc.tensor.matmul(k.PS[:, 2, (t - 1) * experts:t * experts], hT[:, (t - 1) % 2, c, :],
                                        weights[:, c, :], start=c == 0, stop=c == KC - 1)
            last.then_inc(scored, 1)


def router_scalar(k, act, turned, hT, hT_ready, scored):
    for t in range(TILES):
        act.wait_ge(turned, t + 1)
        at_least(act, scored, t - 1)
        k.nc.scalar.activation(hT[:, t % 2, :, :],
                               k.PS[:, t % 2, 0:D].rearrange("p (c q) -> p c q", c=KC),
                               ACT.Copy).then_inc(hT_ready, 1)


def first_of_largest(k, own, one_hot, scores, top, order, experts):
    nc = k.nc
    shape = (P, TILES, experts)
    own.then(nc.vector.tensor_reduce(top, scores, X_AXIS, ALU.max))
    own.then(nc.vector.tensor_tensor(one_hot, scores, wide(top, shape, 2), ALU.is_equal))
    own.then(nc.vector.tensor_tensor(one_hot, one_hot, wide(order, shape, 1), ALU.mult))
    own.then(nc.vector.tensor_reduce(top, one_hot, X_AXIS, ALU.max))
    own.then(nc.vector.tensor_tensor(one_hot, one_hot, wide(top, shape, 2), ALU.is_equal))


def route0_stage(k):
    nc = k.nc
    with ExitStack() as own_memory:
        def sb(name, shape, dt=F32):
            return own_memory.enter_context(nc.sbuf_tensor(name, shape, dt))

        def sem(name):
            return own_memory.enter_context(nc.semaphore(name))

        hT = sb("hT0", [P, 2, KC, P])
        logits = sb("logits", [P, TILES, E0])
        one_hot = sb("one_hot", [P, TILES, E0])
        earlier = sb("earlier", [P, TILES, E0])
        place = sb("place", [P, TILES, E0])
        top = sb("top", [P, TILES])
        grid = sb("grid", [P, E0, TILES])
        count = sb("count", [P, E0])
        tiles_of = sb("tiles_of", [P, E0])
        start = sb("start", [P, E0])
        square = sb("square", [P, E0, E0])
        over = sb("over", [P, SLOT_TILES0, E0])
        expert = sb("expert", [P, SLOT_TILES0])
        slot = sb("slot", [P, TILES])
        dve_own, sums, powers = sem("dve_own"), sem("sums"), sem("powers")
        xn_ready, turned, hT_ready, scored = sem("xn_ready"), sem("turned"), sem("hT_ready"), sem("scored")
        chosen, ranked, slots_ready, scattered = sem("chosen"), sem("ranked"), sem("slots_ready"), sem("scattered")
        with nc.Block() as block:
            @block.tensor
            def _(pe):
                router_tensor(k, pe, E0, k.small["wr0"], xn_ready, turned, hT, hT_ready, scored)
                pe.wait_ge(chosen, 1)
                nc.tensor.matmul(k.PS[:, 3, 0:TILES * E0], k.small["tri"][:, :],
                                 one_hot[:, :, :], start=True, stop=False)
                nc.tensor.matmul(k.PS[:, 3, 0:TILES * E0], k.small["ones"][:, :],
                                 earlier[:, :, :], start=False, stop=True)
                nc.tensor.matmul(k.PS[:, 4, 0:E0], k.small["ones"][:, :], count[:, :],
                                 start=True, stop=True).then_inc(ranked, 1)

            @block.scalar
            def _(act):
                router_scalar(k, act, turned, hT, hT_ready, scored)

            @block.gpsimd
            def _(pool):
                inverse_roots(k, pool, sums, powers)
                pool.wait_ge(slots_ready, 1)
                for t in range(TILES):
                    nc.gpsimd.indirect_dma_start(
                        out=k.slots0, out_offset=bass.IndirectOffsetOnAxis(ap=k.slot0[:, t:t + 1], axis=0),
                        in_=k.XN[:, t, :], in_offset=None).then_inc(scattered, 16)
                pool.wait_ge(scattered, 16 * TILES)

            @block.vector
            def _(dve):
                own = Own(dve, dve_own)
                normalise_vector(k, dve, own, sums, powers, xn_ready)
                dve.wait_ge(scored, TILES)
                own.then(nc.vector.tensor_tensor(
                    logits[:, :, :], k.PS[:, 2, 0:TILES * E0].rearrange("p (t e) -> p t e", t=TILES),
                    wide(k.small["br0"][:, :], (P, TILES, E0), 1), ALU.add))
                first_of_largest(k, own, one_hot[:, :, :], logits[:, :, :], top[:, :], k.small["order0"][:, :], E0)
                own.then(nc.vector.memset(earlier[:, 0, :], 0.0))
                for t in range(1, TILES):
                    own.then(nc.vector.tensor_tensor(earlier[:, t, :], earlier[:, t - 1, :],
                                                     one_hot[:, t - 1, :], ALU.add))
                nc.vector.tensor_tensor(count[:, :], earlier[:, TILES - 1, :], one_hot[:, TILES - 1, :],
                                        ALU.add).then_inc(chosen, 1)
                dve.wait_ge(ranked, 1)
                own.then(nc.vector.tensor_tensor(
                    grid[:, :, :], wide(k.PS[:, 4, 0:E0], (P, E0, TILES), 2),
                    wide(k.small["thresh0"][:, :], (P, E0, TILES), 1), ALU.is_gt))
                own.then(nc.vector.tensor_reduce(tiles_of[:, :], grid[:, :, :], X_AXIS, ALU.add))
                own.then(nc.vector.tensor_tensor(square[:, :, :], k.small["before0"][:, :, :],
                                                 wide(tiles_of[:, :], (P, E0, E0), 1), ALU.mult))
                own.then(nc.vector.tensor_reduce(start[:, :], square[:, :, :], X_AXIS, ALU.add))
                own.then(nc.vector.tensor_tensor(tiles_of[:, :], tiles_of[:, :], start[:, :], ALU.add))
                own.then(nc.vector.tensor_tensor(
                    over[:, :, :], wide(k.small["tile_no"][:, :], (P, SLOT_TILES0, E0), 2),
                    wide(tiles_of[:, :], (P, SLOT_TILES0, E0), 1), ALU.is_ge))
                own.then(nc.vector.tensor_reduce(expert[:, :], over[:, :, :], X_AXIS, ALU.add))
                own.then(nc.vector.tensor_scalar(k.expert0[:, :], expert[:, :], float(E0 - 1), None, ALU.min))
                own.then(nc.vector.tensor_scalar(start[:, :], start[:, :], float(P), None, ALU.mult))
                own.then(nc.vector.tensor_tensor(
                    place[:, :, :], k.PS[:, 3, 0:TILES * E0].rearrange("p (t e) -> p t e", t=TILES),
                    wide(start[:, :], (P, TILES, E0), 1), ALU.add))
                own.then(nc.vector.tensor_tensor(place[:, :, :], place[:, :, :], one_hot[:, :, :], ALU.mult))
                own.then(nc.vector.tensor_reduce(slot[:, :], place[:, :, :], X_AXIS, ALU.add))
                nc.vector.tensor_copy(k.slot0[:, :], slot[:, :]).then_inc(slots_ready, 1)


def attention1_stage(k):
    nc = k.nc
    with ExitStack() as own_memory:
        def sb(name, shape, dt=F32):
            return own_memory.enter_context(nc.sbuf_tensor(name, shape, dt))

        def sem(name):
            return own_memory.enter_context(nc.semaphore(name))

        wq, w1, w2 = sb("wq", [P, KC, INNER]), sb("w1", [P, KC, F]), sb("w2", [P, FC, D])
        mean2 = sb("mean2", [P, TILES, 2])
        rstd2 = sb("rstd2", [P, TILES])
        xh = sb("xh", [P, D])
        xhT = sb("xhT", [P, KC, P])
        sq = sb("sq1", [P, INNER])
        ss = sb("ss1", [P, H1])
        rn = sb("rn1", [P, H1])
        qn = sb("qn", [P, INNER])
        qnT = sb("qnT", [P, IC, P])
        qb = sb("qb", [P, 2, D])
        x1 = sb("x1", [P, 1, D])
        st1 = sb("st1", [P, 6])
        mv1 = sb("mv1", [P, 2])
        rs1 = sb("rs1", [P, 1])
        xh1 = sb("xh1", [P, D])
        xh1T = sb("xh1T", [P, KC, P])
        hT = sb("hT1", [P, FC, P])
        w_in, gathered = sem("w_in"), sem("gathered")
        dve_own, pool_own, act_own = sem("dve_own"), sem("pool_own"), sem("act_own")
        sums, powers, sums2, powers2 = sem("sums"), sem("powers"), sem("sums2"), sem("powers2")
        xh_ready, xh_turned, xhT_ready = sem("xh_ready"), sem("xh_turned"), sem("xhT_ready")
        q_made, squared, q_summed, q_rooted, qn_ready = (sem(n) for n in (
            "q_made", "squared", "q_summed", "q_rooted", "qn_ready"))
        qn_turned, qnT_ready, o_made, x1_ready = (sem(n) for n in (
            "qn_turned", "qnT_ready", "o_made", "x1_ready"))
        x1_summed, x1_rooted, xh1_ready, xh1_turned, xh1T_ready = (sem(n) for n in (
            "x1_summed", "x1_rooted", "xh1_ready", "xh1_turned", "xh1T_ready"))
        upped, bent, downed, x_ready, xn_free = (sem(n) for n in (
            "upped", "bent", "downed", "x_ready", "xn_free"))
        BANK_Q, BANK_QT, BANK_H, BANK_Y, BANK_T = 0, 2, 4, 6, 7

        with nc.Block() as block:
            @block.sync
            def _(sp):
                sp.dma_start(wq[:, :, :], k.ap["wq1"]).then_inc(w_in, 16)
                sp.dma_start(w1[:, :, :], k.ap["mw1"]).then_inc(w_in, 16)
                sp.dma_start(w2[:, :, :], k.ap["mw2"]).then_inc(w_in, 16)
                sp.wait_ge(w_in, 48)

            def turns(eng, one):
                one(0, "ba")
                one(1, "bcda")
                one(2, "becfdag")
                with eng.Fori(3, TPB) as s:
                    one(s, "becfdag", 0)
                one(TPB, "becfdag", 0)
                with eng.Fori(TPB + 1, TILES - 1) as s:
                    one(s, "becfdag", 1)
                one(TILES - 1, "becfdg", 1)
                one(TILES, "ecfdg", 1)
                one(TILES + 1, "efg", 1)

            @block.tensor
            def _(pe):
                def a(t):
                    pe.wait_ge(xh_ready, t + 1)
                    if not isinstance(t, int) or t > 2:
                        pe.wait_ge(xh1T_ready, t - 2)
                    for c in range(KC):
                        last = nc.tensor.transpose(k.PS[:, BANK_T, c * P:(c + 1) * P], xh[:, c * P:(c + 1) * P],
                                                   k.ident)
                    last.then_inc(xh_turned, 1)

                def b(t):
                    pe.wait_ge(xhT_ready, t + 1)
                    at_least(pe, qn_ready, t)
                    for q in range(2):
                        for c in range(KC):
                            last = nc.tensor.matmul(k.PS[:, BANK_Q + q, :], xhT[:, c, :],
                                                    wq[:, c, q * 512:(q + 1) * 512],
                                                    start=c == 0, stop=c == KC - 1)
                    last.then_inc(q_made, 1)

                def c(t):
                    pe.wait_ge(qn_ready, t + 1)
                    at_least(pe, qnT_ready, t)
                    for i in range(IC):
                        last = nc.tensor.transpose(k.PS[:, BANK_QT + i // 4, (i % 4) * P:(i % 4 + 1) * P],
                                                   qn[:, i * P:(i + 1) * P], k.ident)
                    last.then_inc(qn_turned, 1)

                def d(t, batch):
                    pe.wait_ge(qnT_ready, t + 1)
                    if not isinstance(t, int) or t > 0:
                        at_least(pe, x_ready, t - 1)
                    for i in range(IC):
                        last = nc.tensor.matmul(k.PS[:, BANK_Y, 0:D], qnT[:, i, :], k.keyval1[:, batch, i, :],
                                                start=i == 0, stop=i == IC - 1)
                    last.then_inc(o_made, 1)

                def e(t):
                    pe.wait_ge(xh1_ready, t + 1)
                    pe.wait_ge(xhT_ready, t + 3 if not isinstance(t, int) or t + 3 < TILES else TILES)
                    for c in range(KC):
                        last = nc.tensor.transpose(k.PS[:, BANK_T, c * P:(c + 1) * P],
                                                   xh1[:, c * P:(c + 1) * P], k.ident)
                    last.then_inc(xh1_turned, 1)

                def f(t):
                    pe.wait_ge(xh1T_ready, t + 1)
                    for q in range(2):
                        at_least(pe, bent, 2 * (t - 1) + q + 1)
                        for f in range(4 * q, 4 * q + 4):
                            for c in range(KC):
                                last = nc.tensor.matmul(k.PS[:, BANK_H + q, (f - 4 * q) * P:(f - 4 * q + 1) * P],
                                                        w1[:, c, f * P:(f + 1) * P], xh1T[:, c, :],
                                                        start=c == 0, stop=c == KC - 1)
                        last.then_inc(upped, 1)

                def g(t, last_x1):
                    pe.wait_ge(bent, 2 * t + 2)
                    pe.wait_ge(x1_ready, last_x1)
                    for f in range(FC):
                        last = nc.tensor.matmul(k.PS[:, BANK_Y, 0:D], hT[:, f, :], w2[:, f, :],
                                                start=f == 0, stop=f == FC - 1)
                    last.then_inc(downed, 1)

                def turn(s, steps, batch=0):
                    for step in steps:
                        if step == "a":
                            a(s + 1)
                        elif step == "b":
                            b(s)
                        elif step == "c":
                            c(s - 1)
                        elif step == "d":
                            d(s - 1, batch)
                        elif step == "e":
                            e(s - 2)
                        elif step == "f":
                            f(s - 2)
                        else:
                            g(s - 2, TILES if isinstance(s, int) and s > TILES else s)

                pe.wait_ge(w_in, 48)
                a(0)
                turns(pe, turn)

            @block.scalar
            def _(act):
                def square(t):
                    act.wait_ge(q_made, t + 1)
                    at_least(act, q_summed, t)
                    nc.scalar.activation(sq[:, :], k.PS[:, BANK_Q:BANK_Q + 2, :], ACT.Square)\
                        .then_inc(squared, 1)

                def keep_q(t):
                    act.wait_ge(qn_turned, t + 1)
                    at_least(act, o_made, t)
                    nc.scalar.activation(qnT[:, :, :], k.PS[:, BANK_QT:BANK_QT + 2, :]
                                         .rearrange("p b (c q) -> p (b c) q", c=4), ACT.Copy)\
                        .then_inc(qnT_ready, 1)

                def bend(t):
                    at_least(act, downed, t)
                    for q in range(2):
                        act.wait_ge(upped, 2 * t + q + 1)
                        for f in range(4 * q, 4 * q + 4):
                            last = nc.scalar.activation(
                                hT[:, f, :], k.PS[:, BANK_H + q, (f - 4 * q) * P:(f - 4 * q + 1) * P],
                                ACT.Gelu, bias=k.small["mb1"][:, f:f + 1])
                        last.then_inc(bent, 1)

                def turn(s, steps, batch=0):
                    if "b" in steps:
                        square(s)
                    if "c" in steps:
                        keep_q(s - 1)
                    if "f" in steps:
                        bend(s - 2)

                turns(act, turn)

            @block.gpsimd
            def _(pool):
                own = Own(pool, pool_own)
                for t in range(TILES):
                    nc.gpsimd.indirect_dma_start(
                        out=k.XN[:, t, :], out_offset=None, in_=k.made0,
                        in_offset=bass.IndirectOffsetOnAxis(ap=k.slot0[:, t:t + 1], axis=0))\
                        .then_inc(gathered, 16)
                inverse_roots(k, pool, sums, powers)
                pool.wait_ge(sums2, 1)
                nc.gpsimd.tensor_tensor(rstd2[:, :], rstd2[:, :], k.half_neg[:, 0:TILES], ALU.pow)\
                    .then_inc(powers2, 1)

                def root_q(t):
                    pool.wait_ge(q_summed, t + 1)
                    at_least(pool, qn_ready, t)
                    nc.gpsimd.tensor_tensor(rn[:, :], ss[:, :], k.half_pos[:, 0:H1], ALU.pow)\
                        .then_inc(q_rooted, 1)

                def root_x1(t):
                    pool.wait_ge(x1_summed, t + 1)
                    nc.gpsimd.tensor_tensor(rs1[:, :], rs1[:, :], k.half_neg[:, 0:1], ALU.pow)\
                        .then_inc(x1_rooted, 1)

                def turn(s, steps, batch=0):
                    if "b" in steps:
                        root_q(s)
                    if "d" in steps:
                        root_x1(s - 1)

                pool.wait_ge(xn_free, 1)
                turns(pool, turn)

            @block.vector
            def _(dve):
                own = Own(dve, dve_own)
                for t in range(TILES):
                    dve.wait_ge(gathered, 16 * TILES)
                    last = nc.vector.tensor_tensor(k.X[:, t, :], k.X[:, t, :], k.XN[:, t, :], ALU.add)
                own.then(last)
                own.then(normalise_vector(k, dve, own, sums, powers))
                for t in range(TILES):
                    last = nc.vector.bn_stats(k.stats[:, t, :], k.XN[:, t, :])
                own.then(last)
                for t in range(TILES):
                    last = nc.vector.bn_aggr(mean2[:, t, :], k.stats[:, t, :])
                own.then(last)
                nc.vector.tensor_scalar(rstd2[:, :], mean2[:, :, 1], EPS, None, ALU.add).then_inc(sums2, 1)
                dve.sem_inc(xn_free, 1)
                dve.wait_ge(powers2, 1)

                def normalise_again(t):
                    at_least(dve, xh_turned, t)
                    nc.vector.tensor_scalar(xh[:, :], k.XN[:, t, :], mean2[:, t, 0:1], rstd2[:, bass.ds(t, 1)],
                                            ALU.subtract, ALU.mult).then_inc(xh_ready, 1)

                def keep_xh(t):
                    dve.wait_ge(xh_turned, t + 1)
                    at_least(dve, q_made, t)
                    for c in range(KC):
                        last = nc.vector.tensor_scalar(xhT[:, c, :], k.PS[:, BANK_T, c * P:(c + 1) * P],
                                                       k.small["g1"][:, c:c + 1], k.small["be1"][:, c:c + 1],
                                                       ALU.mult, ALU.add)
                    last.then_inc(xhT_ready, 1)

                def sum_q(t):
                    dve.wait_ge(squared, t + 1)
                    at_least(dve, q_rooted, t)
                    nc.vector.tensor_reduce(ss[:, :], sq[:, :].rearrange("p (h d) -> p h d", h=H1),
                                            X_AXIS, ALU.add).then_inc(q_summed, 1)

                def unit_q(t):
                    dve.wait_ge(q_rooted, t + 1)
                    own.then(nc.vector.tensor_scalar(rn[:, :], rn[:, :], 1e-12, None, ALU.max))
                    own.then(nc.vector.reciprocal(rn[:, :], rn[:, :]))
                    at_least(dve, qn_turned, t)
                    nc.vector.tensor_tensor(
                        qn[:, :].rearrange("p (h d) -> p h d", h=H1),
                        k.PS[:, BANK_Q:BANK_Q + 2, :].rearrange("p b (h d) -> p (b h) d", d=HD1),
                        wide(rn[:, :], (P, H1, HD1), 2), ALU.mult).then_inc(qn_ready, 1)

                def residual(t):
                    own.then(nc.vector.tensor_tensor(qb[:, 0, :], k.XN[:, t, :], k.small["bo1"][:, :], ALU.add))
                    dve.wait_ge(o_made, t + 1)
                    nc.vector.tensor_tensor(x1[:, 0, :], k.PS[:, BANK_Y, 0:D], qb[:, 0, :], ALU.add)\
                        .then_inc(x1_ready, 1)
                    dve.wait_ge(x1_ready, t + 1)
                    own.then(nc.vector.bn_stats(st1[:, :], x1[:, 0, :]))
                    nc.vector.tensor_tensor(qb[:, 1, :], k.X[:, t, :], k.small["mb2"][:, :], ALU.add)
                    own.then(nc.vector.bn_aggr(mv1[:, :], st1[:, :]))
                    nc.vector.tensor_scalar(rs1[:, :], mv1[:, 1:2], EPS, None, ALU.add).then_inc(x1_summed, 1)
                    own.then(nc.vector.tensor_tensor(k.X[:, t, :], qb[:, 1, :], x1[:, 0, :], ALU.add))

                def normalise_x1(t):
                    dve.wait_ge(x1_rooted, t + 1)
                    at_least(dve, xh1_turned, t)
                    nc.vector.tensor_scalar(xh1[:, :], x1[:, 0, :], mv1[:, 0:1], rs1[:, 0:1],
                                            ALU.subtract, ALU.mult).then_inc(xh1_ready, 1)

                def keep_xh1(t):
                    dve.wait_ge(xh1_turned, t + 1)
                    at_least(dve, upped, 2 * t)
                    for c in range(KC):
                        last = nc.vector.tensor_scalar(xh1T[:, c, :], k.PS[:, BANK_T, c * P:(c + 1) * P],
                                                       k.small["g2"][:, c:c + 1], k.small["be2"][:, c:c + 1],
                                                       ALU.mult, ALU.add)
                    last.then_inc(xh1T_ready, 1)

                def finish(t):
                    dve.wait_ge(downed, t + 1)
                    nc.vector.tensor_tensor(k.X[:, t, :], k.PS[:, BANK_Y, 0:D], k.X[:, t, :], ALU.add)\
                        .then_inc(x_ready, 1)

                def turn(s, steps, batch=0):
                    if "e" in steps:
                        keep_xh1(s - 2)
                    if "b" in steps:
                        sum_q(s)
                    if "a" in steps:
                        normalise_again(s + 1)
                    if "d" in steps:
                        residual(s - 1)
                    if "b" in steps:
                        unit_q(s)
                    if "a" in steps:
                        keep_xh(s + 1)
                    if "d" in steps:
                        normalise_x1(s - 1)
                    if "g" in steps:
                        finish(s - 2)

                def counted(s, steps, batch=0):
                    if isinstance(s, int):
                        turn(s, steps, batch)
                    else:
                        first, turns_ = (3, TPB - 3) if batch == 0 else (TPB + 1, TPB - 2)
                        own.enter(s, first, 6)
                        turn(s, steps, batch)
                        own.leave(turns_)

                normalise_again(0)
                keep_xh(0)
                turns(dve, counted)


def route1_stage(k):
    nc = k.nc
    with ExitStack() as own_memory:
        def sb(name, shape, dt=F32):
            return own_memory.enter_context(nc.sbuf_tensor(name, shape, dt))

        def sem(name):
            return own_memory.enter_context(nc.semaphore(name))

        hT = sb("hT2", [P, 2, KC, P])
        wide3 = [P, TILES, E1]
        logits, probs, first, second, both = (sb(n, wide3) for n in ("logits1", "probs1", "first", "second", "both"))
        earlier, rank, work = (sb(n, wide3) for n in ("earlier1", "rank1", "work1"))
        top, total, kept, gate_sum = (sb(n, [P, TILES]) for n in ("top1", "total1", "kept1", "gate_sum"))
        gate = sb("gate", [P, 2, TILES])
        where = sb("where", [P, 2, TILES])
        drop = sb("drop", [P, 2, TILES])
        junk = sb("junk", [P, D])
        square = sb("square_sum", [P, TILES])
        dve_own, sums, powers, sums2, powers2 = (sem(n) for n in ("dve_own", "sums", "powers", "sums2", "powers2"))
        xn_ready, turned, hT_ready, scored = sem("xn_ready"), sem("turned"), sem("hT_ready"), sem("scored")
        ln_ready, squared, raising, raised = sem("ln_ready"), sem("squared"), sem("raising"), sem("raised")
        chosen, ranked, rows_known, scattered = sem("chosen"), sem("ranked"), sem("rows_known"), sem("scattered")
        act_own = sem("act_own")
        with nc.Block() as block:
            @block.tensor
            def _(pe):
                router_tensor(k, pe, E1, k.small["wr1"], xn_ready, turned, hT, hT_ready, scored)
                pe.wait_ge(chosen, 1)
                nc.tensor.matmul(k.PS[:, 3, 0:TILES * E1], k.small["tri"][:, :], both[:, :, :],
                                 start=True, stop=False)
                nc.tensor.matmul(k.PS[:, 3, 0:TILES * E1], k.small["ones"][:, :], earlier[:, :, :],
                                 start=False, stop=True).then_inc(ranked, 1)

            @block.scalar
            def _(act):
                own = Own(act, act_own)
                for t in range(TILES):
                    act.wait_ge(ln_ready, t + 1)
                    own.then(nc.scalar.activation(junk[:, :], k.XN[:, t, :], ACT.Square,
                                                  accum_out=square[:, t:t + 1]))
                act.sem_inc(squared, 1)
                router_scalar(k, act, turned, hT, hT_ready, scored)
                act.wait_ge(raising, 1)
                nc.scalar.activation(probs[:, :, :], probs[:, :, :], ACT.Exp).then_inc(raised, 1)

            @block.gpsimd
            def _(pool):
                inverse_roots(k, pool, sums, powers)
                pool.wait_ge(sums2, 1)
                nc.gpsimd.tensor_tensor(square[:, :], square[:, :], k.half_neg[:, 0:TILES], ALU.pow)\
                    .then_inc(powers2, 1)
                for n in range(2):
                    pool.wait_ge(rows_known, n + 1)
                    for t in range(TILES):
                        nc.gpsimd.indirect_dma_start(
                            out=k.slots1, out_offset=bass.IndirectOffsetOnAxis(ap=k.slot1[:, n, t:t + 1], axis=0),
                            in_=k.XN[:, t, :], in_offset=None, bounds_check=ROWS1 - 1,
                            oob_is_err=False).then_inc(scattered, 16)
                pool.wait_ge(scattered, 16 * 2 * TILES)

            @block.vector
            def _(dve):
                own = Own(dve, dve_own)
                normalise_vector(k, dve, own, sums, powers, ln_ready)
                dve.wait_ge(ln_ready, TILES)
                dve.wait_ge(squared, 1)
                nc.vector.tensor_scalar(square[:, :], square[:, :], 1.0 / D, EPS, ALU.mult, ALU.add)\
                    .then_inc(sums2, 1)
                dve.wait_ge(powers2, 1)
                for t in range(TILES):
                    nc.vector.scalar_tensor_tensor(k.XN[:, t, :], k.XN[:, t, :], square[:, t:t + 1],
                                                   k.small["nw"][:, :], ALU.mult, ALU.mult).then_inc(xn_ready, 1)
                dve.wait_ge(scored, TILES)
                own.then(nc.vector.tensor_tensor(
                    logits[:, :, :], k.PS[:, 2, 0:TILES * E1].rearrange("p (t e) -> p t e", t=TILES),
                    wide(k.small["br1"][:, :], wide3, 1), ALU.add))
                own.then(nc.vector.tensor_reduce(top[:, :], logits[:, :, :], X_AXIS, ALU.max))
                nc.vector.tensor_tensor(probs[:, :, :], logits[:, :, :], wide(top[:, :], wide3, 2),
                                        ALU.subtract).then_inc(raising, 1)
                dve.wait_ge(raising, 1)
                order = k.small["order1"][:, :]
                first_of_largest(k, own, first[:, :, :], logits[:, :, :], top[:, :], order, E1)
                own.then(nc.vector.tensor_scalar(work[:, :, :], first[:, :, :], -3e38, None, ALU.mult))
                own.then(nc.vector.tensor_tensor(logits[:, :, :], logits[:, :, :], work[:, :, :], ALU.add))
                first_of_largest(k, own, second[:, :, :], logits[:, :, :], top[:, :], order, E1)
                own.then(nc.vector.tensor_tensor(both[:, :, :], first[:, :, :], second[:, :, :], ALU.add))
                own.then(nc.vector.memset(earlier[:, 0, :], 0.0))
                for t in range(1, TILES):
                    last = nc.vector.tensor_tensor(earlier[:, t, :], earlier[:, t - 1, :], both[:, t - 1, :],
                                                   ALU.add)
                    own.then(last)
                dve.sem_inc(chosen, 1)
                dve.wait_ge(raised, 1)
                own.then(nc.vector.tensor_reduce(total[:, :], probs[:, :, :], X_AXIS, ALU.add))
                own.then(nc.vector.reciprocal(total[:, :], total[:, :]))
                own.then(nc.vector.tensor_tensor(probs[:, :, :], probs[:, :, :], wide(total[:, :], wide3, 2),
                                                 ALU.mult))
                for n, one_hot in enumerate((first, second)):
                    own.then(nc.vector.tensor_tensor(work[:, :, :], probs[:, :, :], one_hot[:, :, :], ALU.mult))
                    own.then(nc.vector.tensor_reduce(gate[:, n, :], work[:, :, :], X_AXIS, ALU.add))
                dve.wait_ge(ranked, 1)
                own.then(nc.vector.tensor_copy(rank[:, :, :], k.PS[:, 3, 0:TILES * E1]
                                               .rearrange("p (t e) -> p t e", t=TILES)))
                for n, one_hot in enumerate((first, second)):
                    own.then(nc.vector.tensor_tensor(work[:, :, :], rank[:, :, :], one_hot[:, :, :], ALU.mult))
                    own.then(nc.vector.tensor_reduce(where[:, n, :], work[:, :, :], X_AXIS, ALU.add))
                    own.then(nc.vector.tensor_scalar(drop[:, n, :], where[:, n, :], float(CAP), None, ALU.is_ge))
                    own.then(nc.vector.tensor_tensor(
                        work[:, :, :], one_hot[:, :, :], wide(k.small["base1"][:, :], wide3, 1), ALU.mult))
                    own.then(nc.vector.tensor_reduce(top[:, :], work[:, :, :], X_AXIS, ALU.add))
                    own.then(nc.vector.tensor_tensor(where[:, n, :], where[:, n, :], top[:, :], ALU.add))
                    own.then(nc.vector.scalar_tensor_tensor(where[:, n, :], drop[:, n, :], float(SKIP),
                                                            where[:, n, :], ALU.mult, ALU.add))
                    nc.vector.tensor_copy(k.slot1[:, n, :], where[:, n, :]).then_inc(rows_known, 1)
                own.then(nc.vector.tensor_scalar(drop[:, :, :], drop[:, :, :], -1.0, 1.0, ALU.mult, ALU.add))
                own.then(nc.vector.tensor_tensor(gate[:, :, :], gate[:, :, :], drop[:, :, :], ALU.mult))
                own.then(nc.vector.tensor_tensor(gate_sum[:, :], gate[:, 0, :], gate[:, 1, :], ALU.add))
                own.then(nc.vector.tensor_scalar(kept[:, :], gate_sum[:, :], 0.0, None, ALU.is_le))
                own.then(nc.vector.tensor_tensor(gate_sum[:, :], gate_sum[:, :], kept[:, :], ALU.add))
                own.then(nc.vector.reciprocal(gate_sum[:, :], gate_sum[:, :]))
                own.then(nc.vector.tensor_tensor(
                    gate[:, :, :], gate[:, :, :],
                    gate_sum[:, :].rearrange("p (a t) -> p a t", a=1).to_broadcast((P, 2, TILES)), ALU.mult))
                own.then(nc.vector.tensor_tensor(first[:, :, :], first[:, :, :], wide(gate[:, 0, :], wide3, 2),
                                                 ALU.mult))
                own.then(nc.vector.tensor_tensor(second[:, :, :], second[:, :, :], wide(gate[:, 1, :], wide3, 2),
                                                 ALU.mult))
                own.then(nc.vector.tensor_tensor(k.plain[:, :, :], first[:, :, 0:PLAIN], second[:, :, 0:PLAIN],
                                                 ALU.add))
                own.then(nc.vector.tensor_scalar(drop[:, :, :], where[:, :, :], float(SKIP), None, ALU.is_lt))
                own.then(nc.vector.tensor_tensor(k.gate1[:, :, :], gate[:, :, :], drop[:, :, :], ALU.mult))
                own.then(nc.vector.tensor_tensor(where[:, :, :], where[:, :, :], drop[:, :, :], ALU.mult))
                own.then(nc.vector.tensor_copy(k.read1[:, :, :], where[:, :, :]))
                for t in range(TILES):
                    own.then(nc.vector.scalar_tensor_tensor(k.X[:, t, :], k.XN[:, t, :], k.plain[:, t, 1:2],
                                                            k.X[:, t, :], ALU.mult, ALU.add))
                    for c in range(2):
                        own.then(nc.vector.scalar_tensor_tensor(
                            k.X[:, t, :], k.small["cv"][:, c, :], k.plain[:, t, 2 + c:3 + c], k.X[:, t, :],
                            ALU.mult, ALU.add))


def combine_stage(k):
    nc = k.nc
    with ExitStack() as own_memory:
        def sem(name):
            return own_memory.enter_context(nc.semaphore(name))

        Y = own_memory.enter_context(nc.sbuf_tensor("Y", [P, 2, TILES, D], F32))
        PART = TILES // 4
        gathered = [sem(f"gathered{q}") for q in range(4)]
        own_sem, x_ready, stored = sem("dve_own"), sem("x_ready"), sem("stored")
        with nc.Block() as block:
            @block.gpsimd
            def _(pool):
                for t in range(TILES):
                    for n in range(2):
                        nc.gpsimd.indirect_dma_start(
                            out=Y[:, n, t, :], out_offset=None, in_=k.made1,
                            in_offset=bass.IndirectOffsetOnAxis(ap=k.read1[:, n, t:t + 1], axis=0))\
                            .then_inc(gathered[t // PART], 16)

            @block.vector
            def _(dve):
                own = Own(dve, own_sem)
                for t in range(TILES):
                    dve.wait_ge(gathered[t // PART], 16 * 2 * PART)
                    own.then(nc.vector.scalar_tensor_tensor(k.X[:, t, :], Y[:, 0, t, :], k.gate1[:, 0, t:t + 1],
                                                            k.X[:, t, :], ALU.mult, ALU.add))
                    nc.vector.scalar_tensor_tensor(k.X[:, t, :], Y[:, 1, t, :], k.gate1[:, 1, t:t + 1],
                                                   k.X[:, t, :], ALU.mult, ALU.add).then_inc(x_ready, 1)

            @block.sync
            def _(sp):
                for t in range(0, TILES, 2):
                    sp.wait_ge(x_ready, t + 2)
                    sp.dma_start(k.out[t * P:(t + 2) * P, :].rearrange("(t p) d -> p t d", p=P),
                                 k.X[:, t:t + 2, :]).then_inc(stored, 16)
                sp.wait_ge(stored, 16 * TILES // 2)


def build(nc, ap, out, until=9):
    with ExitStack() as ctx:
        def sb(name, shape, dt=F32):
            return ctx.enter_context(nc.sbuf_tensor(name, shape, dt))

        def sem(name):
            return ctx.enter_context(nc.semaphore(name))

        k = Core()
        k.nc, k.ap, k.out = nc, ap, out
        k.slots0 = nc.dram_tensor("slots0", [ROWS0, D], F32, kind="Internal").ap()
        k.made0 = nc.dram_tensor("made0", [ROWS0, D], F32, kind="Internal").ap()
        k.slots1 = nc.dram_tensor("slots1", [ROWS1, D], F32, kind="Internal").ap()
        k.made1 = nc.dram_tensor("made1", [ROWS1, D], F32, kind="Internal").ap()
        k.X = sb("X", [P, TILES, D])
        k.XN = sb("XN", [P, TILES, D])
        k.stats = sb("stats", [P, TILES, 6])
        k.mv = sb("mv", [P, TILES, 2])
        k.rstd = sb("rstd", [P, TILES])
        k.half_neg = sb("half_neg", [P, H1 * 4])
        k.half_pos = sb("half_pos", [P, H1 * 4])
        k.keyval1 = sb("keyval1", [P, BATCH, IC, D])
        k.small = {name: sb(name, list(shape)) for name, shape in SMALL}
        k.ident = k.small["ident"][:, :]
        k.PS = ctx.enter_context(nc.psum_tensor("PS", [P, 8, 512], F32))
        with ExitStack() as first:
            def sb1(name, shape, dt=F32):
                return first.enter_context(nc.sbuf_tensor(name, shape, dt))
            k.keys0 = sb1("keys0", [P, BATCH, HALVES, HALF_HEADS, CTX])
            k.values0 = sb1("values0", [P, BATCH, HALVES, CHUNKS, 2, VW])
            k.probs = sb1("probs", [P, HALVES, PADDED])
            k.wq0 = sb1("wq0", [P, KC, D])
            k.wo0 = sb1("wo0", [P, KC, D])
            k.w0_in, k.v0_taken = sem("w0_in"), sem("v0_taken")
            context_stage(k)
            if until >= 1:
                attention0_stage(k)
        k.slot0 = sb("slot0", [P, TILES], U32)
        k.expert0 = sb("expert0", [P, SLOT_TILES0], I32)
        if until >= 2:
            route0_stage(k)
            experts_stage(k, "e0", SLOT_TILES0, 1, k.slots0, k.made0,
                          lambda eng, tile: eng.value_load(k.expert0[0:1, bass.ds(tile, 1)],
                                                           min_val=0, max_val=E0 - 1))
            attention1_stage(k)
        if until >= 4:
            k.slot1 = sb("slot1", [P, 2, TILES], U32)
            k.read1 = sb("read1", [P, 2, TILES], U32)
            k.gate1 = sb("gate1", [P, 2, TILES])
            k.plain = sb("plain", [P, TILES, PLAIN])
            route1_stage(k)
            experts_stage(k, "e1", MLPS, CAP // P, k.slots1, k.made1, lambda eng, tile: tile)
            combine_stage(k)
        if until < 9:
            done = sem("done_")
            with nc.Block() as block:
                @block.sync
                def _(sp):
                    sp.dma_start(out.rearrange("(t p) d -> p t d", p=P), k.X[:, :, :]).then_inc(done, 16)
                    sp.wait_ge(done, 16)


def kernel(**inputs):
    import numpy as np
    import concourse.bacc as bacc
    from concourse.bass_utils import run_bass_kernel_spmd

    laid = lay_out(inputs)
    nc = bacc.Bacc("TRN2", target_bir_lowering=False, num_devices=1)
    ap, arrays = {}, {}
    for name, a in laid.items():
        arrays[f"in_{name}"] = a
        ap[name] = nc.dram_tensor(f"in_{name}", a.shape, mybir.dt.from_np(a.dtype), kind="ExternalInput").ap()
    out = nc.dram_tensor("out_0", [N, D], F32, kind="ExternalOutput").ap()
    build(nc, ap, out)
    r = run_bass_kernel_spmd(nc, [arrays], core_ids=[0])
    return r.results[0]["out_0"].reshape(BATCH, SEQ, D)


def lay_out(inputs):
    import numpy as np
    g = {n: np.asarray(a) for n, a in inputs.items()}

    def rows(w):
        return np.ascontiguousarray(w.reshape(w.shape[0] // P, P, *w.shape[1:]).swapaxes(0, 1))

    def f32(a):
        return np.ascontiguousarray(a, dtype=np.float32)

    ctx = g["ctx_1024"]
    ctxT = ctx.transpose(2, 0, 1)
    turn = np.arange(PADDED) % CTX
    ctxTr = np.where(np.arange(PADDED) < ROWS, ctxT[:, :, turn], np.zeros((), ctx.dtype))
    pad = np.zeros((BATCH, 2 * P, D), ctx.dtype)
    pad[:, :CTX] = ctx
    cols = np.array([[h * P + PAIR0[c] * HD0 + np.arange(2 * HD0) for c in range(CHUNKS)] for h in range(HALVES)])
    row = np.arange(PADDED).reshape(CHUNKS, P).T
    head = np.where(row < ROWS, row // CTX, -1)
    part = np.arange(P)
    e8, e16 = np.arange(E0), np.arange(E1)
    laid = {
        "x": g["x"].reshape(N, D),
        "ctx": pad.reshape(BATCH, 2, P, D).transpose(2, 0, 1, 3),
        "ctxT": rows(ctxT), "ctxTr": rows(ctxTr),
        "wq0": rows(g["L0_xattn_Wq"]), "wk0": rows(g["L0_xattn_Wk"]), "wo0": rows(g["L0_xattn_Wo"]),
        "wvg0": rows(g["L0_xattn_Wv"][:, cols]),
        "bq0": g["L0_xattn_bq"].reshape(KC, P).T, "bk0": g["L0_xattn_bk"].reshape(KC, P).T,
        "bvg0": g["L0_xattn_bv"][cols].reshape(1, -1), "bo0": g["L0_xattn_bo"].reshape(1, D),
        "vmask": f32(head[:, :, None] == np.array(PAIR0)[None, :, None] + np.arange(2)),
        "headmask": f32(part[:, None] // HD0 == np.arange(HALF_HEADS)),
        "pairmask": f32(part[:, None] // HD1 == part[None, :] // HD1),
        "wk1": rows(g["L1_xattn_wk"]), "wv1": rows(g["L1_xattn_wv"]), "wq1": rows(g["L1_xattn_wq"]),
        "wo1": rows(g["L1_xattn_wo"]),
        "g1": g["L1_xattn_ln1_g"].reshape(KC, P).T, "be1": g["L1_xattn_ln1_b"].reshape(KC, P).T,
        "g2": g["L1_xattn_ln2_g"].reshape(KC, P).T, "be2": g["L1_xattn_ln2_b"].reshape(KC, P).T,
        "bo1": g["L1_xattn_bo"].reshape(1, D), "mb2": g["L1_xattn_b2"].reshape(1, D),
        "mb1": g["L1_xattn_b1"].reshape(FC, P).T,
        "mw1": rows(g["L1_xattn_w1"]), "mw2": rows(g["L1_xattn_w2"]),
        "wr0": rows(g["L0_ffn_wr"]), "br0": g["L0_ffn_br"].reshape(1, E0),
        "wr1": rows(g["L1_ffn_router_weight"].T), "br1": g["L1_ffn_router_bias"].reshape(1, E1),
        "nw": g["L1_ffn_norm_weight"].reshape(1, D), "cv": g["L1_ffn_constant_vectors"].reshape(1, 2 * D),
        "e0w1": g["L0_ffn_w1"].reshape(E0, KC, P, F).transpose(0, 2, 1, 3),
        "e0w2": g["L0_ffn_w2"].reshape(E0, FC, P, D).transpose(0, 2, 1, 3),
        "e0b1": g["L0_ffn_b1"].reshape(E0, FC, P).transpose(0, 2, 1), "e0b2": g["L0_ffn_b2"],
        "e1w1": g["L1_ffn_fc1_weight"].transpose(0, 2, 1).reshape(MLPS, KC, P, F).transpose(0, 2, 1, 3),
        "e1w2": g["L1_ffn_fc2_weight"].transpose(0, 2, 1).reshape(MLPS, FC, P, D).transpose(0, 2, 1, 3),
        "e1b1": g["L1_ffn_fc1_bias"].reshape(MLPS, FC, P).transpose(0, 2, 1), "e1b2": g["L1_ffn_fc2_bias"],
        "tri": f32(part[:, None] < part[None, :]), "ones": np.ones((P, P), np.float32),
        "ident": np.eye(P, dtype=np.float32),
        "order0": f32(E0 - e8)[None], "order1": f32(E1 - e16)[None],
        "thresh0": f32(P * np.arange(TILES))[None],
        "before0": f32(e8[None, :] < e8[:, None]).reshape(1, -1),
        "tile_no": f32(np.arange(SLOT_TILES0))[None],
        "base1": f32(np.where(e16 < PLAIN, SKIP, (e16 - PLAIN) * CAP))[None],
    }
    shape = {name: s for name, s in SMALL}
    for name, a in laid.items():
        if name in shape and name not in BROADCAST:
            a = a.reshape(P, -1)
        laid[name] = np.ascontiguousarray(a)
    return laid
```

```python
import math
from contextlib import ExitStack

import concourse.bass as bass
from concourse import mybir

F32 = mybir.dt.float32
I32 = mybir.dt.int32
U32 = mybir.dt.uint32
F32R = mybir.dt.float32r
PARTS = ("high", "low")
ACT = mybir.ActivationFunctionType
ALU = mybir.AluOpType
X_AXIS = mybir.AxisListType.X

P = 128
D = 256
KC = D // P
BATCH, SEQ, CTX = 2, 1024, 154
N = BATCH * SEQ
TILES = N // P
TPB = SEQ // P
CTX_SPLIT = ((0, P), (P, CTX - P))
EPS = 1e-5

H0, HD0 = 16, 16
HALF_HEADS = P // HD0
HALVES = H0 // HALF_HEADS
GROUP = 4
GROUPS = H0 // GROUP
GW = GROUP * CTX
ROWS = HALF_HEADS * CTX
CHUNKS = -(-ROWS // P)
PADDED = CHUNKS * P
FILLS = ((0, 4), (4, 4), (8, CHUNKS - 8))
NF = len(FILLS)
VW = HD0 + 1
PAIR0 = [min(P * c // CTX, HALF_HEADS - 2) for c in range(CHUNKS)]

E0, F = 8, 1024
FC = F // P
BLOCKS = 2
W = BLOCKS * P
SLOT_TILES0 = N // W + E0 - 1
ROWS0 = SLOT_TILES0 * W

H1, HD1 = 16, 64
INNER = H1 * HD1
IC = INNER // P

E1, PLAIN = 16, 4
MLPS = E1 - PLAIN
CAP = N * 2 // E1
ROWS1 = MLPS * CAP
ZM = 4
SLOT_STORES = -(-ROWS0 // (ZM * P)) + -(-ROWS1 // (ZM * P))
SKIP = 1 << 20

ROUTER_BANKS = (0, 1, 7)

SMALL = (
    ("bq0", (P, KC)), ("bk0", (P, KC)), ("bv0", (P, D)),
    ("bo0", (P, D)), ("vmask", (P, CHUNKS, 2)), ("headmask", (P, HALF_HEADS)),
    ("pairmask", (P, P)), ("g1", (P, KC)), ("be1", (P, KC)), ("g2", (P, KC)),
    ("be2", (P, KC)), ("bo1", (P, D)), ("mb1", (P, FC)), ("mb2", (P, D)),
    ("wr0", (P, KC, E0)), ("br0", (P, E0)), ("wr1", (P, KC, E1)), ("br1", (P, E1)),
    ("nw", (P, D)), ("cv", (P, 2, D)), ("tri", (P, P)), ("ones", (P, P)), ("ident", (P, P)),
    ("token_no", (P, TILES)), ("order0", (P, E0)), ("order1", (P, E1)), ("thresh0", (P, N // W)),
    ("before0", (P, E0, E0)), ("tile_no", (P, SLOT_TILES0)), ("base1", (P, E1)),
)
BROADCAST = {"bo0", "bo1", "mb2", "br0", "br1", "nw", "cv", "bv0", "order0", "order1", "thresh0",
             "before0", "tile_no", "base1"}

PLAIN_WIDTH = sum(math.prod(s[1:]) for n, s in SMALL if n not in BROADCAST)
SPREAD_WIDTH = sum(math.prod(s[1:]) for n, s in SMALL if n in BROADCAST)


class Own:

    def __init__(self, eng, sem):
        self.eng, self.sem, self.done, self.ahead = eng, sem, 0, 0

    def then(self, ins):
        ins.then_inc(self.sem, 1)
        self.done += 1
        self.eng.wait_ge(self.sem, self.ahead + self.done)

    def enter(self, i, first, per):
        self.base, self.per = self.done, per
        self.ahead = (i - first) * per

    def leave(self, turns):
        assert self.done - self.base == self.per, (self.done - self.base, self.per)
        self.done = self.base + turns * self.per
        self.ahead = 0


class Core:

    def __init__(self):
        self.count = 0
        self.in_use = []

    def stage_semaphore(self, name):
        self.count += 1
        sem = self.nc.alloc_semaphore(name=f"{name}_{self.count}")
        self.in_use.append(sem)
        return sem

    def stage_begins(self):
        self.spent, self.in_use = self.in_use, []

    def clear_spent(self):
        self.nc.clear_and_free_semaphores(self.spent)


def at_least(eng, sem, value):
    if not isinstance(value, int) or value > 0:
        eng.wait_ge(sem, value)


def wide(ap2, shape, axis):
    return ap2.rearrange("p (e a) -> p e a" if axis == 2 else "p (a e) -> p a e", a=1).to_broadcast(shape)


def statistics(k, own, sums):
    nc = k.nc
    for t in range(TILES):
        last = nc.vector.bn_aggr(k.mv[:, t, :], k.stats[:, t, :])
    own.then(last)
    nc.vector.tensor_scalar(k.rstd[:, :], k.mv[:, :, 1], EPS, None, ALU.add).then_inc(sums, 1)


def apply_normalisation(k, t):
    return k.nc.vector.tensor_scalar(k.XN[:, t, :], k.X[:, t, :], k.mv[:, t, 0:1],
                                     k.rstd[:, t:t + 1], ALU.subtract, ALU.mult)


def normalise_vector(k, dve, own, sums, powers, each=None, taken=False):
    if not taken:
        for t in range(TILES):
            last = k.nc.vector.bn_stats(k.stats[:, t, :], k.X[:, t, :])
        own.then(last)
    statistics(k, own, sums)
    dve.wait_ge(powers, 1)
    for t in range(TILES):
        last = apply_normalisation(k, t)
        if each is not None:
            last.then_inc(each, 1)
    return last


def inverse_roots(k, pool, sums, powers):
    pool.wait_ge(sums, 1)
    k.nc.gpsimd.tensor_tensor(k.rstd[:, :], k.rstd[:, :], k.half_neg[:, 0:TILES],
                              ALU.pow).then_inc(powers, 1)


def context_stage(k):
    nc = k.nc
    with ExitStack() as own_memory:
        def sb(name, shape, dt=F32):
            return own_memory.enter_context(nc.sbuf_tensor(name, shape, dt))

        def sem(name):
            return k.stage_semaphore(name)

        ctxT = sb("ctxT", [P, KC, BATCH, CTX])
        C = sb("C", [P, BATCH, 2, D])
        wk0, wv0 = sb("wk0", [P, KC, D]), sb("wv0", [P, KC, D])
        kT = sb("kT", [P, BATCH, HALVES, CTX])
        v0 = sb("v0", [P, BATCH, 2, D])
        v0_rows = sb("v0_rows", [P, BATCH, HALVES, CHUNKS, HD0])
        cst = sb("cst", [P, BATCH, 2, 6])
        cmv = sb("cmv", [P, BATCH, 2, 2])
        crs = sb("crs", [P, BATCH, 2])

        c_in, w0_in = sem("c_in"), sem("w0_in")
        x_in = [sem(f"x_in{q}") for q in range(4)]
        plain_in, spread_in = sem("plain_in"), sem("spread_in")
        dve_own = sem("dve_own")
        cleared, consts_set = sem("cleared"), sem("consts_set")
        k0_made, v0_made, ctx_sums, ctx_roots = sem("k0_made"), sem("v0_made"), sem("ctx_sums"), sem("ctx_roots")
        v0_ready, v0_stored, v0_rows_in = (sem(n) for n in (
            "v0_ready", "v0_stored", "v0_rows_in"))
        c_ready, cT_made = sem("c_ready"), sem("cT_made")
        x_sums, x_roots, x_kept, xb = sem("x_sums"), sem("x_roots"), sem("x_kept"), sem("xb")

        with nc.Block() as block:
            @block.sync
            def _(sp):
                sp.dma_start(ctxT[:, :, :, :], k.ap["ctxT"]).then_inc(w0_in, 16)
                sp.dma_start(wk0[:, :, :], k.ap["wk0"]).then_inc(w0_in, 16)
                sp.dma_start(wv0[:, :, :], k.ap["wv0"]).then_inc(w0_in, 16)
                for q in range(4):
                    sp.dma_start(k.X[:, q * TILES // 4:(q + 1) * TILES // 4, :],
                                 k.ap["x"][q * N // 4:(q + 1) * N // 4, :]
                                 .rearrange("(t p) d -> p t d", p=P)).then_inc(x_in[q], 16)
                sp.dma_start(C[:, :, :, :], k.ap["ctx"]).then_inc(c_in, 16)
                for n in range(4):
                    b, j = divmod(n, 2)
                    a, rows = CTX_SPLIT[j]
                    sp.wait_ge(v0_ready, n + 1)
                    sp.dma_start(k.heads0[b, :, a:a + rows, :].rearrange("h k d -> k h d"),
                                 v0[0:rows, b, j, :].rearrange("p (h d) -> p h d", h=H0)).then_inc(v0_stored, 16)
                sp.wait_ge(v0_stored, 16 * 4)
                for b in range(BATCH):
                    for h in range(HALVES):
                        src = k.heads0[b, h * HALF_HEADS:(h + 1) * HALF_HEADS, :, :].rearrange("h k d -> (h k) d")
                        full = CHUNKS - 1
                        sp.dma_start(v0_rows[:, b, h, 0:full, :],
                                     src[0:full * P, :].rearrange("(i p) d -> p i d", p=P)).then_inc(v0_rows_in, 16)
                        if b == h == 0:
                            sp.wait_ge(cleared, 1)
                        sp.dma_start(v0_rows[0:ROWS - full * P, b, h, full, :],
                                     src[full * P:ROWS, :]).then_inc(v0_rows_in, 16)
                sp.dma_start(k.wq0[:, :, :], k.ap["wq0"]).then_inc(k.w0_in, 16)
                sp.dma_start(k.wo0[:, :, :], k.ap["wo0"]).then_inc(k.w0_in, 16)
                for to, name in ((k.wk1, "wk1"), (k.wv1, "wv1"), (k.wo1, "wo1")):
                    sp.dma_start(to[:, :, :], k.ap[name]).then_inc(k.kv_w_in, 16)
                sp.wait_ge(cleared, 3)
                for rows, buffer in ((ROWS0, k.slots0), (ROWS1, k.slots1)):
                    for a in range(0, rows, ZM * P):
                        m = min(ZM, (rows - a) // P)
                        sp.dma_start(buffer[a:a + m * P, :].rearrange("(p m) d -> p m d", m=m),
                                     k.zeros[:, 0:m, :]).then_inc(k.zeroed, 16)
                sp.wait_ge(k.w0_in, 32)

            @block.scalar
            def _(act):
                act.dma_start(k.plain_pack[:, :], k.ap["plain_pack"]).then_inc(plain_in, 16)
                act.dma_start(k.spread_pack[:, :],
                              k.ap["spread_pack"].to_broadcast((P, SPREAD_WIDTH))).then_inc(spread_in, 16)

            @block.gpsimd
            def _(pool):
                nc.gpsimd.memset(v0_rows[:, :, :, CHUNKS - 1, :], 0.0).then_inc(cleared, 1)
                nc.gpsimd.memset(k.zeros[:, :, 0:D], 0.0).then_inc(cleared, 1)
                nc.gpsimd.memset(k.zeros[:, :, D:D + 1], float(SKIP)).then_inc(cleared, 1)
                pool.wait_ge(consts_set, 2)
                inverse_roots(k, pool, x_sums, x_roots)
                pool.wait_ge(ctx_sums, 1)
                nc.gpsimd.tensor_tensor(crs[:, :, :], crs[:, :, :],
                                        k.half_neg[:, 0:4].rearrange("p (b j) -> p b j", b=2),
                                        ALU.pow).then_inc(ctx_roots, 1)

                pool.wait_ge(spread_in, 16)
                for q in range(4):
                    pool.wait_ge(x_kept, q + 1)
                    x = k.X[:, q * TILES // 4:(q + 1) * TILES // 4, :]
                    nc.gpsimd.tensor_tensor(x, x, wide(k.small["bo0"], (P, TILES // 4, D), 1),
                                            ALU.add).then_inc(xb, 1)
                pool.wait_ge(xb, 4)

            @block.tensor
            def _(pe):
                pe.wait_ge(w0_in, 16 * 3)
                for n in range(4):
                    b, h = divmod(n, 2)
                    for c in range(KC):
                        last = nc.tensor.matmul(k.PS[:, 4 + n // 2, (n % 2) * CTX:(n % 2 + 1) * CTX],
                                                wk0[:, c, h * P:(h + 1) * P], ctxT[:, c, b, :],
                                                start=c == 0, stop=c == KC - 1)
                last.then_inc(k0_made, 1)
                for n in range(4):
                    b, j = divmod(n, 2)
                    a, rows = CTX_SPLIT[j]
                    for c in range(KC):
                        last = nc.tensor.matmul(k.PS[0:rows, n, 0:D], ctxT[:, c, b, a:a + rows], wv0[:, c, :],
                                                start=c == 0, stop=c == KC - 1)
                    last.then_inc(v0_made, 1)
                pe.wait_ge(plain_in, 16)
                pe.wait_ge(c_ready, 1)
                for b in range(BATCH):
                    for j, (a, rows) in enumerate(CTX_SPLIT):
                        for c in range(KC):
                            last = nc.tensor.transpose(
                                k.PS[:, 6 + b, c * CTX + a:c * CTX + a + rows],
                                C[0:rows, b, j, c * P:(c + 1) * P], k.ident[0:rows, 0:rows])
                last.then_inc(cT_made, 1)

            @block.vector
            def _(dve):
                own = Own(dve, dve_own)
                nc.vector.memset(k.half_neg[:, :], -0.5).then_inc(consts_set, 1)
                nc.vector.memset(k.half_pos[:, :], 0.5).then_inc(consts_set, 1)
                for h in range(HALVES):
                    nc.vector.memset(k.probs[:, h, ROWS:PADDED], 0.0)
                own.then(nc.vector.memset(crs[:, :, :], 1.0))
                for q in range(4):
                    dve.wait_ge(x_in[q], 16)
                    for t in range(q * TILES // 4, (q + 1) * TILES // 4):
                        last = nc.vector.bn_stats(k.stats[:, t, :], k.X[:, t, :])
                own.then(last)
                statistics(k, own, x_sums)
                dve.wait_ge(spread_in, 16)
                for n in range(4):
                    b, j = divmod(n, 2)
                    rows = CTX_SPLIT[j][1]
                    dve.wait_ge(v0_made, n + 1)
                    nc.vector.tensor_tensor(v0[0:rows, b, j, :], k.PS[0:rows, n, 0:D], k.small["bv0"][0:rows, :],
                                            ALU.add).then_inc(v0_ready, 1)
                dve.wait_ge(c_in, 16)
                for b in range(BATCH):
                    for j, (a, rows) in enumerate(CTX_SPLIT):
                        last = nc.vector.bn_stats(cst[0:rows, b, j, :], C[0:rows, b, j, :])
                own.then(last)
                for b in range(BATCH):
                    for j, (a, rows) in enumerate(CTX_SPLIT):
                        last = nc.vector.bn_aggr(cmv[0:rows, b, j, :], cst[0:rows, b, j, :])
                own.then(last)
                for j, (a, rows) in enumerate(CTX_SPLIT):
                    last = nc.vector.tensor_scalar(crs[0:rows, :, j], cmv[0:rows, :, j, 1], EPS, None, ALU.add)
                last.then_inc(ctx_sums, 1)
                dve.wait_ge(x_roots, 1)
                for t in range(TILES):
                    last = apply_normalisation(k, t)
                    if t % (TILES // 4) == TILES // 4 - 1:
                        last.then_inc(x_kept, 1)
                dve.wait_ge(ctx_roots, 1)
                for b in range(BATCH):
                    for j, (a, rows) in enumerate(CTX_SPLIT):
                        last = nc.vector.tensor_scalar(C[0:rows, b, j, :], C[0:rows, b, j, :],
                                                       cmv[0:rows, b, j, 0:1], crs[0:rows, b, j:j + 1],
                                                       ALU.subtract, ALU.mult)
                last.then_inc(c_ready, 1)
                dve.wait_ge(k0_made, 1)
                dve.wait_ge(plain_in, 16)
                for n in range(4):
                    b, h = divmod(n, 2)
                    last = nc.vector.tensor_scalar(kT[:, b, h, :],
                                                   k.PS[:, 4 + n // 2, (n % 2) * CTX:(n % 2 + 1) * CTX],
                                                   k.small["bk0"][:, h:h + 1], None, ALU.add)
                own.then(last)
                for n in range(4):
                    b, h = divmod(n, 2)
                    nc.vector.tensor_tensor(k.keys0[:, b, h, :, :], wide(kT[:, b, h, :], (P, HALF_HEADS, CTX), 1),
                                            wide(k.small["headmask"], (P, HALF_HEADS, CTX), 2), ALU.mult)
                dve.wait_ge(cT_made, 1)
                for b in range(BATCH):
                    for c in range(KC):
                        nc.vector.tensor_scalar(k.cnT[:, c, b, :], k.PS[:, 6 + b, c * CTX:(c + 1) * CTX],
                                                k.small["g1"][:, c:c + 1], k.small["be1"][:, c:c + 1],
                                                ALU.mult, ALU.add)
                dve.wait_ge(v0_rows_in, 16 * 8)
                for n in range(4):
                    b, h = divmod(n, 2)
                    for w in range(2):
                        mask = k.small["vmask"][:, :, w:w + 1]
                        nc.vector.tensor_tensor(k.values0[:, b, h, :, w, 0:HD0], v0_rows[:, b, h, :, :],
                                                mask.to_broadcast((P, CHUNKS, HD0)), ALU.mult)
                        nc.vector.tensor_copy(k.values0[:, b, h, :, w, HD0:VW], mask)


def attention0_stage(k):
    nc = k.nc
    k.stage_begins()
    with ExitStack() as own_memory:
        def sb(name, shape, dt=F32):
            return own_memory.enter_context(nc.sbuf_tensor(name, shape, dt))

        def sem(name):
            return k.stage_semaphore(name)

        xT = sb("xT", [P, KC, P])
        qT = sb("qT", [P, HALVES, P])
        peak = sb("peak", [P, GROUPS, GROUP])
        pT = sb("pT", [P, HALVES, CHUNKS, P])
        inv = sb("inv", [P, H0])
        O = sb("O", [P, H0, HD0])
        oT = sb("oT", [P, KC, P])

        scored = sem("scored")
        shifted = sem("shifted")
        raised = sem("raised")
        turned = sem("turned")
        turned_kept = sem("turned_kept")
        summed = sem("summed")
        divided = sem("divided")
        x_turned, xT_ready = sem("x_turned"), sem("xT_ready")
        q_made, qT_ready = sem("q_made"), sem("qT_ready")
        o_turned, oT_ready = sem("o_turned"), sem("oT_ready")
        o_made, x_added = sem("o_made"), sem("x_added")
        x_in_ready = sem("x_in_ready")
        xin = sb("xin", [P, D])
        dve_own = sem("dve_own")
        BANK_T, BANK_V, BANK_M = 4, 6, 7
        M = k.PS[:, BANK_M, :]

        def group_bank(g):
            return 2 * (g % 2)

        with nc.Block() as block:
            @block.tensor
            def _(pe):
                def turn_x(t):
                    at_least(pe, x_added, t - 2)
                    for c in range(KC):
                        last = nc.tensor.transpose(M[:, c * P:(c + 1) * P], xin[:, c * P:(c + 1) * P], k.ident)
                    last.then_inc(x_turned, 1)

                def project_q(t):
                    pe.wait_ge(xT_ready, t + 1)
                    for h in range(HALVES):
                        for c in range(KC):
                            last = nc.tensor.matmul(M[:, h * P:(h + 1) * P], k.wq0[:, c, h * P:(h + 1) * P],
                                                    xT[:, c, :], start=c == 0, stop=c == KC - 1)
                    last.then_inc(q_made, 1)

                def score(t, h, b):
                    if h == 0:
                        pe.wait_ge(qT_ready, t + 1)
                    for g in (2 * h, 2 * h + 1):
                        at_least(pe, shifted, 4 * t + g - 1)
                        for q in range(2):
                            a = (g % 2) * GROUP + q * 2
                            last = nc.tensor.matmul(
                                k.PS[:, group_bank(g) + q, 0:2 * CTX], qT[:, h, :],
                                k.keys0[:, b, h, a:a + 2, :], start=True, stop=True)
                        last.then_inc(scored, 1)

                def turn(t, h):
                    pe.wait_ge(raised, 4 * t + 2 * h + 2)
                    for f, (c0, m) in enumerate(FILLS):
                        n = 2 * NF * t + NF * h + f
                        at_least(pe, turned_kept, n - 1)
                        for c in range(m):
                            last = nc.tensor.transpose(
                                k.PS[:, BANK_T + (NF * h + f) % 2, c * P:(c + 1) * P],
                                k.probs[:, h, (c0 + c) * P:(c0 + c + 1) * P], k.ident)
                        last.then_inc(turned, 1)

                def weigh(t, h, b):
                    at_least(pe, divided, 2 * t + h)
                    for f, (c0, m) in enumerate(FILLS):
                        pe.wait_ge(turned_kept, 2 * NF * t + NF * h + f + 1)
                        for c in range(c0, c0 + m):
                            a = PAIR0[c] * VW
                            last = nc.tensor.matmul(
                                k.PS[:, BANK_V, a:a + 2 * VW], pT[:, h, c, :],
                                k.values0[:, b, h, c, :, :], start=c == 0, stop=c == CHUNKS - 1,
                                skip_group_check=True)
                    last.then_inc(summed, 1)

                def turn_o(t, prepared):
                    pe.wait_ge(qT_ready, prepared)
                    pe.wait_ge(divided, 2 * t + 2)
                    flat = O[:, :, :].rearrange("p h d -> p (h d)")
                    for c in range(KC):
                        last = nc.tensor.transpose(M[:, c * P:(c + 1) * P], flat[:, c * P:(c + 1) * P], k.ident)
                    last.then_inc(o_turned, 1)

                def project_o(t):
                    pe.wait_ge(oT_ready, t + 1)
                    for c in range(KC):
                        last = nc.tensor.matmul(M[:, 0:D], oT[:, c, :], k.wo0[:, c, :],
                                                start=c == 0, stop=c == KC - 1)
                    last.then_inc(o_made, 1)

                def tile(t, b, before, after):
                    score(t, 0, b)
                    if after:
                        pe.wait_ge(x_in_ready, t + 2)
                        turn_x(t + 1)
                    if before:
                        turn(t - 1, 1)
                        weigh(t - 1, 1, b_before(t, b))
                    score(t, 1, b)
                    if after:
                        project_q(t + 1)
                    turn(t, 0)
                    if before:
                        turn_o(t - 1, t + 2 if after else TILES)
                    weigh(t, 0, b)
                    if before:
                        project_o(t - 1)

                def b_before(t, b):
                    return 0 if isinstance(t, int) and t == TPB else b

                pe.wait_ge(x_in_ready, 1)
                turn_x(0)
                project_q(0)
                tile(0, 0, False, True)
                tile(1, 0, True, True)
                with pe.Fori(2, TPB) as t:
                    tile(t, 0, True, True)
                tile(TPB, 1, True, True)
                with pe.Fori(TPB + 1, TILES - 1) as t:
                    tile(t, 1, True, True)
                tile(TILES - 1, 1, True, False)
                turn(TILES - 1, 1)
                weigh(TILES - 1, 1, 1)
                turn_o(TILES - 1, TILES)
                project_o(TILES - 1)

            @block.gpsimd
            def _(pool):
                def stage_in(t):
                    at_least(pool, x_turned, t)
                    nc.gpsimd.tensor_copy(xin[:, :], k.XN[:, t, :]).then_inc(x_in_ready, 1)

                k.clear_spent()
                stage_in(0)
                with pool.Fori(1, TILES) as t:
                    stage_in(t)

            @block.scalar
            def _(act):
                def raise_scores(t, h):
                    for g in (2 * h, 2 * h + 1):
                        act.wait_ge(shifted, 4 * t + g + 1)
                        part = k.probs[:, h, (g % 2) * GW:(g % 2 + 1) * GW]
                        nc.scalar.activation(part, part, ACT.Exp, scale=HD0 ** -0.5).then_inc(raised, 1)

                def keep_turned(t, h):
                    at_least(act, summed, 2 * t + h - 1)
                    for f, (c0, m) in enumerate(FILLS):
                        act.wait_ge(turned, 2 * NF * t + NF * h + f + 1)
                        nc.scalar.activation(
                            pT[:, h, c0:c0 + m, :],
                            k.PS[:, BANK_T + (NF * h + f) % 2, 0:m * P].rearrange("p (c q) -> p c q", c=m),
                            ACT.Copy).then_inc(turned_kept, 1)

                def keep_o(t):
                    act.wait_ge(o_turned, t + 1)
                    nc.scalar.activation(oT[:, :, :], M[:, 0:D].rearrange("p (c q) -> p c q", c=KC),
                                         ACT.Copy).then_inc(oT_ready, 1)

                def tile(t, before):
                    if before:
                        keep_turned(t - 1, 1)
                    raise_scores(t, 0)
                    keep_turned(t, 0)
                    if before:
                        keep_o(t - 1)
                    raise_scores(t, 1)

                tile(0, False)
                tile(1, True)
                with act.Fori(2, TILES) as t:
                    tile(t, True)
                keep_turned(TILES - 1, 1)
                keep_o(TILES - 1)

            @block.vector
            def _(dve):
                own = Own(dve, dve_own)

                def shift(t, g):
                    h = g // 2
                    scores = k.PS[:, group_bank(g):group_bank(g) + 2, 0:2 * CTX].rearrange(
                        "p q (h k) -> p q h k", h=2)
                    top = peak[:, g, :].rearrange("p (q h) -> p q h", q=2)
                    dve.wait_ge(scored, 4 * t + g + 1)
                    own.then(nc.vector.tensor_reduce(top, scores, X_AXIS, ALU.max))
                    at_least(dve, turned, 2 * NF * (t - 1) + NF * (h + 1))
                    for q in range(2):
                        a = (g % 2) * GW + q * 2 * CTX
                        last = nc.vector.tensor_tensor(
                            k.probs[:, h, a:a + 2 * CTX].rearrange("p (h k) -> p h k", h=2),
                            scores[:, q, :, :],
                            peak[:, g, 2 * q:2 * q + 2].rearrange("p (h a) -> p h a", a=1)
                            .to_broadcast((P, 2, CTX)), ALU.subtract)
                    last.then_inc(shifted, 1)

                def keep_x(t):
                    dve.wait_ge(x_turned, t + 1)
                    nc.vector.tensor_copy(xT[:, :, :], M[:, 0:D].rearrange("p (c q) -> p c q", c=KC))\
                        .then_inc(xT_ready, 1)

                def keep_q(t):
                    dve.wait_ge(q_made, t + 1)
                    for h in range(HALVES):
                        last = nc.vector.tensor_scalar(qT[:, h, :], M[:, h * P:(h + 1) * P],
                                                       k.small["bq0"][:, h:h + 1], None, ALU.add)
                    last.then_inc(qT_ready, 1)

                def divide(t, h):
                    out = k.PS[:, BANK_V, 0:HALF_HEADS * VW].rearrange("p (h v) -> p h v", v=VW)
                    part = inv[:, h * HALF_HEADS:(h + 1) * HALF_HEADS].rearrange("p (h a) -> p h a", a=1)
                    dve.wait_ge(summed, 2 * t + h + 1)
                    own.then(nc.vector.reciprocal(part, out[:, :, HD0:VW]))
                    at_least(dve, o_turned, t)
                    nc.vector.tensor_tensor(O[:, h * HALF_HEADS:(h + 1) * HALF_HEADS, :], out[:, :, 0:HD0],
                                            part.to_broadcast((P, HALF_HEADS, HD0)),
                                            ALU.mult).then_inc(divided, 1)

                def add_x(t):
                    dve.wait_ge(o_made, t + 1)
                    nc.vector.tensor_tensor(k.X[:, t, :], M[:, 0:D], k.X[:, t, :], ALU.add)\
                        .then_inc(x_added, 1)
                    dve.wait_ge(x_added, t + 1)
                    nc.vector.bn_stats(k.stats[:, t, :], k.X[:, t, :])

                def tile(t, before, after):
                    shift(t, 0)
                    shift(t, 1)
                    if after:
                        keep_x(t + 1)
                    if before:
                        divide(t - 1, 1)
                    shift(t, 2)
                    shift(t, 3)
                    if after:
                        keep_q(t + 1)
                    divide(t, 0)
                    if before:
                        add_x(t - 1)

                keep_x(0)
                keep_q(0)
                tile(0, False, True)
                tile(1, True, True)
                with dve.Fori(2, TILES - 1) as t:
                    own.enter(t, 2, GROUPS + HALVES)
                    tile(t, True, True)
                own.leave(TILES - 3)
                tile(TILES - 1, True, False)
                divide(TILES - 1, 1)
                add_x(TILES - 1)


def experts_stage(k, layer, count, slots, made, expert_of):
    nc = k.nc
    w1, w2, b1, b2 = (k.ap[f"{layer}{w}"] for w in ("w1", "w2", "b1", "b2"))
    HB = W * FC // 512
    CPB = FC // HB
    BANK_X, BANK_Y = 4, 5
    with ExitStack() as own_memory:
        def sb(name, shape, dt=F32):
            return own_memory.enter_context(nc.sbuf_tensor(f"{layer}_{name}", shape, dt))

        def sem(name):
            return k.stage_semaphore(f"{layer}_{name}")

        rows = sb("rows", [P, 2, BLOCKS, D + 1])
        numbers = sb("numbers", [P, count, BLOCKS])
        to = sb("to", [P, 2, BLOCKS], U32)
        seen = sb("seen", [P, count])
        xT = [sb(f"rowsT_{part}", [P, 2, KC, W], F32R) for part in PARTS]
        h = sb("h", [P, FC, W])
        hT = [sb(f"hT_{part}", [P, 2, FC, W], F32R) for part in PARTS]
        w1_sb, w2_sb = sb("w1_sb", [P, KC, F]), sb("w2_sb", [P, FC, D])
        w1_parts = [sb(f"w1_{part}", [P, 2, KC, F], F32R) for part in PARTS]
        w2_parts = [sb(f"w2_{part}", [P, 2, FC, D], F32R) for part in PARTS]
        b1_sb, b2_sb = sb("b1_sb", [P, 2, FC]), sb("b2_sb", [P, 2, D])
        y = sb("y", [P, 2, BLOCKS, D])
        w1_in, w2_in = sem("w1_in"), sem("w2_in")
        rows_in, b1_in, b2_in, stored = (
            [sem(f"{name}{r}") for r in range(2)] for name in ("rows_in", "b1_in", "b2_in", "stored"))
        turned, numbered = sem("rows_turned"), sem("numbered")
        xT_high, xT_ready = sem("rowsT_high"), sem("rowsT_ready")
        w1_high, w1_ready, w2_high, w2_ready = (sem(n) for n in ("w1_high", "w1_ready", "w2_high", "w2_ready"))
        upped = sem("upped")
        bent = sem("bent")
        h_high, h_ready = sem("h_high"), sem("h_ready")
        downed, y_ready = sem("downed"), sem("y_ready")

        def after(i, back=0):
            j, r = i
            return 2 * j + r + 1 - back

        def place(n):
            return divmod(n, 2)

        def tiles(eng, one):
            for n in range(3):
                one(place(n), n == 0, False)
            turns = (count - 4) // 2
            with eng.Fori(1, 1 + turns) as j:
                one((j, 1), False, False)
                one((j + 1, 0), False, False)
            for n in range(3 + 2 * turns, count):
                one(place(n), False, n == count - 1)

        def before(i):
            j, r = i
            return (j, 0) if r else (j - 1, 1)

        def behind(i):
            j, r = i
            return (j + 1, 0) if r else (j, 1)

        with nc.Block() as block:
            @block.sync
            def _(sp):
                def load(i):
                    j, r = i
                    e = expert_of(sp, 2 * j + r)
                    at_least(sp, w1_ready, after(i, 1))
                    sp.dma_start(w1_sb[:, :, :], w1[bass.ds(e, 1), :, :, :]
                                 .rearrange("a p c f -> p (a c) f")).then_inc(w1_in, 16)
                    at_least(sp, numbered, after(i, 2))
                    sp.dma_start(rows[:, r, :, :],
                                 slots.rearrange("(i n p) d -> i p n d", p=P, n=BLOCKS)[
                                     bass.ds(2 * j + r, 1), :, :, :]
                                 .rearrange("a p n d -> p (a n) d")).then_inc(rows_in[r], 16)
                    at_least(sp, w2_ready, after(i, 1))
                    sp.dma_start(w2_sb[:, :, :], w2[bass.ds(e, 1), :, :, :]
                                 .rearrange("a p c d -> p (a c) d")).then_inc(w2_in, 16)
                    at_least(sp, bent, HB * after(i, 2))
                    sp.dma_start(b1_sb[:, r, :], b1[bass.ds(e, 1), :, :].rearrange("a p f -> p (a f)"))\
                        .then_inc(b1_in[r], 16)

                def load_last_bias(i):
                    j, r = i
                    e = expert_of(sp, 2 * j + r)
                    at_least(sp, y_ready, after(i, 2))
                    sp.dma_start(b2_sb[:, r, :], b2[bass.ds(e, 1), :].to_broadcast((P, D))).then_inc(b2_in[r], 16)

                def tile(i, first, last):
                    load(i)
                    if not first:
                        load_last_bias(before(i))

                tiles(sp, tile)
                load_last_bias(place(count - 1))

            @block.tensor
            def _(pe):
                def product(out, left, right, first, last):
                    for n, (a, b) in enumerate(((0, 0), (0, 1), (1, 0))):
                        ins = nc.tensor.matmul(out, left(a), right(b), start=first and n == 0, stop=last and n == 2)
                    return ins

                def turn(i):
                    j, r = i
                    pe.wait_ge(rows_in[r], 16 * (j + 1))
                    at_least(pe, xT_ready, after(i, 1))
                    for n in range(BLOCKS):
                        for c in range(KC):
                            last = nc.tensor.transpose(k.PS[:, BANK_X, c * W + n * P:c * W + (n + 1) * P],
                                                       rows[:, r, n, c * P:(c + 1) * P], k.ident)
                    last.then_inc(turned, 1)

                def up(i, first):
                    j, r = i
                    pe.wait_ge(w1_ready, after(i))
                    pe.wait_ge(xT_ready, after(i))
                    for q in range(HB):
                        if not first:
                            at_least(pe, bent, HB * after(i, 2) + q + 1)
                        for f in range(q * CPB, (q + 1) * CPB):
                            for c in range(KC):
                                last = product(k.PS[:, q, (f - q * CPB) * W:(f - q * CPB + 1) * W],
                                               lambda a: w1_parts[a][:, r, c, f * P:(f + 1) * P],
                                               lambda b: xT[b][:, r, c, :], c == 0, c == KC - 1)
                        last.then_inc(upped, 1)

                def down(i):
                    j, r = i
                    pe.wait_ge(w2_ready, after(i))
                    pe.wait_ge(h_ready, HB * after(i))
                    at_least(pe, y_ready, after(i, 2))
                    for n in range(BLOCKS):
                        for f in range(FC):
                            last = product(k.PS[:, BANK_Y + r, n * D:(n + 1) * D],
                                           lambda a: hT[a][:, r, f, n * P:(n + 1) * P],
                                           lambda b: w2_parts[b][:, r, f, :], f == 0, f == FC - 1)
                    last.then_inc(downed, 1)

                def tile(i, first, last):
                    up(i, first)
                    if not last:
                        turn(behind(i))
                    if not first:
                        down(before(i))

                turn((0, 0))
                tiles(pe, tile)
                down(place(count - 1))

            @block.scalar
            def _(act):
                def high_w1(i):
                    j, r = i
                    act.wait_ge(w1_in, 16 * after(i))
                    at_least(act, upped, HB * after(i, 2))
                    nc.scalar.activation(w1_parts[0][:, r, :, :], w1_sb[:, :, :], ACT.Copy).then_inc(w1_high, 1)

                def high_w2(i):
                    j, r = i
                    act.wait_ge(w2_in, 16 * after(i))
                    at_least(act, downed, after(i, 2))
                    nc.scalar.activation(w2_parts[0][:, r, :, :], w2_sb[:, :, :], ACT.Copy).then_inc(w2_high, 1)

                def high_x(i):
                    j, r = i
                    act.wait_ge(turned, after(i))
                    at_least(act, upped, HB * after(i, 2))
                    nc.scalar.activation(xT[0][:, r, :, :],
                                         k.PS[:, BANK_X, 0:KC * W].rearrange("p (c w) -> p c w", c=KC),
                                         ACT.Copy).then_inc(xT_high, 1)

                def bend(i, first):
                    j, r = i
                    act.wait_ge(b1_in[r], 16 * (j + 1))
                    at_least(act, downed, after(i, 2))
                    for q in range(HB):
                        act.wait_ge(upped, HB * after(i, 1) + q + 1)
                        if not first:
                            at_least(act, h_ready, HB * after(i, 2) + q + 1)
                        for f in range(q * CPB, (q + 1) * CPB):
                            last = nc.scalar.activation(
                                h[:, f, :], k.PS[:, q, (f - q * CPB) * W:(f - q * CPB + 1) * W],
                                ACT.Gelu, bias=b1_sb[:, r, f:f + 1])
                        last.then_inc(bent, 1)
                        act.wait_ge(bent, HB * after(i, 1) + q + 1)
                        part = slice(q * CPB, (q + 1) * CPB)
                        nc.scalar.activation(hT[0][:, r, part, :], h[:, part, :], ACT.Copy).then_inc(h_high, 1)

                def tile(i, first, last):
                    if not last:
                        high_w1(behind(i))
                    bend(i, first)
                    if not last:
                        high_x(behind(i))
                        high_w2(behind(i))

                high_x((0, 0))
                high_w1((0, 0))
                high_w2((0, 0))
                tiles(act, tile)

            @block.gpsimd
            def _(pool):
                def store(i):
                    pool.wait_ge(y_ready, after(i))
                    nc.gpsimd.tensor_tensor(seen[:, bass.ds(2 * i[0] + i[1], 1)], k.half_neg[:, 0:1],
                                            k.half_neg[:, 0:1], ALU.add)
                    for n in range(BLOCKS):
                        nc.gpsimd.indirect_dma_start(
                            out=made, out_offset=bass.IndirectOffsetOnAxis(ap=to[:, i[1], n:n + 1], axis=0),
                            in_=y[:, i[1], n, :], in_offset=None, bounds_check=made.shape[0] - 1,
                            oob_is_err=False).then_inc(stored[i[1]], 16)

                tiles(pool, lambda i, first, last: store(i))
                for r in range(2):
                    pool.wait_ge(stored[r], 16 * BLOCKS * ((count + 1 - r) // 2))

            @block.vector
            def _(dve):
                def low(to, of, high):
                    return nc.vector.tensor_tensor(to, of, high.bitcast(F32), ALU.subtract)

                def low_w1(i):
                    r = i[1]
                    dve.wait_ge(w1_high, after(i))
                    low(w1_parts[1][:, r, :, :], w1_sb[:, :, :], w1_parts[0][:, r, :, :]).then_inc(w1_ready, 1)

                def low_w2(i):
                    r = i[1]
                    dve.wait_ge(w2_high, after(i))
                    low(w2_parts[1][:, r, :, :], w2_sb[:, :, :], w2_parts[0][:, r, :, :]).then_inc(w2_ready, 1)

                def low_x(i):
                    j, r = i
                    dve.wait_ge(xT_high, after(i))
                    low(xT[1][:, r, :, :], k.PS[:, BANK_X, 0:KC * W].rearrange("p (c w) -> p c w", c=KC),
                        xT[0][:, r, :, :]).then_inc(xT_ready, 1)
                    nc.vector.tensor_copy(numbers[:, bass.ds(2 * j + r, 1), :],
                                          rows[:, r:r + 1, :, D]).then_inc(numbered, 1)

                def low_h(i):
                    r = i[1]
                    for q in range(HB):
                        part = slice(q * CPB, (q + 1) * CPB)
                        dve.wait_ge(h_high, HB * after(i, 1) + q + 1)
                        low(hT[1][:, r, part, :], h[:, part, :], hT[0][:, r, part, :]).then_inc(h_ready, 1)

                def keep_y(i):
                    j, r = i
                    dve.wait_ge(b2_in[r], 16 * (j + 1))
                    dve.wait_ge(downed, after(i))
                    at_least(dve, stored[r], 16 * BLOCKS * j)
                    dve.wait_ge(numbered, after(i))
                    nc.vector.tensor_copy(to[:, r:r + 1, :], numbers[:, bass.ds(2 * j + r, 1), :])
                    nc.vector.tensor_tensor(
                        y[:, r, :, :], k.PS[:, BANK_Y + r, 0:BLOCKS * D].rearrange("p (n d) -> p n d", n=BLOCKS),
                        b2_sb[:, r:r + 1, :].to_broadcast((P, BLOCKS, D)), ALU.add).then_inc(y_ready, 1)

                def tile(i, first, last):
                    if not last:
                        low_w1(behind(i))
                    low_h(i)
                    if not last:
                        low_x(behind(i))
                        low_w2(behind(i))
                    if not first:
                        keep_y(before(i))

                low_x((0, 0))
                low_w1((0, 0))
                low_w2((0, 0))
                tiles(dve, tile)
                keep_y(place(count - 1))


def router_tensor(k, pe, experts, weights, xn_ready, turned, hT, hT_ready, scored):
    nc = k.nc
    for t in range(TILES + 2):
        if t < TILES:
            pe.wait_ge(xn_ready, t + 1)
            at_least(pe, hT_ready, t - 2)
            for c in range(KC):
                last = nc.tensor.transpose(k.PS[:, ROUTER_BANKS[t % 3], c * P:(c + 1) * P],
                                           k.XN[:, t, c * P:(c + 1) * P], k.ident)
            last.then_inc(turned, 1)
        if t > 1:
            pe.wait_ge(hT_ready, t - 1)
            for c in range(KC):
                last = nc.tensor.matmul(k.PS[:, 2, (t - 2) * experts:(t - 1) * experts], hT[:, (t - 2) % 3, c, :],
                                        weights[:, c, :], start=c == 0, stop=c == KC - 1)
            last.then_inc(scored, 1)


def router_scalar(k, act, turned, hT, hT_ready, scored):
    for t in range(TILES):
        act.wait_ge(turned, t + 1)
        at_least(act, scored, t - 2)
        k.nc.scalar.activation(hT[:, t % 3, :, :],
                               k.PS[:, ROUTER_BANKS[t % 3], 0:D].rearrange("p (c q) -> p c q", c=KC),
                               ACT.Copy).then_inc(hT_ready, 1)


def running_sum(k, own, source, odd, even):
    nc = k.nc
    for step, to in ((1, odd), (2, even), (4, odd), (8, even)):
        nc.vector.tensor_copy(to[:, 0:step, :], source[:, 0:step, :])
        own.then(nc.vector.tensor_tensor(to[:, step:TILES, :], source[:, step:TILES, :],
                                         source[:, 0:TILES - step, :], ALU.add))
        source = to


def first_of_largest(k, own, one_hot, scores, top, order, experts):
    nc = k.nc
    shape = (P, TILES, experts)
    own.then(nc.vector.tensor_reduce(top, scores, X_AXIS, ALU.max))
    own.then(nc.vector.tensor_tensor(one_hot, scores, wide(top, shape, 2), ALU.is_equal))
    own.then(nc.vector.tensor_tensor(one_hot, one_hot, wide(order, shape, 1), ALU.mult))
    own.then(nc.vector.tensor_reduce(top, one_hot, X_AXIS, ALU.max))
    own.then(nc.vector.tensor_tensor(one_hot, one_hot, wide(top, shape, 2), ALU.is_equal))


def route0_stage(k):
    nc = k.nc
    with ExitStack() as own_memory:
        def sb(name, shape, dt=F32):
            return own_memory.enter_context(nc.sbuf_tensor(name, shape, dt))

        def sem(name):
            return k.stage_semaphore(name)

        hT = sb("hT0", [P, 3, KC, P])
        logits = sb("logits", [P, TILES, E0])
        one_hot = sb("one_hot", [P, TILES, E0])
        upto, part_sum = sb("upto", [P, TILES + 1, E0]), sb("part_sum", [P, TILES, E0])
        place = sb("place", [P, TILES, E0])
        top = sb("top", [P, TILES])
        grid = sb("grid", [P, E0, N // W])
        tiles_of = sb("tiles_of", [P, E0])
        start = sb("start", [P, E0])
        square = sb("square", [P, E0, E0])
        over = sb("over", [P, SLOT_TILES0, E0])
        expert = sb("expert", [P, SLOT_TILES0])
        slot = sb("slot", [P, TILES])
        dve_own, sums, powers = sem("dve_own"), sem("sums"), sem("powers")
        xn_ready, turned, hT_ready, scored = sem("xn_ready"), sem("turned"), sem("hT_ready"), sem("scored")
        chosen, ranked, slots_ready, scattered = sem("chosen"), sem("ranked"), sem("slots_ready"), sem("scattered")
        kn = sb("kn", [P, BATCH, 2, INNER])
        vn = sb("vn", [P, BATCH, 2, INNER])
        sq = sb("sq", [P, INNER])
        kvT = sb("kvT", [P, 2, P])
        ss = sb("ss", [P, BATCH, 2, H1])
        k_made, v_made, sq_made, v_taken = sem("k_made"), sem("v_made"), sem("sq_made"), sem("v_taken")
        k_copied, k_sums, k_roots, kn_ready = sem("k_copied"), sem("k_sums"), sem("k_roots"), sem("kn_ready")
        kvT_made, kvT_ready, m_made, m_taken = sem("kvT_made"), sem("kvT_ready"), sem("m_made"), sem("m_taken")
        BANK_K, BANK_V = 3, 5
        BANK_R = 2
        RANKS, COUNTS = TILES * E0, 2 * TILES * E0
        PAIR_BANKS, M_BANKS = (0, 1), (7, 3)
        with nc.Block() as block:
            @block.tensor
            def _(pe):
                def keys(n):
                    project(n, k.wk1, BANK_K, k_copied, k_made)

                def values(n):
                    project(n, k.wv1, BANK_V, v_taken, v_made)

                def project(n, weights, bank, taken, made):
                    b, j = divmod(n, 2)
                    a, rows = CTX_SPLIT[j]
                    at_least(pe, taken, n)
                    for q in range(2):
                        for c in range(KC):
                            last = nc.tensor.matmul(k.PS[0:rows, bank + q, :], k.cnT[:, c, b, a:a + rows],
                                                    weights[:, c, q * 512:(q + 1) * 512],
                                                    start=c == 0, stop=c == KC - 1)
                    last.then_inc(made, 1)

                pe.wait_ge(k.kv_w_in, 16 * 3)
                keys(0)
                values(0)
                router_tensor(k, pe, E0, k.small["wr0"], xn_ready, turned, hT, hT_ready, scored)
                keys(1)
                pe.wait_ge(chosen, 1)
                nc.tensor.matmul(k.PS[:, BANK_R, RANKS:RANKS + TILES * E0], k.small["tri"],
                                 one_hot[:, :, :], start=True, stop=False)
                nc.tensor.matmul(k.PS[:, BANK_R, RANKS:RANKS + TILES * E0], k.small["ones"],
                                 upto[:, 0:TILES, :], start=False, stop=True)
                nc.tensor.matmul(k.PS[:, BANK_R, COUNTS:COUNTS + E0], k.small["ones"], upto[:, TILES, :],
                                 start=True, stop=True).then_inc(ranked, 1)
                values(1)
                for n in (2, 3):
                    keys(n)
                    values(n)

                def pair_product(n):
                    b, i = divmod(n, IC)
                    pe.wait_ge(kn_ready, 2 * b + 2)
                    pe.wait_ge(v_taken, 2 * b + 2)
                    at_least(pe, kvT_ready, n - 1)
                    for j, (a, rows) in enumerate(CTX_SPLIT):
                        last = nc.tensor.matmul(k.PS[:, PAIR_BANKS[n % 2], 0:P], vn[0:rows, b, j, i * P:(i + 1) * P],
                                                kn[0:rows, b, j, i * P:(i + 1) * P], start=j == 0, stop=j == 1)
                    last.then_inc(kvT_made, 1)

                pair_product(0)
                pe.wait_ge(k_copied, 4)
                for n in range(BATCH * IC):
                    if n + 1 < BATCH * IC:
                        pair_product(n + 1)
                    pe.wait_ge(kvT_ready, n + 1)
                    at_least(pe, m_taken, n - 1)
                    nc.tensor.matmul(k.PS[:, M_BANKS[n % 2], 0:D], kvT[:, n % 2, :], k.wo1[:, n % IC, :],
                                     start=True, stop=True).then_inc(m_made, 1)

            @block.scalar
            def _(act):
                def square_keys(n):
                    rows = CTX_SPLIT[n % 2][1]
                    act.wait_ge(k_made, n + 1)
                    at_least(act, k_sums, n)
                    nc.scalar.activation(sq[0:rows, :], k.PS[0:rows, BANK_K:BANK_K + 2, :],
                                         ACT.Square).then_inc(sq_made, 1)

                def keep_values(n):
                    b, j = divmod(n, 2)
                    rows = CTX_SPLIT[j][1]
                    act.wait_ge(v_made, n + 1)
                    nc.scalar.activation(vn[0:rows, b, j, :], k.PS[0:rows, BANK_V:BANK_V + 2, :],
                                         ACT.Copy).then_inc(v_taken, 1)

                square_keys(0)
                keep_values(0)
                router_scalar(k, act, turned, hT, hT_ready, scored)
                for n in range(1, 4):
                    square_keys(n)
                    keep_values(n)
                for n in range(BATCH * IC):
                    b, i = divmod(n, IC)
                    act.wait_ge(m_made, n + 1)
                    nc.scalar.activation(k.keyval1[:, b, i, :], k.PS[:, M_BANKS[n % 2], 0:D],
                                         ACT.Copy).then_inc(m_taken, 1)

            @block.gpsimd
            def _(pool):
                def root_keys(n):
                    b, j = divmod(n, 2)
                    rows = CTX_SPLIT[j][1]
                    pool.wait_ge(k_sums, n + 1)
                    nc.gpsimd.tensor_tensor(ss[0:rows, b, j, :], ss[0:rows, b, j, :],
                                            k.half_pos[0:rows, 0:H1], ALU.pow).then_inc(k_roots, 1)

                inverse_roots(k, pool, sums, powers)
                root_keys(0)
                root_keys(1)
                pool.wait_ge(k.zeroed, 16 * SLOT_STORES)
                pool.wait_ge(slots_ready, 1)
                for t in range(TILES):
                    nc.gpsimd.indirect_dma_start(
                        out=k.slots0, out_offset=bass.IndirectOffsetOnAxis(ap=k.slot0[:, t:t + 1], axis=0),
                        in_=k.rows_out[:, t, :], in_offset=None).then_inc(scattered, 16)
                    if t == 3:
                        root_keys(2)
                    if t == 6:
                        root_keys(3)
                pool.wait_ge(scattered, 16 * TILES)

            @block.vector
            def _(dve):
                own = Own(dve, dve_own)

                def sum_keys(n):
                    b, j = divmod(n, 2)
                    rows = CTX_SPLIT[j][1]
                    dve.wait_ge(sq_made, n + 1)
                    nc.vector.tensor_copy(kn[0:rows, b, j, :], k.PS[0:rows, BANK_K:BANK_K + 2, :])\
                        .then_inc(k_copied, 1)
                    nc.vector.tensor_reduce(ss[0:rows, b, j, :],
                                            sq[0:rows, :].rearrange("p (h d) -> p h d", h=H1),
                                            X_AXIS, ALU.add).then_inc(k_sums, 1)

                def unit_keys(n):
                    b, j = divmod(n, 2)
                    rows = CTX_SPLIT[j][1]
                    norms = ss[0:rows, b, j, :]
                    dve.wait_ge(k_roots, n + 1)
                    own.then(nc.vector.tensor_scalar(norms, norms, 1e-12, None, ALU.max))
                    own.then(nc.vector.reciprocal(norms, norms))
                    view = kn[0:rows, b, j, :].rearrange("p (h d) -> p h d", h=H1)
                    dve.wait_ge(k_copied, n + 1)
                    nc.vector.tensor_tensor(view, view, wide(norms, (rows, H1, HD1), 2),
                                            ALU.mult).then_inc(kn_ready, 1)

                nc.vector.tensor_copy(k.rows_out[:, :, D], k.small["token_no"])
                statistics(k, own, sums)
                dve.wait_ge(powers, 1)
                for t in range(TILES):
                    apply_normalisation(k, t).then_inc(xn_ready, 1)
                    if t == 7:
                        sum_keys(0)
                dve.wait_ge(scored, TILES)
                own.then(nc.vector.tensor_tensor(
                    logits[:, :, :], k.PS[:, BANK_R, 0:TILES * E0].rearrange("p (t e) -> p t e", t=TILES),
                    wide(k.small["br0"], (P, TILES, E0), 1), ALU.add))
                first_of_largest(k, own, one_hot[:, :, :], logits[:, :, :], top[:, :], k.small["order0"], E0)
                own.then(nc.vector.memset(upto[:, 0, :], 0.0))
                running_sum(k, own, one_hot, part_sum, upto[:, 1:TILES + 1, :])
                dve.sem_inc(chosen, 1)
                sum_keys(1)
                dve.wait_ge(ranked, 1)
                own.then(nc.vector.tensor_tensor(
                    grid[:, :, :], wide(k.PS[:, BANK_R, COUNTS:COUNTS + E0], (P, E0, N // W), 2),
                    wide(k.small["thresh0"], (P, E0, N // W), 1), ALU.is_gt))
                own.then(nc.vector.tensor_reduce(tiles_of[:, :], grid[:, :, :], X_AXIS, ALU.add))
                own.then(nc.vector.tensor_tensor(square[:, :, :], k.small["before0"],
                                                 wide(tiles_of[:, :], (P, E0, E0), 1), ALU.mult))
                own.then(nc.vector.tensor_reduce(start[:, :], square[:, :, :], X_AXIS, ALU.add))
                nc.vector.tensor_tensor(tiles_of[:, :], tiles_of[:, :], start[:, :], ALU.add)
                own.then(nc.vector.tensor_scalar(start[:, :], start[:, :], float(W), None, ALU.mult))
                own.then(nc.vector.tensor_tensor(
                    place[:, :, :], k.PS[:, BANK_R, RANKS:RANKS + TILES * E0]
                    .rearrange("p (t e) -> p t e", t=TILES),
                    wide(start[:, :], (P, TILES, E0), 1), ALU.add))
                own.then(nc.vector.tensor_tensor(place[:, :, :], place[:, :, :], one_hot[:, :, :], ALU.mult))
                own.then(nc.vector.tensor_reduce(slot[:, :], place[:, :, :], X_AXIS, ALU.add))
                nc.vector.tensor_copy(k.slot0[:, :], slot[:, :]).then_inc(slots_ready, 1)
                own.then(nc.vector.tensor_tensor(
                    over[:, :, :], wide(k.small["tile_no"], (P, SLOT_TILES0, E0), 2),
                    wide(tiles_of[:, :], (P, SLOT_TILES0, E0), 1), ALU.is_ge))
                own.then(nc.vector.tensor_reduce(expert[:, :], over[:, :, :], X_AXIS, ALU.add))
                nc.vector.tensor_scalar(k.expert0[:, :], expert[:, :], float(E0 - 1), None, ALU.min)
                unit_keys(0)
                unit_keys(1)
                sum_keys(2)
                sum_keys(3)
                unit_keys(2)
                for n in range(BATCH * IC):
                    if n == 2:
                        unit_keys(3)
                    dve.wait_ge(kvT_made, n + 1)
                    at_least(dve, m_made, n - 1)
                    nc.vector.tensor_tensor(kvT[:, n % 2, :], k.PS[:, PAIR_BANKS[n % 2], 0:P], k.small["pairmask"],
                                            ALU.mult).then_inc(kvT_ready, 1)


def attention1_stage(k):
    nc = k.nc
    k.stage_begins()
    with ExitStack() as own_memory:
        def sb(name, shape, dt=F32):
            return own_memory.enter_context(nc.sbuf_tensor(name, shape, dt))

        def sem(name):
            return k.stage_semaphore(name)

        wq, w1, w2 = sb("wq", [P, KC, INNER]), sb("w1", [P, KC, F]), sb("w2", [P, FC, D])
        w_in = sem("w_in")
        mean2 = sb("mean2", [P, TILES, 2])
        rstd2 = sb("rstd2", [P, TILES])
        xh = sb("xh", [P, D])
        xhT = sb("xhT", [P, KC, P])
        sq = sb("sq1", [P, INNER])
        ss = sb("ss1", [P, H1])
        rn = sb("rn1", [P, H1])
        qn = sb("qn", [P, INNER])
        qnT = sb("qnT", [P, IC, P])
        qb = sb("qb", [P, 2, D])
        x1 = sb("x1", [P, 1, D])
        st1 = sb("st1", [P, 6])
        mv1 = sb("mv1", [P, 2])
        rs1 = sb("rs1", [P, 1])
        xh1 = sb("xh1", [P, D])
        xh1T = sb("xh1T", [P, KC, P])
        hT = sb("hT1", [P, FC, P])
        QT = TILES // 4
        made_in = [sem(f"made_in{q}") for q in range(4)]
        dve_own, x_whole = sem("dve_own"), sem("x_whole")
        sums, powers, sums2, powers2 = sem("sums"), sem("powers"), sem("sums2"), sem("powers2")
        xh_ready, xh_turned, xhT_ready = sem("xh_ready"), sem("xh_turned"), sem("xhT_ready")
        q_made, squared, q_summed, q_rooted, qn_ready = (sem(n) for n in (
            "q_made", "squared", "q_summed", "q_rooted", "qn_ready"))
        qn_turned, qnT_ready, o_made, x1_ready = (sem(n) for n in (
            "qn_turned", "qnT_ready", "o_made", "x1_ready"))
        x1_summed, x1_rooted, xh1_ready, xh1_turned, xh1T_ready = (sem(n) for n in (
            "x1_summed", "x1_rooted", "xh1_ready", "xh1_turned", "xh1T_ready"))
        upped, bent, downed, x_ready = (sem(n) for n in (
            "upped", "bent", "downed", "x_ready"))
        BANK_Q, BANK_QT, BANK_H, BANK_Y, BANK_T = 0, 2, 4, 6, 7

        with nc.Block() as block:
            @block.sync
            def _(sp):
                for q in range(4):
                    sp.dma_start(k.XN[:, q * TILES // 4:(q + 1) * TILES // 4, :],
                                 k.made0[q * N // 4:(q + 1) * N // 4, :]
                                 .rearrange("(t p) d -> p t d", p=P)).then_inc(made_in[q], 16)
                    if q == 0:
                        sp.dma_start(wq[:, :, :], k.ap["wq1"]).then_inc(w_in, 16)
                sp.dma_start(w1[:, :, :], k.ap["mw1"]).then_inc(w_in, 16)
                sp.dma_start(w2[:, :, :], k.ap["mw2"]).then_inc(w_in, 16)
                for a in range(0, 2 * N, ZM * P):
                    sp.dma_start(k.made1[a:a + ZM * P, :].rearrange("(p m) d -> p m d", m=ZM),
                                 k.zeros[:, :, 0:D]).then_inc(k.zeroed, 16)

            def turns(eng, one):
                one(0, "ba")
                one(1, "bcda")
                one(2, "becfdag")
                with eng.Fori(3, TPB) as s:
                    one(s, "becfdag", 0)
                one(TPB, "becfdag", 0)
                with eng.Fori(TPB + 1, TILES - 1) as s:
                    one(s, "becfdag", 1)
                one(TILES - 1, "becfdg", 1)
                one(TILES, "ecfdg", 1)
                one(TILES + 1, "efg", 1)

            @block.tensor
            def _(pe):
                def a(t):
                    pe.wait_ge(xh_ready, t + 1)
                    if not isinstance(t, int) or t > 2:
                        pe.wait_ge(xh1T_ready, t - 2)
                    for c in range(KC):
                        last = nc.tensor.transpose(k.PS[:, BANK_T, c * P:(c + 1) * P], xh[:, c * P:(c + 1) * P],
                                                   k.ident)
                    last.then_inc(xh_turned, 1)

                def b(t):
                    pe.wait_ge(xhT_ready, t + 1)
                    at_least(pe, qn_ready, t)
                    for q in range(2):
                        for c in range(KC):
                            last = nc.tensor.matmul(k.PS[:, BANK_Q + q, :], xhT[:, c, :],
                                                    wq[:, c, q * 512:(q + 1) * 512],
                                                    start=c == 0, stop=c == KC - 1)
                    last.then_inc(q_made, 1)

                def c(t):
                    pe.wait_ge(qn_ready, t + 1)
                    at_least(pe, qnT_ready, t)
                    for i in range(IC):
                        last = nc.tensor.transpose(k.PS[:, BANK_QT + i // 4, (i % 4) * P:(i % 4 + 1) * P],
                                                   qn[:, i * P:(i + 1) * P], k.ident)
                    last.then_inc(qn_turned, 1)

                def d(t, batch):
                    pe.wait_ge(qnT_ready, t + 1)
                    if not isinstance(t, int) or t > 0:
                        at_least(pe, x_ready, t - 1)
                    for i in range(IC):
                        last = nc.tensor.matmul(k.PS[:, BANK_Y, 0:D], qnT[:, i, :], k.keyval1[:, batch, i, :],
                                                start=i == 0, stop=i == IC - 1)
                    last.then_inc(o_made, 1)

                def e(t):
                    pe.wait_ge(xh1_ready, t + 1)
                    pe.wait_ge(xhT_ready, t + 3 if not isinstance(t, int) or t + 3 < TILES else TILES)
                    for c in range(KC):
                        last = nc.tensor.transpose(k.PS[:, BANK_T, c * P:(c + 1) * P],
                                                   xh1[:, c * P:(c + 1) * P], k.ident)
                    last.then_inc(xh1_turned, 1)

                def f(t):
                    pe.wait_ge(xh1T_ready, t + 1)
                    for q in range(2):
                        at_least(pe, bent, 2 * (t - 1) + q + 1)
                        for f in range(4 * q, 4 * q + 4):
                            for c in range(KC):
                                last = nc.tensor.matmul(k.PS[:, BANK_H + q, (f - 4 * q) * P:(f - 4 * q + 1) * P],
                                                        w1[:, c, f * P:(f + 1) * P], xh1T[:, c, :],
                                                        start=c == 0, stop=c == KC - 1)
                        last.then_inc(upped, 1)

                def g(t, last_x1):
                    pe.wait_ge(bent, 2 * t + 2)
                    pe.wait_ge(x1_ready, last_x1)
                    for f in range(FC):
                        last = nc.tensor.matmul(k.PS[:, BANK_Y, 0:D], hT[:, f, :], w2[:, f, :],
                                                start=f == 0, stop=f == FC - 1)
                    last.then_inc(downed, 1)

                def turn(s, steps, batch=0):
                    for step in steps:
                        if step == "a":
                            a(s + 1)
                        elif step == "b":
                            b(s)
                        elif step == "c":
                            c(s - 1)
                        elif step == "d":
                            d(s - 1, batch)
                        elif step == "e":
                            e(s - 2)
                        elif step == "f":
                            f(s - 2)
                        else:
                            g(s - 2, TILES if isinstance(s, int) and s > TILES else s)

                pe.wait_ge(w_in, 48)
                a(0)
                turns(pe, turn)

            @block.scalar
            def _(act):
                def square(t):
                    act.wait_ge(q_made, t + 1)
                    at_least(act, q_summed, t)
                    nc.scalar.activation(sq[:, :], k.PS[:, BANK_Q:BANK_Q + 2, :], ACT.Square)\
                        .then_inc(squared, 1)

                def keep_q(t):
                    act.wait_ge(qn_turned, t + 1)
                    at_least(act, o_made, t)
                    nc.scalar.activation(qnT[:, :, :], k.PS[:, BANK_QT:BANK_QT + 2, :]
                                         .rearrange("p b (c q) -> p (b c) q", c=4), ACT.Copy)\
                        .then_inc(qnT_ready, 1)

                def bend(t):
                    at_least(act, downed, t)
                    for q in range(2):
                        act.wait_ge(upped, 2 * t + q + 1)
                        for f in range(4 * q, 4 * q + 4):
                            last = nc.scalar.activation(
                                hT[:, f, :], k.PS[:, BANK_H + q, (f - 4 * q) * P:(f - 4 * q + 1) * P],
                                ACT.Gelu, bias=k.small["mb1"][:, f:f + 1])
                        last.then_inc(bent, 1)

                def turn(s, steps, batch=0):
                    if "b" in steps:
                        square(s)
                    if "c" in steps:
                        keep_q(s - 1)
                    if "f" in steps:
                        bend(s - 2)

                turns(act, turn)

            @block.gpsimd
            def _(pool):
                k.clear_spent()

                def prepare(q):
                    part = slice(q * QT, (q + 1) * QT)
                    pool.wait_ge(sums, q + 1)
                    nc.gpsimd.tensor_tensor(k.rstd[:, part], k.rstd[:, part], k.half_neg[:, 0:QT],
                                            ALU.pow).then_inc(powers, 1)
                    pool.wait_ge(sums2, q + 1)
                    nc.gpsimd.tensor_tensor(rstd2[:, part], rstd2[:, part], k.half_neg[:, 0:QT], ALU.pow)\
                        .then_inc(powers2, 1)

                def root_q(t):
                    pool.wait_ge(q_summed, t + 1)
                    at_least(pool, qn_ready, t)
                    nc.gpsimd.tensor_tensor(rn[:, :], ss[:, :], k.half_pos[:, 0:H1], ALU.pow)\
                        .then_inc(q_rooted, 1)

                def root_x1(t):
                    pool.wait_ge(x1_summed, t + 1)
                    nc.gpsimd.tensor_tensor(rs1[:, :], rs1[:, :], k.half_neg[:, 0:1], ALU.pow)\
                        .then_inc(x1_rooted, 1)

                def turn(s, steps, batch=0):
                    if "b" in steps:
                        root_q(s)
                    if "d" in steps:
                        root_x1(s - 1)
                    if isinstance(s, int) and s < 3:
                        prepare(s + 1)

                prepare(0)
                turns(pool, turn)

            @block.vector
            def _(dve):
                own = Own(dve, dve_own)

                def prepare(q):
                    tiles = range(q * QT, (q + 1) * QT)
                    part = slice(q * QT, (q + 1) * QT)
                    dve.wait_ge(made_in[q], 16)
                    for t in tiles:
                        last = nc.vector.tensor_tensor(k.X[:, t, :], k.X[:, t, :], k.XN[:, t, :], ALU.add)
                    own.then(last)
                    for t in tiles:
                        last = nc.vector.bn_stats(k.stats[:, t, :], k.X[:, t, :])
                    own.then(last)
                    for t in tiles:
                        last = nc.vector.bn_aggr(k.mv[:, t, :], k.stats[:, t, :])
                    own.then(last)
                    nc.vector.tensor_scalar(k.rstd[:, part], k.mv[:, part, 1], EPS, None, ALU.add)\
                        .then_inc(sums, 1)
                    dve.wait_ge(powers, q + 1)
                    for t in tiles:
                        last = apply_normalisation(k, t)
                    own.then(last)
                    for t in tiles:
                        last = nc.vector.bn_stats(k.stats[:, t, :], k.XN[:, t, :])
                    own.then(last)
                    for t in tiles:
                        last = nc.vector.bn_aggr(mean2[:, t, :], k.stats[:, t, :])
                    own.then(last)
                    nc.vector.tensor_scalar(rstd2[:, part], mean2[:, part, 1], EPS, None, ALU.add)\
                        .then_inc(sums2, 1)

                def normalise_again(t):
                    at_least(dve, xh_turned, t)
                    nc.vector.tensor_scalar(xh[:, :], k.XN[:, t, :], mean2[:, t, 0:1], rstd2[:, bass.ds(t, 1)],
                                            ALU.subtract, ALU.mult).then_inc(xh_ready, 1)

                def keep_xh(t):
                    dve.wait_ge(xh_turned, t + 1)
                    at_least(dve, q_made, t)
                    for c in range(KC):
                        last = nc.vector.tensor_scalar(xhT[:, c, :], k.PS[:, BANK_T, c * P:(c + 1) * P],
                                                       k.small["g1"][:, c:c + 1], k.small["be1"][:, c:c + 1],
                                                       ALU.mult, ALU.add)
                    last.then_inc(xhT_ready, 1)

                def sum_q(t):
                    dve.wait_ge(squared, t + 1)
                    at_least(dve, q_rooted, t)
                    nc.vector.tensor_reduce(ss[:, :], sq[:, :].rearrange("p (h d) -> p h d", h=H1),
                                            X_AXIS, ALU.add).then_inc(q_summed, 1)

                def unit_q(t):
                    dve.wait_ge(q_rooted, t + 1)
                    own.then(nc.vector.tensor_scalar(rn[:, :], rn[:, :], 1e-12, None, ALU.max))
                    own.then(nc.vector.reciprocal(rn[:, :], rn[:, :]))
                    at_least(dve, qn_turned, t)
                    nc.vector.tensor_tensor(
                        qn[:, :].rearrange("p (h d) -> p h d", h=H1),
                        k.PS[:, BANK_Q:BANK_Q + 2, :].rearrange("p b (h d) -> p (b h) d", d=HD1),
                        wide(rn[:, :], (P, H1, HD1), 2), ALU.mult).then_inc(qn_ready, 1)

                def residual(t):
                    own.then(nc.vector.tensor_tensor(qb[:, 0, :], k.XN[:, t, :], k.small["bo1"][:, :], ALU.add))
                    dve.wait_ge(o_made, t + 1)
                    nc.vector.tensor_tensor(x1[:, 0, :], k.PS[:, BANK_Y, 0:D], qb[:, 0, :], ALU.add)\
                        .then_inc(x1_ready, 1)
                    dve.wait_ge(x1_ready, t + 1)
                    own.then(nc.vector.bn_stats(st1[:, :], x1[:, 0, :]))
                    nc.vector.tensor_tensor(qb[:, 1, :], k.X[:, t, :], k.small["mb2"][:, :], ALU.add)
                    own.then(nc.vector.bn_aggr(mv1[:, :], st1[:, :]))
                    nc.vector.tensor_scalar(rs1[:, :], mv1[:, 1:2], EPS, None, ALU.add).then_inc(x1_summed, 1)
                    own.then(nc.vector.tensor_tensor(k.X[:, t, :], qb[:, 1, :], x1[:, 0, :], ALU.add))

                def normalise_x1(t):
                    dve.wait_ge(x1_rooted, t + 1)
                    at_least(dve, xh1_turned, t)
                    nc.vector.tensor_scalar(xh1[:, :], x1[:, 0, :], mv1[:, 0:1], rs1[:, 0:1],
                                            ALU.subtract, ALU.mult).then_inc(xh1_ready, 1)

                def keep_xh1(t):
                    dve.wait_ge(xh1_turned, t + 1)
                    at_least(dve, upped, 2 * t)
                    for c in range(KC):
                        last = nc.vector.tensor_scalar(xh1T[:, c, :], k.PS[:, BANK_T, c * P:(c + 1) * P],
                                                       k.small["g2"][:, c:c + 1], k.small["be2"][:, c:c + 1],
                                                       ALU.mult, ALU.add)
                    last.then_inc(xh1T_ready, 1)

                def finish(t):
                    dve.wait_ge(downed, t + 1)
                    nc.vector.tensor_tensor(k.X[:, t, :], k.PS[:, BANK_Y, 0:D], k.X[:, t, :], ALU.add)\
                        .then_inc(x_ready, 1)
                    dve.wait_ge(x_ready, t + 1)
                    nc.vector.bn_stats(k.stats[:, t, :], k.X[:, t, :])

                def turn(s, steps, batch=0):
                    if "e" in steps:
                        keep_xh1(s - 2)
                    if "b" in steps:
                        sum_q(s)
                    if "a" in steps:
                        normalise_again(s + 1)
                    if "d" in steps:
                        residual(s - 1)
                    if "b" in steps:
                        unit_q(s)
                    if "a" in steps:
                        keep_xh(s + 1)
                    if "d" in steps:
                        normalise_x1(s - 1)
                    if "g" in steps:
                        finish(s - 2)

                def counted(s, steps, batch=0):
                    if isinstance(s, int):
                        turn(s, steps, batch)
                        if s < 3:
                            prepare(s + 1)
                            dve.wait_ge(powers2, s + 2)
                    else:
                        first, turns_ = (3, TPB - 3) if batch == 0 else (TPB + 1, TPB - 2)
                        own.enter(s, first, 6)
                        turn(s, steps, batch)
                        own.leave(turns_)

                prepare(0)
                dve.wait_ge(powers2, 1)
                normalise_again(0)
                keep_xh(0)
                turns(dve, counted)


def route1_stage(k):
    nc = k.nc
    with ExitStack() as own_memory:
        def sb(name, shape, dt=F32):
            return own_memory.enter_context(nc.sbuf_tensor(name, shape, dt))

        def sem(name):
            return k.stage_semaphore(name)

        hT = sb("hT2", [P, 3, KC, P])
        wide3 = [P, TILES, E1]
        logits, probs, first, second, both = (sb(n, wide3) for n in ("logits1", "probs1", "first", "second", "both"))
        rank, work = (sb(n, wide3) for n in ("rank1", "work1"))
        earlier = sb("earlier1", [P, TILES + 1, E1])
        top, total, kept, gate_sum = (sb(n, [P, TILES]) for n in ("top1", "total1", "kept1", "gate_sum"))
        gate = sb("gate", [P, 2, TILES])
        where = sb("where", [P, 2, TILES])
        drop = sb("drop", [P, 2, TILES])
        junk = sb("junk", [P, D])
        square = sb("square_sum", [P, TILES])
        dve_own, sums, powers, sums2, powers2 = (sem(n) for n in ("dve_own", "sums", "powers", "sums2", "powers2"))
        xn_ready, turned, hT_ready, scored = sem("xn_ready"), sem("turned"), sem("hT_ready"), sem("scored")
        ln_ready, squared, raising, raised = sem("ln_ready"), sem("squared"), sem("raising"), sem("raised")
        chosen, ranked, rows_known, scattered = sem("chosen"), sem("ranked"), sem("rows_known"), sem("scattered")
        act_own, numbers_set = sem("act_own"), sem("numbers_set")
        with nc.Block() as block:
            @block.tensor
            def _(pe):
                router_tensor(k, pe, E1, k.small["wr1"], xn_ready, turned, hT, hT_ready, scored)
                pe.wait_ge(chosen, 1)
                nc.tensor.matmul(k.PS[:, 3, 0:TILES * E1], k.small["tri"][:, :], both[:, :, :],
                                 start=True, stop=False)
                nc.tensor.matmul(k.PS[:, 3, 0:TILES * E1], k.small["ones"][:, :], earlier[:, 0:TILES, :],
                                 start=False, stop=True).then_inc(ranked, 1)

            @block.scalar
            def _(act):
                own = Own(act, act_own)
                for t in range(TILES):
                    act.wait_ge(ln_ready, t + 1)
                    own.then(nc.scalar.activation(junk[:, :], k.XN[:, t, :], ACT.Square,
                                                  accum_out=square[:, t:t + 1]))
                act.sem_inc(squared, 1)
                router_scalar(k, act, turned, hT, hT_ready, scored)
                act.wait_ge(raising, 1)
                nc.scalar.activation(probs[:, :, :], probs[:, :, :], ACT.Exp).then_inc(raised, 1)

            @block.gpsimd
            def _(pool):
                inverse_roots(k, pool, sums, powers)
                pool.wait_ge(sums2, 1)
                nc.gpsimd.tensor_tensor(square[:, :], square[:, :], k.half_neg[:, 0:TILES], ALU.pow)\
                    .then_inc(powers2, 1)
                pool.wait_ge(k.zeroed, 16 * (SLOT_STORES + 2 * N // (ZM * P)))
                for n in range(2):
                    pool.wait_ge(rows_known, n + 1)
                    if n:
                        pool.wait_ge(scattered, 16 * TILES)
                        nc.gpsimd.tensor_scalar(k.rows_out[:, :, D], k.rows_out[:, :, D], float(N), None, ALU.add)\
                            .then_inc(numbers_set, 1)
                        pool.wait_ge(numbers_set, 1)
                    for t in range(TILES):
                        nc.gpsimd.indirect_dma_start(
                            out=k.slots1, out_offset=bass.IndirectOffsetOnAxis(ap=k.slot1[:, n, t:t + 1], axis=0),
                            in_=k.rows_out[:, t, :], in_offset=None, bounds_check=ROWS1 - 1,
                            oob_is_err=False).then_inc(scattered, 16)
                pool.wait_ge(scattered, 16 * 2 * TILES)

            @block.vector
            def _(dve):
                own = Own(dve, dve_own)
                normalise_vector(k, dve, own, sums, powers, ln_ready, True)
                dve.wait_ge(ln_ready, TILES)
                dve.wait_ge(squared, 1)
                nc.vector.tensor_scalar(square[:, :], square[:, :], 1.0 / D, EPS, ALU.mult, ALU.add)\
                    .then_inc(sums2, 1)
                dve.wait_ge(powers2, 1)
                for t in range(TILES):
                    nc.vector.scalar_tensor_tensor(k.XN[:, t, :], k.XN[:, t, :], square[:, t:t + 1],
                                                   k.small["nw"][:, :], ALU.mult, ALU.mult).then_inc(xn_ready, 1)
                dve.wait_ge(scored, TILES)
                own.then(nc.vector.tensor_tensor(
                    logits[:, :, :], k.PS[:, 2, 0:TILES * E1].rearrange("p (t e) -> p t e", t=TILES),
                    wide(k.small["br1"][:, :], wide3, 1), ALU.add))
                own.then(nc.vector.tensor_reduce(top[:, :], logits[:, :, :], X_AXIS, ALU.max))
                nc.vector.tensor_tensor(probs[:, :, :], logits[:, :, :], wide(top[:, :], wide3, 2),
                                        ALU.subtract).then_inc(raising, 1)
                dve.wait_ge(raising, 1)
                order = k.small["order1"][:, :]
                first_of_largest(k, own, first[:, :, :], logits[:, :, :], top[:, :], order, E1)
                own.then(nc.vector.tensor_scalar(work[:, :, :], first[:, :, :], -3e38, None, ALU.mult))
                own.then(nc.vector.tensor_tensor(logits[:, :, :], logits[:, :, :], work[:, :, :], ALU.add))
                first_of_largest(k, own, second[:, :, :], logits[:, :, :], top[:, :], order, E1)
                own.then(nc.vector.tensor_tensor(both[:, :, :], first[:, :, :], second[:, :, :], ALU.add))
                own.then(nc.vector.memset(earlier[:, 0, :], 0.0))
                running_sum(k, own, both, work, earlier[:, 1:TILES + 1, :])
                dve.sem_inc(chosen, 1)
                dve.wait_ge(raised, 1)
                own.then(nc.vector.tensor_reduce(total[:, :], probs[:, :, :], X_AXIS, ALU.add))
                own.then(nc.vector.reciprocal(total[:, :], total[:, :]))
                own.then(nc.vector.tensor_tensor(probs[:, :, :], probs[:, :, :], wide(total[:, :], wide3, 2),
                                                 ALU.mult))
                for n, one_hot in enumerate((first, second)):
                    own.then(nc.vector.tensor_tensor(work[:, :, :], probs[:, :, :], one_hot[:, :, :], ALU.mult))
                    own.then(nc.vector.tensor_reduce(gate[:, n, :], work[:, :, :], X_AXIS, ALU.add))
                dve.wait_ge(ranked, 1)
                own.then(nc.vector.tensor_copy(rank[:, :, :], k.PS[:, 3, 0:TILES * E1]
                                               .rearrange("p (t e) -> p t e", t=TILES)))
                for n, one_hot in enumerate((first, second)):
                    own.then(nc.vector.tensor_tensor(work[:, :, :], rank[:, :, :], one_hot[:, :, :], ALU.mult))
                    own.then(nc.vector.tensor_reduce(where[:, n, :], work[:, :, :], X_AXIS, ALU.add))
                    own.then(nc.vector.tensor_scalar(drop[:, n, :], where[:, n, :], float(CAP), None, ALU.is_ge))
                    own.then(nc.vector.tensor_tensor(
                        work[:, :, :], one_hot[:, :, :], wide(k.small["base1"][:, :], wide3, 1), ALU.mult))
                    own.then(nc.vector.tensor_reduce(top[:, :], work[:, :, :], X_AXIS, ALU.add))
                    own.then(nc.vector.tensor_tensor(where[:, n, :], where[:, n, :], top[:, :], ALU.add))
                    own.then(nc.vector.scalar_tensor_tensor(where[:, n, :], drop[:, n, :], float(SKIP),
                                                            where[:, n, :], ALU.mult, ALU.add))
                    nc.vector.tensor_copy(k.slot1[:, n, :], where[:, n, :]).then_inc(rows_known, 1)
                own.then(nc.vector.tensor_scalar(drop[:, :, :], drop[:, :, :], -1.0, 1.0, ALU.mult, ALU.add))
                own.then(nc.vector.tensor_tensor(gate[:, :, :], gate[:, :, :], drop[:, :, :], ALU.mult))
                own.then(nc.vector.tensor_tensor(gate_sum[:, :], gate[:, 0, :], gate[:, 1, :], ALU.add))
                own.then(nc.vector.tensor_scalar(kept[:, :], gate_sum[:, :], 0.0, None, ALU.is_le))
                own.then(nc.vector.tensor_tensor(gate_sum[:, :], gate_sum[:, :], kept[:, :], ALU.add))
                own.then(nc.vector.reciprocal(gate_sum[:, :], gate_sum[:, :]))
                own.then(nc.vector.tensor_tensor(
                    gate[:, :, :], gate[:, :, :],
                    gate_sum[:, :].rearrange("p (a t) -> p a t", a=1).to_broadcast((P, 2, TILES)), ALU.mult))
                own.then(nc.vector.tensor_tensor(first[:, :, :], first[:, :, :], wide(gate[:, 0, :], wide3, 2),
                                                 ALU.mult))
                own.then(nc.vector.tensor_tensor(second[:, :, :], second[:, :, :], wide(gate[:, 1, :], wide3, 2),
                                                 ALU.mult))
                own.then(nc.vector.tensor_tensor(k.plain[:, :, :], first[:, :, 0:PLAIN], second[:, :, 0:PLAIN],
                                                 ALU.add))
                nc.vector.tensor_copy(k.gate1[:, :, :], gate[:, :, :])
                for t in range(TILES):
                    own.then(nc.vector.scalar_tensor_tensor(k.X[:, t, :], k.XN[:, t, :], k.plain[:, t, 1:2],
                                                            k.X[:, t, :], ALU.mult, ALU.add))
                    for c in range(2):
                        own.then(nc.vector.scalar_tensor_tensor(
                            k.X[:, t, :], k.small["cv"][:, c, :], k.plain[:, t, 2 + c:3 + c], k.X[:, t, :],
                            ALU.mult, ALU.add))


def combine_stage(k):
    nc = k.nc
    with ExitStack() as own_memory:
        def sem(name):
            return k.stage_semaphore(name)

        Y = own_memory.enter_context(nc.sbuf_tensor("Y", [P, 2, TILES, D], F32))
        PART = TILES // 4
        made_in = [sem(f"made_in{q}") for q in range(4)]
        own_sem, x_ready, stored = sem("dve_own"), sem("x_ready"), sem("stored")
        with nc.Block() as block:
            @block.scalar
            def _(act):
                for q in range(4):
                    for n in range(2):
                        act.dma_start(Y[:, n, q * PART:(q + 1) * PART, :],
                                      k.made1[n * N + q * PART * P:n * N + (q + 1) * PART * P, :]
                                      .rearrange("(t p) d -> p t d", p=P)).then_inc(made_in[q], 16)

            @block.vector
            def _(dve):
                own = Own(dve, own_sem)
                for t in range(TILES):
                    dve.wait_ge(made_in[t // PART], 16 * 2)
                    own.then(nc.vector.scalar_tensor_tensor(k.X[:, t, :], Y[:, 0, t, :], k.gate1[:, 0, t:t + 1],
                                                            k.X[:, t, :], ALU.mult, ALU.add))
                    nc.vector.scalar_tensor_tensor(k.X[:, t, :], Y[:, 1, t, :], k.gate1[:, 1, t:t + 1],
                                                   k.X[:, t, :], ALU.mult, ALU.add).then_inc(x_ready, 1)

            @block.sync
            def _(sp):
                for t in range(0, TILES, 2):
                    sp.wait_ge(x_ready, t + 2)
                    sp.dma_start(k.out[t * P:(t + 2) * P, :].rearrange("(t p) d -> p t d", p=P),
                                 k.X[:, t:t + 2, :]).then_inc(stored, 16)
                sp.wait_ge(stored, 16 * TILES // 2)


def build(nc, ap, out, until=9):
    with ExitStack() as ctx:
        def sb(name, shape, dt=F32):
            return ctx.enter_context(nc.sbuf_tensor(name, shape, dt))

        def sem(name):
            return ctx.enter_context(nc.semaphore(name))

        k = Core()
        k.nc, k.ap, k.out = nc, ap, out
        k.slots0 = nc.dram_tensor("slots0", [ROWS0, D + 1], F32, kind="Internal").ap()
        k.made0 = nc.dram_tensor("made0", [N, D], F32, kind="Internal").ap()
        k.slots1 = nc.dram_tensor("slots1", [ROWS1, D + 1], F32, kind="Internal").ap()
        k.heads0 = nc.dram_tensor("heads0", [BATCH, H0, CTX, HD0], F32, kind="Internal").ap()
        k.made1 = nc.dram_tensor("made1", [2 * N, D], F32, kind="Internal").ap()
        k.X = sb("X", [P, TILES, D])
        k.rows_out = sb("rows_out", [P, TILES, D + 1])
        k.XN = k.rows_out[:, :, 0:D]
        k.zeros = sb("zeros", [P, ZM, D + 1])
        k.zeroed = sem("zeroed")
        k.stats = sb("stats", [P, TILES, 6])
        k.mv = sb("mv", [P, TILES, 2])
        k.rstd = sb("rstd", [P, TILES])
        k.half_neg = sb("half_neg", [P, H1 * 4])
        k.half_pos = sb("half_pos", [P, H1 * 4])
        k.keyval1 = sb("keyval1", [P, BATCH, IC, D])
        k.plain_pack = sb("plain_pack", [P, PLAIN_WIDTH])
        k.spread_pack = sb("spread_pack", [P, SPREAD_WIDTH])
        k.small, at = {}, {True: 0, False: 0}
        for name, shape in SMALL:
            spread, width = name in BROADCAST, math.prod(shape[1:])
            part = (k.spread_pack if spread else k.plain_pack)[:, at[spread]:at[spread] + width]
            at[spread] += width
            k.small[name] = part if len(shape) == 2 else part.rearrange("p (a b) -> p a b", a=shape[1])
        k.ident = k.small["ident"]
        k.PS = ctx.enter_context(nc.psum_tensor("PS", [P, 8, 512], F32))
        k.slot0 = sb("slot0", [P, TILES], U32)
        k.expert0 = sb("expert0", [P, SLOT_TILES0], I32)
        with ExitStack() as keyval:
            def sb_kv(name, shape):
                return keyval.enter_context(nc.sbuf_tensor(name, shape, F32))
            k.cnT = sb_kv("cnT", [P, KC, BATCH, CTX])
            k.wk1, k.wv1 = sb_kv("wk1", [P, KC, INNER]), sb_kv("wv1", [P, KC, INNER])
            k.wo1 = sb_kv("wo1", [P, IC, D])
            k.kv_w_in = keyval.enter_context(nc.semaphore("kv_w_in"))
            with ExitStack() as first:
                def sb1(name, shape):
                    return first.enter_context(nc.sbuf_tensor(name, shape, F32))
                k.keys0 = sb1("keys0", [P, BATCH, HALVES, HALF_HEADS, CTX])
                k.values0 = sb1("values0", [P, BATCH, HALVES, CHUNKS, 2, VW])
                k.probs = sb1("probs", [P, HALVES, PADDED])
                k.wq0 = sb1("wq0", [P, KC, D])
                k.wo0 = sb1("wo0", [P, KC, D])
                k.w0_in = sem("attention0_w_in")
                context_stage(k)
                attention0_stage(k)
            if until >= 2:
                route0_stage(k)
        if until >= 2:
            experts_stage(k, "e0", SLOT_TILES0, k.slots0, k.made0,
                          lambda eng, tile: eng.value_load(k.expert0[0:1, bass.ds(tile, 1)],
                                                           min_val=0, max_val=E0 - 1))
            attention1_stage(k)
        if until >= 4:
            k.slot1 = sb("slot1", [P, 2, TILES], U32)
            k.gate1 = sb("gate1", [P, 2, TILES])
            k.plain = sb("plain", [P, TILES, PLAIN])
            route1_stage(k)
            experts_stage(k, "e1", MLPS, k.slots1, k.made1, lambda eng, tile: tile)
            combine_stage(k)
        if until < 9:
            done = sem("done_")
            with nc.Block() as block:
                @block.sync
                def _(sp):
                    sp.dma_start(out.rearrange("(t p) d -> p t d", p=P), k.X[:, :, :]).then_inc(done, 16)
                    sp.wait_ge(done, 16)


def kernel(**inputs):
    import numpy as np
    import concourse.bacc as bacc
    from concourse.bass_utils import run_bass_kernel_spmd

    laid = lay_out(inputs)
    nc = bacc.Bacc("TRN2", target_bir_lowering=False, num_devices=1)
    ap, arrays = {}, {}
    for name, a in laid.items():
        arrays[f"in_{name}"] = a
        ap[name] = nc.dram_tensor(f"in_{name}", a.shape, mybir.dt.from_np(a.dtype), kind="ExternalInput").ap()
    out = nc.dram_tensor("out_0", [N, D], F32, kind="ExternalOutput").ap()
    build(nc, ap, out)
    r = run_bass_kernel_spmd(nc, [arrays], core_ids=[0])
    return r.results[0]["out_0"].reshape(BATCH, SEQ, D)


def lay_out(inputs):
    import numpy as np
    g = {n: np.asarray(a) for n, a in inputs.items()}

    def rows(w):
        return np.ascontiguousarray(w.reshape(w.shape[0] // P, P, *w.shape[1:]).swapaxes(0, 1))

    def f32(a):
        return np.ascontiguousarray(a, dtype=np.float32)

    ctx = g["ctx_1024"]
    ctxT = ctx.transpose(2, 0, 1)
    pad = np.zeros((BATCH, 2 * P, D), ctx.dtype)
    pad[:, :CTX] = ctx
    row = np.arange(PADDED).reshape(CHUNKS, P).T
    head = np.where(row < ROWS, row // CTX, -1)
    part = np.arange(P)
    e8, e16 = np.arange(E0), np.arange(E1)
    laid = {
        "x": g["x"].reshape(N, D),
        "ctx": pad.reshape(BATCH, 2, P, D).transpose(2, 0, 1, 3),
        "ctxT": rows(ctxT),
        "wq0": rows(g["L0_xattn_Wq"]), "wk0": rows(g["L0_xattn_Wk"]), "wo0": rows(g["L0_xattn_Wo"]),
        "wv0": rows(g["L0_xattn_Wv"]),
        "bq0": g["L0_xattn_bq"].reshape(KC, P).T, "bk0": g["L0_xattn_bk"].reshape(KC, P).T,
        "bv0": g["L0_xattn_bv"].reshape(1, D), "bo0": g["L0_xattn_bo"].reshape(1, D),
        "vmask": f32(head[:, :, None] == np.array(PAIR0)[None, :, None] + np.arange(2)),
        "headmask": f32(part[:, None] // HD0 == np.arange(HALF_HEADS)),
        "pairmask": f32(part[:, None] // HD1 == part[None, :] // HD1),
        "wk1": rows(g["L1_xattn_wk"]), "wv1": rows(g["L1_xattn_wv"]), "wq1": rows(g["L1_xattn_wq"]),
        "wo1": rows(g["L1_xattn_wo"]),
        "g1": g["L1_xattn_ln1_g"].reshape(KC, P).T, "be1": g["L1_xattn_ln1_b"].reshape(KC, P).T,
        "g2": g["L1_xattn_ln2_g"].reshape(KC, P).T, "be2": g["L1_xattn_ln2_b"].reshape(KC, P).T,
        "bo1": g["L1_xattn_bo"].reshape(1, D), "mb2": g["L1_xattn_b2"].reshape(1, D),
        "mb1": g["L1_xattn_b1"].reshape(FC, P).T,
        "mw1": rows(g["L1_xattn_w1"]), "mw2": rows(g["L1_xattn_w2"]),
        "wr0": rows(g["L0_ffn_wr"]), "br0": g["L0_ffn_br"].reshape(1, E0),
        "wr1": rows(g["L1_ffn_router_weight"].T), "br1": g["L1_ffn_router_bias"].reshape(1, E1),
        "nw": g["L1_ffn_norm_weight"].reshape(1, D), "cv": g["L1_ffn_constant_vectors"].reshape(1, 2 * D),
        "e0w1": g["L0_ffn_w1"].reshape(E0, KC, P, F).transpose(0, 2, 1, 3),
        "e0w2": g["L0_ffn_w2"].reshape(E0, FC, P, D).transpose(0, 2, 1, 3),
        "e0b1": g["L0_ffn_b1"].reshape(E0, FC, P).transpose(0, 2, 1), "e0b2": g["L0_ffn_b2"],
        "e1w1": g["L1_ffn_fc1_weight"].transpose(0, 2, 1).reshape(MLPS, KC, P, F).transpose(0, 2, 1, 3),
        "e1w2": g["L1_ffn_fc2_weight"].transpose(0, 2, 1).reshape(MLPS, FC, P, D).transpose(0, 2, 1, 3),
        "e1b1": g["L1_ffn_fc1_bias"].reshape(MLPS, FC, P).transpose(0, 2, 1), "e1b2": g["L1_ffn_fc2_bias"],
        "tri": f32(part[:, None] < part[None, :]), "ones": np.ones((P, P), np.float32),
        "ident": np.eye(P, dtype=np.float32),
        "token_no": f32(part[:, None] + P * np.arange(TILES)),
        "order0": f32(E0 - e8)[None], "order1": f32(E1 - e16)[None],
        "thresh0": f32(W * np.arange(N // W))[None],
        "before0": f32(e8[None, :] < e8[:, None]).reshape(1, -1),
        "tile_no": f32(np.arange(SLOT_TILES0))[None],
        "base1": f32(np.where(e16 < PLAIN, SKIP, (e16 - PLAIN) * CAP))[None],
    }
    small = {name: laid.pop(name) for name, _ in SMALL}
    laid["plain_pack"] = np.concatenate([a.reshape(P, -1) for n, a in small.items() if n not in BROADCAST], 1)
    laid["spread_pack"] = np.concatenate([a.reshape(1, -1) for n, a in small.items() if n in BROADCAST], 1)
    return {name: np.ascontiguousarray(a) for name, a in laid.items()}
```

```python
import math
from contextlib import ExitStack

import concourse.bass as bass
from concourse import mybir

F32 = mybir.dt.float32
I32 = mybir.dt.int32
U32 = mybir.dt.uint32
F32R = mybir.dt.float32r
PARTS = ("high", "low")
ACT = mybir.ActivationFunctionType
ALU = mybir.AluOpType
X_AXIS = mybir.AxisListType.X

P = 128
D = 256
KC = D // P
BATCH, SEQ, CTX = 2, 1024, 154
N = BATCH * SEQ
TILES = N // P
TPB = SEQ // P
CTX_SPLIT = ((0, P), (P, CTX - P))
EPS = 1e-5

H0, HD0 = 16, 16
HALF_HEADS = P // HD0
HALVES = H0 // HALF_HEADS
GROUP = 4
GROUPS = H0 // GROUP
GW = GROUP * CTX
ROWS = HALF_HEADS * CTX
CHUNKS = -(-ROWS // P)
PADDED = CHUNKS * P
FILLS = ((0, 4), (4, 4), (8, CHUNKS - 8))
NF = len(FILLS)
VW = HD0 + 1
PAIR0 = [min(P * c // CTX, HALF_HEADS - 2) for c in range(CHUNKS)]

E0, F = 8, 1024
FC = F // P
BLOCKS = 2
W = BLOCKS * P
SLOT_TILES0 = N // W + E0 - 1
ROWS0 = SLOT_TILES0 * W

H1, HD1 = 16, 64
INNER = H1 * HD1
IC = INNER // P

E1, PLAIN = 16, 4
MLPS = E1 - PLAIN
CAP = N * 2 // E1
ROWS1 = MLPS * CAP
ZM = 4
SLOT_STORES = -(-ROWS0 // (ZM * P)) + -(-ROWS1 // (ZM * P))
SKIP = 1 << 20

ROUTER_BANKS = (0, 1, 7)

SMALL = (
    ("bq0", (P, KC)), ("bk0", (P, KC)), ("bv0", (P, D)),
    ("bo0", (P, D)), ("vmask", (P, CHUNKS, 2)), ("headmask", (P, HALF_HEADS)),
    ("pairmask", (P, P)), ("g1", (P, KC)), ("be1", (P, KC)), ("g2", (P, KC)),
    ("be2", (P, KC)), ("bo1", (P, D)), ("mb1", (P, FC)), ("mb2", (P, D)),
    ("wr0", (P, KC, E0)), ("br0", (P, E0)), ("wr1", (P, KC, E1)), ("br1", (P, E1)),
    ("nw", (P, D)), ("cv", (P, 2, D)), ("tri", (P, P)), ("ones", (P, P)), ("ident", (P, P)),
    ("token_no", (P, TILES)), ("order0", (P, E0)), ("order1", (P, E1)), ("thresh0", (P, N // W)),
    ("before0", (P, E0, E0)), ("tile_no", (P, SLOT_TILES0)), ("base1", (P, E1)),
)
BROADCAST = {"bo0", "bo1", "mb2", "br0", "br1", "nw", "cv", "bv0", "order0", "order1", "thresh0",
             "before0", "tile_no", "base1"}

PLAIN_WIDTH = sum(math.prod(s[1:]) for n, s in SMALL if n not in BROADCAST)
SPREAD_WIDTH = sum(math.prod(s[1:]) for n, s in SMALL if n in BROADCAST)


class Own:

    def __init__(self, eng, sem):
        self.eng, self.sem, self.done, self.ahead = eng, sem, 0, 0

    def then(self, ins):
        ins.then_inc(self.sem, 1)
        self.done += 1
        self.eng.wait_ge(self.sem, self.ahead + self.done)

    def enter(self, i, first, per):
        self.base, self.per = self.done, per
        self.ahead = (i - first) * per

    def leave(self, turns):
        assert self.done - self.base == self.per, (self.done - self.base, self.per)
        self.done = self.base + turns * self.per
        self.ahead = 0


class Core:

    def __init__(self):
        self.count = 0
        self.in_use = []

    def stage_semaphore(self, name):
        self.count += 1
        sem = self.nc.alloc_semaphore(name=f"{name}_{self.count}")
        self.in_use.append(sem)
        return sem

    def stage_begins(self):
        self.spent, self.in_use = self.in_use, []

    def clear_spent(self):
        self.nc.clear_and_free_semaphores(self.spent)


def at_least(eng, sem, value):
    if not isinstance(value, int) or value > 0:
        eng.wait_ge(sem, value)


def wide(ap2, shape, axis):
    return ap2.rearrange("p (e a) -> p e a" if axis == 2 else "p (a e) -> p a e", a=1).to_broadcast(shape)


def product(nc, out, left, right, first, last):
    for n, (a, b) in enumerate(((0, 0), (0, 1), (1, 0))):
        ins = nc.tensor.matmul(out, left(a), right(b), start=first and n == 0, stop=last and n == 2)
    return ins


def statistics(k, own, sums):
    nc = k.nc
    for t in range(TILES):
        last = nc.vector.bn_aggr(k.mv[:, t, :], k.stats[:, t, :])
    own.then(last)
    nc.vector.tensor_scalar(k.rstd[:, :], k.mv[:, :, 1], EPS, None, ALU.add).then_inc(sums, 1)


def apply_normalisation(k, t):
    return k.nc.vector.tensor_scalar(k.XN[:, t, :], k.X[:, t, :], k.mv[:, t, 0:1],
                                     k.rstd[:, t:t + 1], ALU.subtract, ALU.mult)


def inverse_roots(k, pool, sums, powers):
    pool.wait_ge(sums, 1)
    k.nc.gpsimd.tensor_tensor(k.rstd[:, :], k.rstd[:, :], k.half_neg[:, 0:TILES],
                              ALU.pow).then_inc(powers, 1)


def spread_keys(k, eng, b, h, part):
    shape = (P, HALF_HEADS, CTX)
    return eng.tensor_tensor(k.keys0[part][:, b, h, :, :], wide(k.kT_parts[part][:, b, h, :].bitcast(F32), shape, 1),
                             wide(k.small["headmask"], shape, 2), ALU.mult)


def context_stage(k):
    nc = k.nc
    with ExitStack() as own_memory:
        def sb(name, shape, dt=F32):
            return own_memory.enter_context(nc.sbuf_tensor(name, shape, dt))

        def sem(name):
            return k.stage_semaphore(name)

        ctxT = sb("ctxT", [P, KC, BATCH, CTX])
        C = sb("C", [P, BATCH, 2, D])
        wk0, wv0 = sb("wk0", [P, KC, D]), sb("wv0", [P, KC, D])
        kT = sb("kT", [P, BATCH, HALVES, CTX])
        kT_parts = k.kT_parts
        v0 = sb("v0", [P, BATCH, 2, D])
        v0_rows = sb("v0_rows", [P, BATCH, HALVES, CHUNKS, HD0])
        cst = sb("cst", [P, BATCH, 2, 6])
        cmv = sb("cmv", [P, BATCH, 2, 2])
        crs = sb("crs", [P, BATCH, 2])

        c_in, w0_in = sem("c_in"), sem("w0_in")
        x_in = [sem(f"x_in{q}") for q in range(4)]
        plain_in, spread_in = sem("plain_in"), sem("spread_in")
        dve_own = sem("dve_own")
        cleared, consts_set = sem("cleared"), sem("consts_set")
        k0_made, v0_made, ctx_sums, ctx_roots = sem("k0_made"), sem("v0_made"), sem("ctx_sums"), sem("ctx_roots")
        v0_ready, v0_stored, v0_rows_in = (sem(n) for n in (
            "v0_ready", "v0_stored", "v0_rows_in"))
        c_ready, cT_made = sem("c_ready"), sem("cT_made")
        x_sums, x_roots, x_kept, xb = sem("x_sums"), sem("x_roots"), sem("x_kept"), sem("xb")

        with nc.Block() as block:
            @block.sync
            def _(sp):
                sp.dma_start(ctxT[:, :, :, :], k.ap["ctxT"]).then_inc(w0_in, 16)
                sp.dma_start(wk0[:, :, :], k.ap["wk0"]).then_inc(w0_in, 16)
                sp.dma_start(wv0[:, :, :], k.ap["wv0"]).then_inc(w0_in, 16)
                for q in range(4):
                    sp.dma_start(k.X[:, q * TILES // 4:(q + 1) * TILES // 4, :],
                                 k.ap["x"][q * N // 4:(q + 1) * N // 4, :]
                                 .rearrange("(t p) d -> p t d", p=P)).then_inc(x_in[q], 16)
                sp.dma_start(C[:, :, :, :], k.ap["ctx"]).then_inc(c_in, 16)
                for n in range(4):
                    b, j = divmod(n, 2)
                    a, rows = CTX_SPLIT[j]
                    sp.wait_ge(v0_ready, n + 1)
                    sp.dma_start(k.heads0[b, :, a:a + rows, :].rearrange("h k d -> k h d"),
                                 v0[0:rows, b, j, :].rearrange("p (h d) -> p h d", h=H0)).then_inc(v0_stored, 16)
                sp.wait_ge(v0_stored, 16 * 4)
                for b in range(BATCH):
                    for h in range(HALVES):
                        src = k.heads0[b, h * HALF_HEADS:(h + 1) * HALF_HEADS, :, :].rearrange("h k d -> (h k) d")
                        full = CHUNKS - 1
                        sp.dma_start(v0_rows[:, b, h, 0:full, :],
                                     src[0:full * P, :].rearrange("(i p) d -> p i d", p=P)).then_inc(v0_rows_in, 16)
                        if b == h == 0:
                            sp.wait_ge(cleared, 1)
                        sp.dma_start(v0_rows[0:ROWS - full * P, b, h, full, :],
                                     src[full * P:ROWS, :]).then_inc(v0_rows_in, 16)
                sp.dma_start(k.wq0[:, :, :], k.ap["wq0"]).then_inc(k.w0_in, 16)
                sp.dma_start(k.wo0[:, :, :], k.ap["wo0"]).then_inc(k.w0_in, 16)
                for to, name in ((k.wk1, "wk1"), (k.wv1, "wv1"), (k.wo1, "wo1")):
                    sp.dma_start(to[:, :, :], k.ap[name]).then_inc(k.kv_w_in, 16)
                sp.wait_ge(cleared, 3)
                for rows, buffer in ((ROWS0, k.slots0), (ROWS1, k.slots1)):
                    for a in range(0, rows, ZM * P):
                        m = min(ZM, (rows - a) // P)
                        sp.dma_start(buffer[a:a + m * P, :].rearrange("(p m) d -> p m d", m=m),
                                     k.zeros[:, 0:m, :]).then_inc(k.zeroed, 16)
                sp.wait_ge(k.w0_in, 32)

            @block.scalar
            def _(act):
                act.dma_start(k.plain_pack[:, :], k.ap["plain_pack"]).then_inc(plain_in, 16)
                act.dma_start(k.spread_pack[:, :],
                              k.ap["spread_pack"].to_broadcast((P, SPREAD_WIDTH))).then_inc(spread_in, 16)

            @block.gpsimd
            def _(pool):
                nc.gpsimd.memset(v0_rows[:, :, :, CHUNKS - 1, :], 0.0).then_inc(cleared, 1)
                nc.gpsimd.memset(k.zeros[:, :, 0:D], 0.0).then_inc(cleared, 1)
                nc.gpsimd.memset(k.zeros[:, :, D:D + 1], float(SKIP)).then_inc(cleared, 1)
                pool.wait_ge(consts_set, 2)
                inverse_roots(k, pool, x_sums, x_roots)
                pool.wait_ge(ctx_sums, 1)
                nc.gpsimd.tensor_tensor(crs[:, :, :], crs[:, :, :],
                                        k.half_neg[:, 0:4].rearrange("p (b j) -> p b j", b=2),
                                        ALU.pow).then_inc(ctx_roots, 1)

                pool.wait_ge(spread_in, 16)
                for q in range(4):
                    pool.wait_ge(x_kept, q + 1)
                    x = k.X[:, q * TILES // 4:(q + 1) * TILES // 4, :]
                    nc.gpsimd.tensor_tensor(x, x, wide(k.small["bo0"], (P, TILES // 4, D), 1),
                                            ALU.add).then_inc(xb, 1)
                pool.wait_ge(xb, 4)

            @block.tensor
            def _(pe):
                pe.wait_ge(w0_in, 16 * 3)
                for n in range(4):
                    b, h = divmod(n, 2)
                    for c in range(KC):
                        last = nc.tensor.matmul(k.PS[:, 4 + n // 2, (n % 2) * CTX:(n % 2 + 1) * CTX],
                                                wk0[:, c, h * P:(h + 1) * P], ctxT[:, c, b, :],
                                                start=c == 0, stop=c == KC - 1)
                last.then_inc(k0_made, 1)
                for n in range(4):
                    b, j = divmod(n, 2)
                    a, rows = CTX_SPLIT[j]
                    for c in range(KC):
                        last = nc.tensor.matmul(k.PS[0:rows, n, 0:D], ctxT[:, c, b, a:a + rows], wv0[:, c, :],
                                                start=c == 0, stop=c == KC - 1)
                    last.then_inc(v0_made, 1)
                pe.wait_ge(plain_in, 16)
                pe.wait_ge(c_ready, 1)
                for b in range(BATCH):
                    for j, (a, rows) in enumerate(CTX_SPLIT):
                        for c in range(KC):
                            last = nc.tensor.transpose(
                                k.PS[:, 6 + b, c * CTX + a:c * CTX + a + rows],
                                C[0:rows, b, j, c * P:(c + 1) * P], k.ident[0:rows, 0:rows])
                last.then_inc(cT_made, 1)

            @block.vector
            def _(dve):
                own = Own(dve, dve_own)
                nc.vector.memset(k.half_neg[:, :], -0.5).then_inc(consts_set, 1)
                nc.vector.memset(k.half_pos[:, :], 0.5).then_inc(consts_set, 1)
                for h in range(HALVES):
                    nc.vector.memset(k.probs[:, h, ROWS:PADDED], 0.0)
                own.then(nc.vector.memset(crs[:, :, :], 1.0))
                for q in range(4):
                    dve.wait_ge(x_in[q], 16)
                    for t in range(q * TILES // 4, (q + 1) * TILES // 4):
                        last = nc.vector.bn_stats(k.stats[:, t, :], k.X[:, t, :])
                own.then(last)
                statistics(k, own, x_sums)
                dve.wait_ge(spread_in, 16)
                for n in range(4):
                    b, j = divmod(n, 2)
                    rows = CTX_SPLIT[j][1]
                    dve.wait_ge(v0_made, n + 1)
                    nc.vector.tensor_tensor(v0[0:rows, b, j, :], k.PS[0:rows, n, 0:D], k.small["bv0"][0:rows, :],
                                            ALU.add).then_inc(v0_ready, 1)
                dve.wait_ge(c_in, 16)
                for b in range(BATCH):
                    for j, (a, rows) in enumerate(CTX_SPLIT):
                        last = nc.vector.bn_stats(cst[0:rows, b, j, :], C[0:rows, b, j, :])
                own.then(last)
                for b in range(BATCH):
                    for j, (a, rows) in enumerate(CTX_SPLIT):
                        last = nc.vector.bn_aggr(cmv[0:rows, b, j, :], cst[0:rows, b, j, :])
                own.then(last)
                for j, (a, rows) in enumerate(CTX_SPLIT):
                    last = nc.vector.tensor_scalar(crs[0:rows, :, j], cmv[0:rows, :, j, 1], EPS, None, ALU.add)
                last.then_inc(ctx_sums, 1)
                dve.wait_ge(k0_made, 1)
                dve.wait_ge(plain_in, 16)
                for n in range(4):
                    b, h = divmod(n, 2)
                    last = nc.vector.tensor_scalar(kT[:, b, h, :],
                                                   k.PS[:, 4 + n // 2, (n % 2) * CTX:(n % 2 + 1) * CTX],
                                                   k.small["bk0"][:, h:h + 1], None, ALU.add)
                own.then(last)
                own.then(nc.vector.tensor_copy(kT_parts[0][:, :, :, :], kT[:, :, :, :]))
                own.then(nc.vector.tensor_tensor(kT_parts[1][:, :, :, :], kT[:, :, :, :],
                                                 kT_parts[0][:, :, :, :].bitcast(F32), ALU.subtract))
                for part in range(2):
                    spread_keys(k, nc.vector, 0, 0, part)
                dve.wait_ge(x_roots, 1)
                for t in range(TILES):
                    last = apply_normalisation(k, t)
                    if t % (TILES // 4) == TILES // 4 - 1:
                        last.then_inc(x_kept, 1)
                dve.wait_ge(ctx_roots, 1)
                for b in range(BATCH):
                    for j, (a, rows) in enumerate(CTX_SPLIT):
                        last = nc.vector.tensor_scalar(C[0:rows, b, j, :], C[0:rows, b, j, :],
                                                       cmv[0:rows, b, j, 0:1], crs[0:rows, b, j:j + 1],
                                                       ALU.subtract, ALU.mult)
                last.then_inc(c_ready, 1)
                for part in range(2):
                    spread_keys(k, nc.vector, 0, 1, part)
                dve.wait_ge(cT_made, 1)
                for b in range(BATCH):
                    for c in range(KC):
                        nc.vector.tensor_scalar(k.cnT[:, c, b, :], k.PS[:, 6 + b, c * CTX:(c + 1) * CTX],
                                                k.small["g1"][:, c:c + 1], k.small["be1"][:, c:c + 1],
                                                ALU.mult, ALU.add)
                dve.wait_ge(v0_rows_in, 16 * 8)
                for n in range(4):
                    b, h = divmod(n, 2)
                    for w in range(2):
                        mask = k.small["vmask"][:, :, w:w + 1]
                        nc.vector.tensor_tensor(k.values0[:, b, h, :, w, 0:HD0], v0_rows[:, b, h, :, :],
                                                mask.to_broadcast((P, CHUNKS, HD0)), ALU.mult)
                        nc.vector.tensor_copy(k.values0[:, b, h, :, w, HD0:VW], mask)


def attention0_stage(k):
    nc = k.nc
    k.stage_begins()
    with ExitStack() as own_memory:
        def sb(name, shape, dt=F32):
            return own_memory.enter_context(nc.sbuf_tensor(name, shape, dt))

        def sem(name):
            return k.stage_semaphore(name)

        xT = sb("xT", [P, KC, P])
        qT = [sb(f"qT_{part}", [P, HALVES, P], F32R) for part in PARTS]
        peak = sb("peak", [P, GROUPS, GROUP])
        pT = sb("pT", [P, HALVES, CHUNKS, P])
        inv = sb("inv", [P, H0])
        O = sb("O", [P, H0, HD0])
        oT = sb("oT", [P, KC, P])

        scored = sem("scored")
        shifted = sem("shifted")
        raised = sem("raised")
        turned = sem("turned")
        turned_kept = sem("turned_kept")
        summed = sem("summed")
        divided = sem("divided")
        x_turned, xT_ready = sem("x_turned"), sem("xT_ready")
        q_made, qT_ready = sem("q_made"), sem("qT_ready")
        o_turned, oT_ready = sem("o_turned"), sem("oT_ready")
        o_made, x_added = sem("o_made"), sem("x_added")
        keys_spread = sem("keys_spread")
        x_in_ready = sem("x_in_ready")
        xin = sb("xin", [P, D])
        dve_own = sem("dve_own")
        BANK_T, BANK_V, BANK_M = 4, 6, 7
        M = k.PS[:, BANK_M, :]

        def group_bank(g):
            return 2 * (g % 2)

        with nc.Block() as block:
            @block.tensor
            def _(pe):
                def turn_x(t):
                    at_least(pe, x_added, t - 2)
                    for c in range(KC):
                        last = nc.tensor.transpose(M[:, c * P:(c + 1) * P], xin[:, c * P:(c + 1) * P], k.ident)
                    last.then_inc(x_turned, 1)

                def project_q(t):
                    pe.wait_ge(xT_ready, t + 1)
                    for h in range(HALVES):
                        for c in range(KC):
                            last = nc.tensor.matmul(M[:, h * P:(h + 1) * P], k.wq0[:, c, h * P:(h + 1) * P],
                                                    xT[:, c, :], start=c == 0, stop=c == KC - 1)
                    last.then_inc(q_made, 1)

                def score(t, h, b):
                    if h == 0:
                        pe.wait_ge(qT_ready, t + 1)
                    for g in (2 * h, 2 * h + 1):
                        at_least(pe, shifted, 4 * t + g - 1)
                        for q in range(2):
                            a = (g % 2) * GROUP + q * 2
                            last = product(nc, k.PS[:, group_bank(g) + q, 0:2 * CTX],
                                           lambda m: qT[m][:, h, :],
                                           lambda n: k.keys0[n][:, b, h, a:a + 2, :], True, True)
                        last.then_inc(scored, 1)

                def turn(t, h):
                    pe.wait_ge(raised, 4 * t + 2 * h + 2)
                    for f, (c0, m) in enumerate(FILLS):
                        n = 2 * NF * t + NF * h + f
                        at_least(pe, turned_kept, n - 1)
                        for c in range(m):
                            last = nc.tensor.transpose(
                                k.PS[:, BANK_T + (NF * h + f) % 2, c * P:(c + 1) * P],
                                k.probs[:, h, (c0 + c) * P:(c0 + c + 1) * P], k.ident)
                        last.then_inc(turned, 1)

                def weigh(t, h, b):
                    at_least(pe, divided, 2 * t + h)
                    for f, (c0, m) in enumerate(FILLS):
                        pe.wait_ge(turned_kept, 2 * NF * t + NF * h + f + 1)
                        for c in range(c0, c0 + m):
                            a = PAIR0[c] * VW
                            last = nc.tensor.matmul(
                                k.PS[:, BANK_V, a:a + 2 * VW], pT[:, h, c, :],
                                k.values0[:, b, h, c, :, :], start=c == 0, stop=c == CHUNKS - 1,
                                skip_group_check=True)
                    last.then_inc(summed, 1)

                def turn_o(t, prepared):
                    pe.wait_ge(qT_ready, prepared)
                    pe.wait_ge(divided, 2 * t + 2)
                    flat = O[:, :, :].rearrange("p h d -> p (h d)")
                    for c in range(KC):
                        last = nc.tensor.transpose(M[:, c * P:(c + 1) * P], flat[:, c * P:(c + 1) * P], k.ident)
                    last.then_inc(o_turned, 1)

                def project_o(t):
                    pe.wait_ge(oT_ready, t + 1)
                    for c in range(KC):
                        last = nc.tensor.matmul(M[:, 0:D], oT[:, c, :], k.wo0[:, c, :],
                                                start=c == 0, stop=c == KC - 1)
                    last.then_inc(o_made, 1)

                def tile(t, b, before, after):
                    score(t, 0, b)
                    if after:
                        pe.wait_ge(x_in_ready, t + 2)
                        turn_x(t + 1)
                    if before:
                        turn(t - 1, 1)
                        weigh(t - 1, 1, b_before(t, b))
                    score(t, 1, b)
                    if after:
                        project_q(t + 1)
                    turn(t, 0)
                    if before:
                        turn_o(t - 1, t + 2 if after else TILES)
                    weigh(t, 0, b)
                    if before:
                        project_o(t - 1)

                def b_before(t, b):
                    return 0 if isinstance(t, int) and t == TPB else b

                pe.wait_ge(x_in_ready, 1)
                turn_x(0)
                project_q(0)
                tile(0, 0, False, True)
                tile(1, 0, True, True)
                with pe.Fori(2, TPB) as t:
                    tile(t, 0, True, True)
                pe.wait_ge(keys_spread, 2 * HALVES)
                tile(TPB, 1, True, True)
                with pe.Fori(TPB + 1, TILES - 1) as t:
                    tile(t, 1, True, True)
                tile(TILES - 1, 1, True, False)
                turn(TILES - 1, 1)
                weigh(TILES - 1, 1, 1)
                turn_o(TILES - 1, TILES)
                project_o(TILES - 1)

            @block.gpsimd
            def _(pool):
                def stage_in(t):
                    at_least(pool, x_turned, t)
                    nc.gpsimd.tensor_copy(xin[:, :], k.XN[:, t, :]).then_inc(x_in_ready, 1)

                k.clear_spent()
                stage_in(0)
                for h in range(HALVES):
                    for part in range(2):
                        spread_keys(k, nc.gpsimd, 1, h, part).then_inc(keys_spread, 1)
                    stage_in(1 + h)
                with pool.Fori(1 + HALVES, TILES) as t:
                    stage_in(t)

            @block.scalar
            def _(act):
                def raise_scores(t, h):
                    for g in (2 * h, 2 * h + 1):
                        act.wait_ge(shifted, 4 * t + g + 1)
                        part = k.probs[:, h, (g % 2) * GW:(g % 2 + 1) * GW]
                        nc.scalar.activation(part, part, ACT.Exp, scale=HD0 ** -0.5).then_inc(raised, 1)

                def keep_turned(t, h):
                    at_least(act, summed, 2 * t + h - 1)
                    for f, (c0, m) in enumerate(FILLS):
                        act.wait_ge(turned, 2 * NF * t + NF * h + f + 1)
                        nc.scalar.activation(
                            pT[:, h, c0:c0 + m, :],
                            k.PS[:, BANK_T + (NF * h + f) % 2, 0:m * P].rearrange("p (c q) -> p c q", c=m),
                            ACT.Copy).then_inc(turned_kept, 1)

                def keep_o(t):
                    act.wait_ge(o_turned, t + 1)
                    nc.scalar.activation(oT[:, :, :], M[:, 0:D].rearrange("p (c q) -> p c q", c=KC),
                                         ACT.Copy).then_inc(oT_ready, 1)

                def tile(t, before):
                    if before:
                        keep_turned(t - 1, 1)
                    raise_scores(t, 0)
                    keep_turned(t, 0)
                    if before:
                        keep_o(t - 1)
                    raise_scores(t, 1)

                tile(0, False)
                tile(1, True)
                with act.Fori(2, TILES) as t:
                    tile(t, True)
                keep_turned(TILES - 1, 1)
                keep_o(TILES - 1)

            @block.vector
            def _(dve):
                own = Own(dve, dve_own)

                def shift(t, g):
                    h = g // 2
                    scores = k.PS[:, group_bank(g):group_bank(g) + 2, 0:2 * CTX].rearrange(
                        "p q (h k) -> p q h k", h=2)
                    top = peak[:, g, :].rearrange("p (q h) -> p q h", q=2)
                    dve.wait_ge(scored, 4 * t + g + 1)
                    own.then(nc.vector.tensor_reduce(top, scores, X_AXIS, ALU.max))
                    at_least(dve, turned, 2 * NF * (t - 1) + NF * (h + 1))
                    for q in range(2):
                        a = (g % 2) * GW + q * 2 * CTX
                        last = nc.vector.tensor_tensor(
                            k.probs[:, h, a:a + 2 * CTX].rearrange("p (h k) -> p h k", h=2),
                            scores[:, q, :, :],
                            peak[:, g, 2 * q:2 * q + 2].rearrange("p (h a) -> p h a", a=1)
                            .to_broadcast((P, 2, CTX)), ALU.subtract)
                    last.then_inc(shifted, 1)

                def keep_x(t):
                    dve.wait_ge(x_turned, t + 1)
                    nc.vector.tensor_copy(xT[:, :, :], M[:, 0:D].rearrange("p (c q) -> p c q", c=KC))\
                        .then_inc(xT_ready, 1)

                def keep_q(t):
                    dve.wait_ge(q_made, t + 1)
                    for h in range(HALVES):
                        last = nc.vector.tensor_scalar(qT[0][:, h, :], M[:, h * P:(h + 1) * P],
                                                       k.small["bq0"][:, h:h + 1], None, ALU.add)
                    own.then(last)
                    for h in range(HALVES):
                        last = nc.vector.scalar_tensor_tensor(
                            qT[1][:, h, :], M[:, h * P:(h + 1) * P], k.small["bq0"][:, h:h + 1],
                            qT[0][:, h, :].bitcast(F32), ALU.add, ALU.subtract)
                    last.then_inc(qT_ready, 1)

                def divide(t, h):
                    out = k.PS[:, BANK_V, 0:HALF_HEADS * VW].rearrange("p (h v) -> p h v", v=VW)
                    part = inv[:, h * HALF_HEADS:(h + 1) * HALF_HEADS].rearrange("p (h a) -> p h a", a=1)
                    dve.wait_ge(summed, 2 * t + h + 1)
                    own.then(nc.vector.reciprocal(part, out[:, :, HD0:VW]))
                    at_least(dve, o_turned, t)
                    nc.vector.tensor_tensor(O[:, h * HALF_HEADS:(h + 1) * HALF_HEADS, :], out[:, :, 0:HD0],
                                            part.to_broadcast((P, HALF_HEADS, HD0)),
                                            ALU.mult).then_inc(divided, 1)

                def add_x(t):
                    dve.wait_ge(o_made, t + 1)
                    nc.vector.tensor_tensor(k.X[:, t, :], M[:, 0:D], k.X[:, t, :], ALU.add)\
                        .then_inc(x_added, 1)
                    dve.wait_ge(x_added, t + 1)
                    nc.vector.bn_stats(k.stats[:, t, :], k.X[:, t, :])

                def tile(t, before, after):
                    shift(t, 0)
                    shift(t, 1)
                    if after:
                        keep_x(t + 1)
                    if before:
                        divide(t - 1, 1)
                    shift(t, 2)
                    if after:
                        keep_q(t + 1)
                    shift(t, 3)
                    divide(t, 0)
                    if before:
                        add_x(t - 1)

                keep_x(0)
                keep_q(0)
                tile(0, False, True)
                tile(1, True, True)
                with dve.Fori(2, TILES - 1) as t:
                    own.enter(t, 2, GROUPS + HALVES + 1)
                    tile(t, True, True)
                own.leave(TILES - 3)
                tile(TILES - 1, True, False)
                divide(TILES - 1, 1)
                add_x(TILES - 1)


def expert_of_tile(k, eng, tile):
    return eng.value_load(k.expert0[0:1, bass.ds(tile, 1)], min_val=0, max_val=E0 - 1)


def load_w1(k, eng, layer, e):
    eng.dma_start(k.w1_sb[:, :, :], k.ap[f"{layer}w1"][bass.ds(e, 1), :, :, :]
                  .rearrange("a p c f -> p (a c) f")).then_inc(k.weights_in[layer][0], 16)


def load_w2(k, eng, layer, e):
    eng.dma_start(k.w2_sb[:, :, :], k.ap[f"{layer}w2"][bass.ds(e, 1), :, :, :]
                  .rearrange("a p c d -> p (a c) d")).then_inc(k.weights_in[layer][1], 16)


def experts_stage(k, layer, count, slots, made, expert_of):
    nc = k.nc
    b1, b2 = k.ap[f"{layer}b1"], k.ap[f"{layer}b2"]
    HB = W * FC // 512
    CPB = FC // HB
    BANK_X, BANK_Y = 4, 5
    with ExitStack() as own_memory:
        def sb(name, shape, dt=F32):
            return own_memory.enter_context(nc.sbuf_tensor(f"{layer}_{name}", shape, dt))

        def sem(name):
            return k.stage_semaphore(f"{layer}_{name}")

        rows = sb("rows", [P, 2, BLOCKS, D + 1])
        numbers = sb("numbers", [P, count, BLOCKS])
        to = sb("to", [P, 2, BLOCKS], U32)
        seen = sb("seen", [P, count])
        xT = [sb(f"rowsT_{part}", [P, 2, KC, W], F32R) for part in PARTS]
        h = sb("h", [P, FC, W])
        hT = [sb(f"hT_{part}", [P, 2, FC, W], F32R) for part in PARTS]
        w1_sb, w2_sb = k.w1_sb, k.w2_sb
        w1_parts = [sb(f"w1_{part}", [P, 2, KC, F], F32R) for part in PARTS]
        w2_parts = [sb(f"w2_{part}", [P, 2, FC, D], F32R) for part in PARTS]
        b1_sb, b2_sb = sb("b1_sb", [P, 2, FC]), sb("b2_sb", [P, 2, D])
        y = sb("y", [P, 2, BLOCKS, D])
        w1_in, w2_in = k.weights_in[layer]
        rows_in, b1_in, b2_in, stored = (
            [sem(f"{name}{r}") for r in range(2)] for name in ("rows_in", "b1_in", "b2_in", "stored"))
        turned, numbered = sem("rows_turned"), sem("numbered")
        xT_high, xT_ready = sem("rowsT_high"), sem("rowsT_ready")
        w1_high, w1_ready, w2_high, w2_ready = (sem(n) for n in ("w1_high", "w1_ready", "w2_high", "w2_ready"))
        upped = sem("upped")
        bent = sem("bent")
        h_high, h_ready = sem("h_high"), sem("h_ready")
        downed, y_ready = sem("downed"), sem("y_ready")

        def after(i, back=0):
            j, r = i
            return 2 * j + r + 1 - back

        def place(n):
            return divmod(n, 2)

        def tiles(eng, one):
            for n in range(3):
                one(place(n), n == 0, False)
            turns = (count - 4) // 2
            with eng.Fori(1, 1 + turns) as j:
                one((j, 1), False, False)
                one((j + 1, 0), False, False)
            for n in range(3 + 2 * turns, count):
                one(place(n), False, n == count - 1)

        def before(i):
            j, r = i
            return (j, 0) if r else (j - 1, 1)

        def behind(i):
            j, r = i
            return (j + 1, 0) if r else (j, 1)

        with nc.Block() as block:
            @block.sync
            def _(sp):
                def load(i, first):
                    j, r = i
                    e = expert_of(sp, 2 * j + r)
                    if not first:
                        at_least(sp, w1_ready, after(i, 1))
                        load_w1(k, sp, layer, e)
                    at_least(sp, numbered, after(i, 2))
                    sp.dma_start(rows[:, r, :, :],
                                 slots.rearrange("(i n p) d -> i p n d", p=P, n=BLOCKS)[
                                     bass.ds(2 * j + r, 1), :, :, :]
                                 .rearrange("a p n d -> p (a n) d")).then_inc(rows_in[r], 16)
                    if not first:
                        at_least(sp, w2_ready, after(i, 1))
                        load_w2(k, sp, layer, e)
                    at_least(sp, bent, HB * after(i, 2))
                    sp.dma_start(b1_sb[:, r, :], b1[bass.ds(e, 1), :, :].rearrange("a p f -> p (a f)"))\
                        .then_inc(b1_in[r], 16)

                def load_last_bias(i):
                    j, r = i
                    e = expert_of(sp, 2 * j + r)
                    at_least(sp, y_ready, after(i, 2))
                    sp.dma_start(b2_sb[:, r, :], b2[bass.ds(e, 1), :].to_broadcast((P, D))).then_inc(b2_in[r], 16)

                def tile(i, first, last):
                    load(i, first)
                    if not first:
                        load_last_bias(before(i))

                tiles(sp, tile)
                load_last_bias(place(count - 1))

            @block.tensor
            def _(pe):
                def turn(i):
                    j, r = i
                    pe.wait_ge(rows_in[r], 16 * (j + 1))
                    at_least(pe, xT_ready, after(i, 1))
                    for n in range(BLOCKS):
                        for c in range(KC):
                            last = nc.tensor.transpose(k.PS[:, BANK_X, c * W + n * P:c * W + (n + 1) * P],
                                                       rows[:, r, n, c * P:(c + 1) * P], k.ident)
                    last.then_inc(turned, 1)

                def up(i, first):
                    j, r = i
                    pe.wait_ge(w1_ready, after(i))
                    pe.wait_ge(xT_ready, after(i))
                    for q in range(HB):
                        if not first:
                            at_least(pe, bent, HB * after(i, 2) + q + 1)
                        for f in range(q * CPB, (q + 1) * CPB):
                            for c in range(KC):
                                last = product(nc, k.PS[:, q, (f - q * CPB) * W:(f - q * CPB + 1) * W],
                                               lambda a: w1_parts[a][:, r, c, f * P:(f + 1) * P],
                                               lambda b: xT[b][:, r, c, :], c == 0, c == KC - 1)
                        last.then_inc(upped, 1)

                def down(i):
                    j, r = i
                    pe.wait_ge(w2_ready, after(i))
                    pe.wait_ge(h_ready, HB * after(i))
                    at_least(pe, y_ready, after(i, 2))
                    for n in range(BLOCKS):
                        for f in range(FC):
                            last = product(nc, k.PS[:, BANK_Y + r, n * D:(n + 1) * D],
                                           lambda a: hT[a][:, r, f, n * P:(n + 1) * P],
                                           lambda b: w2_parts[b][:, r, f, :], f == 0, f == FC - 1)
                    last.then_inc(downed, 1)

                def tile(i, first, last):
                    up(i, first)
                    if not last:
                        turn(behind(i))
                    if not first:
                        down(before(i))

                turn((0, 0))
                tiles(pe, tile)
                down(place(count - 1))

            @block.scalar
            def _(act):
                def high_w1(i):
                    j, r = i
                    act.wait_ge(w1_in, 16 * after(i))
                    at_least(act, upped, HB * after(i, 2))
                    nc.scalar.activation(w1_parts[0][:, r, :, :], w1_sb[:, :, :], ACT.Copy).then_inc(w1_high, 1)

                def high_w2(i):
                    j, r = i
                    act.wait_ge(w2_in, 16 * after(i))
                    at_least(act, downed, after(i, 2))
                    nc.scalar.activation(w2_parts[0][:, r, :, :], w2_sb[:, :, :], ACT.Copy).then_inc(w2_high, 1)

                def high_x(i):
                    j, r = i
                    act.wait_ge(turned, after(i))
                    at_least(act, upped, HB * after(i, 2))
                    nc.scalar.activation(xT[0][:, r, :, :],
                                         k.PS[:, BANK_X, 0:KC * W].rearrange("p (c w) -> p c w", c=KC),
                                         ACT.Copy).then_inc(xT_high, 1)

                def bend(i, first):
                    j, r = i
                    act.wait_ge(b1_in[r], 16 * (j + 1))
                    at_least(act, downed, after(i, 2))
                    for q in range(HB):
                        act.wait_ge(upped, HB * after(i, 1) + q + 1)
                        if not first:
                            at_least(act, h_ready, HB * after(i, 2) + q + 1)
                        for f in range(q * CPB, (q + 1) * CPB):
                            last = nc.scalar.activation(
                                h[:, f, :], k.PS[:, q, (f - q * CPB) * W:(f - q * CPB + 1) * W],
                                ACT.Gelu, bias=b1_sb[:, r, f:f + 1])
                        last.then_inc(bent, 1)
                        act.wait_ge(bent, HB * after(i, 1) + q + 1)
                        part = slice(q * CPB, (q + 1) * CPB)
                        nc.scalar.activation(hT[0][:, r, part, :], h[:, part, :], ACT.Copy).then_inc(h_high, 1)

                def tile(i, first, last):
                    if not last and not first:
                        high_w1(behind(i))
                    bend(i, first)
                    if first:
                        high_w1(behind(i))
                    if not last:
                        high_x(behind(i))
                        high_w2(behind(i))

                high_w1((0, 0))
                high_x((0, 0))
                high_w2((0, 0))
                tiles(act, tile)

            @block.gpsimd
            def _(pool):
                def store(i):
                    pool.wait_ge(y_ready, after(i))
                    nc.gpsimd.tensor_tensor(seen[:, bass.ds(2 * i[0] + i[1], 1)], k.half_neg[:, 0:1],
                                            k.half_neg[:, 0:1], ALU.add)
                    for n in range(BLOCKS):
                        nc.gpsimd.indirect_dma_start(
                            out=made, out_offset=bass.IndirectOffsetOnAxis(ap=to[:, i[1], n:n + 1], axis=0),
                            in_=y[:, i[1], n, :], in_offset=None, bounds_check=made.shape[0] - 1,
                            oob_is_err=False).then_inc(stored[i[1]], 16)

                tiles(pool, lambda i, first, last: store(i))
                for r in range(2):
                    pool.wait_ge(stored[r], 16 * BLOCKS * ((count + 1 - r) // 2))

            @block.vector
            def _(dve):
                def low(to, of, high):
                    return nc.vector.tensor_tensor(to, of, high.bitcast(F32), ALU.subtract)

                def low_w1(i):
                    r = i[1]
                    dve.wait_ge(w1_high, after(i))
                    low(w1_parts[1][:, r, :, :], w1_sb[:, :, :], w1_parts[0][:, r, :, :]).then_inc(w1_ready, 1)

                def low_w2(i):
                    r = i[1]
                    dve.wait_ge(w2_high, after(i))
                    low(w2_parts[1][:, r, :, :], w2_sb[:, :, :], w2_parts[0][:, r, :, :]).then_inc(w2_ready, 1)

                def low_x(i):
                    j, r = i
                    dve.wait_ge(xT_high, after(i))
                    low(xT[1][:, r, :, :], k.PS[:, BANK_X, 0:KC * W].rearrange("p (c w) -> p c w", c=KC),
                        xT[0][:, r, :, :]).then_inc(xT_ready, 1)
                    nc.vector.tensor_copy(numbers[:, bass.ds(2 * j + r, 1), :],
                                          rows[:, r:r + 1, :, D]).then_inc(numbered, 1)

                def low_h(i):
                    r = i[1]
                    for q in range(HB):
                        part = slice(q * CPB, (q + 1) * CPB)
                        dve.wait_ge(h_high, HB * after(i, 1) + q + 1)
                        low(hT[1][:, r, part, :], h[:, part, :], hT[0][:, r, part, :]).then_inc(h_ready, 1)

                def keep_y(i):
                    j, r = i
                    dve.wait_ge(b2_in[r], 16 * (j + 1))
                    dve.wait_ge(downed, after(i))
                    at_least(dve, stored[r], 16 * BLOCKS * j)
                    dve.wait_ge(numbered, after(i))
                    nc.vector.tensor_copy(to[:, r:r + 1, :], numbers[:, bass.ds(2 * j + r, 1), :])
                    nc.vector.tensor_tensor(
                        y[:, r, :, :], k.PS[:, BANK_Y + r, 0:BLOCKS * D].rearrange("p (n d) -> p n d", n=BLOCKS),
                        b2_sb[:, r:r + 1, :].to_broadcast((P, BLOCKS, D)), ALU.add).then_inc(y_ready, 1)

                def tile(i, first, last):
                    if not last and not first:
                        low_w1(behind(i))
                    low_h(i)
                    if first:
                        low_w1(behind(i))
                    if not last:
                        low_x(behind(i))
                        low_w2(behind(i))
                    if not first:
                        keep_y(before(i))

                low_w1((0, 0))
                low_x((0, 0))
                low_w2((0, 0))
                tiles(dve, tile)
                keep_y(place(count - 1))


def router_tensor(k, pe, experts, weights, xn_ready, turned, hT, hT_ready, scored):
    nc = k.nc
    for t in range(TILES + 2):
        if t < TILES:
            pe.wait_ge(xn_ready, t + 1)
            at_least(pe, hT_ready, t - 2)
            for c in range(KC):
                last = nc.tensor.transpose(k.PS[:, ROUTER_BANKS[t % 3], c * P:(c + 1) * P],
                                           k.XN[:, t, c * P:(c + 1) * P], k.ident)
            last.then_inc(turned, 1)
        if t > 1:
            pe.wait_ge(hT_ready, t - 1)
            for c in range(KC):
                last = nc.tensor.matmul(k.PS[:, 2, (t - 2) * experts:(t - 1) * experts], hT[:, (t - 2) % 3, c, :],
                                        weights[:, c, :], start=c == 0, stop=c == KC - 1)
            last.then_inc(scored, 1)


def router_scalar(k, act, turned, hT, hT_ready, scored):
    for t in range(TILES):
        act.wait_ge(turned, t + 1)
        at_least(act, scored, t - 2)
        k.nc.scalar.activation(hT[:, t % 3, :, :],
                               k.PS[:, ROUTER_BANKS[t % 3], 0:D].rearrange("p (c q) -> p c q", c=KC),
                               ACT.Copy).then_inc(hT_ready, 1)


def running_sum(k, own, source, odd, even):
    nc = k.nc
    for step, to in ((1, odd), (2, even), (4, odd), (8, even)):
        nc.vector.tensor_copy(to[:, 0:step, :], source[:, 0:step, :])
        own.then(nc.vector.tensor_tensor(to[:, step:TILES, :], source[:, step:TILES, :],
                                         source[:, 0:TILES - step, :], ALU.add))
        source = to


def first_of_largest(k, own, one_hot, scores, top, order, experts):
    nc = k.nc
    shape = (P, TILES, experts)
    own.then(nc.vector.tensor_reduce(top, scores, X_AXIS, ALU.max))
    own.then(nc.vector.tensor_tensor(one_hot, scores, wide(top, shape, 2), ALU.is_equal))
    own.then(nc.vector.tensor_tensor(one_hot, one_hot, wide(order, shape, 1), ALU.mult))
    own.then(nc.vector.tensor_reduce(top, one_hot, X_AXIS, ALU.max))
    own.then(nc.vector.tensor_tensor(one_hot, one_hot, wide(top, shape, 2), ALU.is_equal))


def route0_stage(k):
    nc = k.nc
    with ExitStack() as own_memory:
        def sb(name, shape, dt=F32):
            return own_memory.enter_context(nc.sbuf_tensor(name, shape, dt))

        def sem(name):
            return k.stage_semaphore(name)

        hT = sb("hT0", [P, 3, KC, P])
        logits = sb("logits", [P, TILES, E0])
        one_hot = sb("one_hot", [P, TILES, E0])
        upto, part_sum = sb("upto", [P, TILES + 1, E0]), sb("part_sum", [P, TILES, E0])
        place = sb("place", [P, TILES, E0])
        top = sb("top", [P, TILES])
        grid = sb("grid", [P, E0, N // W])
        tiles_of = sb("tiles_of", [P, E0])
        start = sb("start", [P, E0])
        square = sb("square", [P, E0, E0])
        over = sb("over", [P, SLOT_TILES0, E0])
        expert = sb("expert", [P, SLOT_TILES0])
        slot = sb("slot", [P, TILES])
        dve_own, sums, powers = sem("dve_own"), sem("sums"), sem("powers")
        xn_ready, turned, hT_ready, scored = sem("xn_ready"), sem("turned"), sem("hT_ready"), sem("scored")
        chosen, ranked, slots_ready, scattered = sem("chosen"), sem("ranked"), sem("slots_ready"), sem("scattered")
        kn = sb("kn", [P, BATCH, 2, INNER])
        vn = sb("vn", [P, BATCH, 2, INNER])
        sq = sb("sq", [P, INNER])
        kvT = sb("kvT", [P, 2, P])
        ss = sb("ss", [P, BATCH, 2, H1])
        k_made, v_made, sq_made, v_taken = sem("k_made"), sem("v_made"), sem("sq_made"), sem("v_taken")
        k_copied, k_sums, k_roots, kn_ready = sem("k_copied"), sem("k_sums"), sem("k_roots"), sem("kn_ready")
        kvT_made, kvT_ready, m_made, m_taken = sem("kvT_made"), sem("kvT_ready"), sem("m_made"), sem("m_taken")
        BANK_K, BANK_V = 3, 5
        BANK_R = 2
        RANKS, COUNTS = TILES * E0, 2 * TILES * E0
        PAIR_BANKS, M_BANKS = (0, 1), (7, 3)
        experts_known = sem("experts_known")
        with nc.Block() as block:
            @block.sync
            def _(sp):
                sp.wait_ge(experts_known, 1)
                e = expert_of_tile(k, sp, 0)
                load_w1(k, sp, "e0", e)
                load_w2(k, sp, "e0", e)

            @block.tensor
            def _(pe):
                def keys(n):
                    project(n, k.wk1, BANK_K, k_copied, k_made)

                def values(n):
                    project(n, k.wv1, BANK_V, v_taken, v_made)

                def project(n, weights, bank, taken, made):
                    b, j = divmod(n, 2)
                    a, rows = CTX_SPLIT[j]
                    at_least(pe, taken, n)
                    for q in range(2):
                        for c in range(KC):
                            last = nc.tensor.matmul(k.PS[0:rows, bank + q, :], k.cnT[:, c, b, a:a + rows],
                                                    weights[:, c, q * 512:(q + 1) * 512],
                                                    start=c == 0, stop=c == KC - 1)
                    last.then_inc(made, 1)

                pe.wait_ge(k.kv_w_in, 16 * 3)
                keys(0)
                values(0)
                router_tensor(k, pe, E0, k.small["wr0"], xn_ready, turned, hT, hT_ready, scored)
                keys(1)
                pe.wait_ge(chosen, 1)
                nc.tensor.matmul(k.PS[:, BANK_R, RANKS:RANKS + TILES * E0], k.small["tri"],
                                 one_hot[:, :, :], start=True, stop=False)
                nc.tensor.matmul(k.PS[:, BANK_R, RANKS:RANKS + TILES * E0], k.small["ones"],
                                 upto[:, 0:TILES, :], start=False, stop=True)
                nc.tensor.matmul(k.PS[:, BANK_R, COUNTS:COUNTS + E0], k.small["ones"], upto[:, TILES, :],
                                 start=True, stop=True).then_inc(ranked, 1)
                values(1)
                for n in (2, 3):
                    keys(n)
                    values(n)

                def pair_product(n):
                    b, i = divmod(n, IC)
                    pe.wait_ge(kn_ready, 2 * b + 2)
                    pe.wait_ge(v_taken, 2 * b + 2)
                    at_least(pe, kvT_ready, n - 1)
                    for j, (a, rows) in enumerate(CTX_SPLIT):
                        last = nc.tensor.matmul(k.PS[:, PAIR_BANKS[n % 2], 0:P], vn[0:rows, b, j, i * P:(i + 1) * P],
                                                kn[0:rows, b, j, i * P:(i + 1) * P], start=j == 0, stop=j == 1)
                    last.then_inc(kvT_made, 1)

                pair_product(0)
                pe.wait_ge(k_copied, 4)
                for n in range(BATCH * IC):
                    if n + 1 < BATCH * IC:
                        pair_product(n + 1)
                    pe.wait_ge(kvT_ready, n + 1)
                    at_least(pe, m_taken, n - 1)
                    nc.tensor.matmul(k.PS[:, M_BANKS[n % 2], 0:D], kvT[:, n % 2, :], k.wo1[:, n % IC, :],
                                     start=True, stop=True).then_inc(m_made, 1)

            @block.scalar
            def _(act):
                def square_keys(n):
                    rows = CTX_SPLIT[n % 2][1]
                    act.wait_ge(k_made, n + 1)
                    at_least(act, k_sums, n)
                    nc.scalar.activation(sq[0:rows, :], k.PS[0:rows, BANK_K:BANK_K + 2, :],
                                         ACT.Square).then_inc(sq_made, 1)

                def keep_values(n):
                    b, j = divmod(n, 2)
                    rows = CTX_SPLIT[j][1]
                    act.wait_ge(v_made, n + 1)
                    nc.scalar.activation(vn[0:rows, b, j, :], k.PS[0:rows, BANK_V:BANK_V + 2, :],
                                         ACT.Copy).then_inc(v_taken, 1)

                square_keys(0)
                keep_values(0)
                router_scalar(k, act, turned, hT, hT_ready, scored)
                for n in range(1, 4):
                    square_keys(n)
                    keep_values(n)
                for n in range(BATCH * IC):
                    b, i = divmod(n, IC)
                    act.wait_ge(m_made, n + 1)
                    nc.scalar.activation(k.keyval1[:, b, i, :], k.PS[:, M_BANKS[n % 2], 0:D],
                                         ACT.Copy).then_inc(m_taken, 1)

            @block.gpsimd
            def _(pool):
                def root_keys(n):
                    b, j = divmod(n, 2)
                    rows = CTX_SPLIT[j][1]
                    pool.wait_ge(k_sums, n + 1)
                    nc.gpsimd.tensor_tensor(ss[0:rows, b, j, :], ss[0:rows, b, j, :],
                                            k.half_pos[0:rows, 0:H1], ALU.pow).then_inc(k_roots, 1)

                inverse_roots(k, pool, sums, powers)
                root_keys(0)
                root_keys(1)
                pool.wait_ge(k.zeroed, 16 * SLOT_STORES)
                pool.wait_ge(slots_ready, 1)
                for t in range(TILES):
                    nc.gpsimd.indirect_dma_start(
                        out=k.slots0, out_offset=bass.IndirectOffsetOnAxis(ap=k.slot0[:, t:t + 1], axis=0),
                        in_=k.rows_out[:, t, :], in_offset=None).then_inc(scattered, 16)
                    if t == 3:
                        root_keys(2)
                    if t == 6:
                        root_keys(3)
                pool.wait_ge(scattered, 16 * TILES)

            @block.vector
            def _(dve):
                own = Own(dve, dve_own)

                def sum_keys(n):
                    b, j = divmod(n, 2)
                    rows = CTX_SPLIT[j][1]
                    dve.wait_ge(sq_made, n + 1)
                    nc.vector.tensor_copy(kn[0:rows, b, j, :], k.PS[0:rows, BANK_K:BANK_K + 2, :])\
                        .then_inc(k_copied, 1)
                    nc.vector.tensor_reduce(ss[0:rows, b, j, :],
                                            sq[0:rows, :].rearrange("p (h d) -> p h d", h=H1),
                                            X_AXIS, ALU.add).then_inc(k_sums, 1)

                def unit_keys(n):
                    b, j = divmod(n, 2)
                    rows = CTX_SPLIT[j][1]
                    norms = ss[0:rows, b, j, :]
                    dve.wait_ge(k_roots, n + 1)
                    own.then(nc.vector.tensor_scalar(norms, norms, 1e-12, None, ALU.max))
                    own.then(nc.vector.reciprocal(norms, norms))
                    view = kn[0:rows, b, j, :].rearrange("p (h d) -> p h d", h=H1)
                    dve.wait_ge(k_copied, n + 1)
                    nc.vector.tensor_tensor(view, view, wide(norms, (rows, H1, HD1), 2),
                                            ALU.mult).then_inc(kn_ready, 1)

                nc.vector.tensor_copy(k.rows_out[:, :, D], k.small["token_no"])
                statistics(k, own, sums)
                dve.wait_ge(powers, 1)
                for t in range(TILES):
                    apply_normalisation(k, t).then_inc(xn_ready, 1)
                    if t == 7:
                        sum_keys(0)
                dve.wait_ge(scored, TILES)
                own.then(nc.vector.tensor_tensor(
                    logits[:, :, :], k.PS[:, BANK_R, 0:TILES * E0].rearrange("p (t e) -> p t e", t=TILES),
                    wide(k.small["br0"], (P, TILES, E0), 1), ALU.add))
                first_of_largest(k, own, one_hot[:, :, :], logits[:, :, :], top[:, :], k.small["order0"], E0)
                own.then(nc.vector.memset(upto[:, 0, :], 0.0))
                running_sum(k, own, one_hot, part_sum, upto[:, 1:TILES + 1, :])
                dve.sem_inc(chosen, 1)
                sum_keys(1)
                dve.wait_ge(ranked, 1)
                own.then(nc.vector.tensor_tensor(
                    grid[:, :, :], wide(k.PS[:, BANK_R, COUNTS:COUNTS + E0], (P, E0, N // W), 2),
                    wide(k.small["thresh0"], (P, E0, N // W), 1), ALU.is_gt))
                own.then(nc.vector.tensor_reduce(tiles_of[:, :], grid[:, :, :], X_AXIS, ALU.add))
                own.then(nc.vector.tensor_tensor(square[:, :, :], k.small["before0"],
                                                 wide(tiles_of[:, :], (P, E0, E0), 1), ALU.mult))
                own.then(nc.vector.tensor_reduce(start[:, :], square[:, :, :], X_AXIS, ALU.add))
                nc.vector.tensor_tensor(tiles_of[:, :], tiles_of[:, :], start[:, :], ALU.add)
                own.then(nc.vector.tensor_scalar(start[:, :], start[:, :], float(W), None, ALU.mult))
                own.then(nc.vector.tensor_tensor(
                    place[:, :, :], k.PS[:, BANK_R, RANKS:RANKS + TILES * E0]
                    .rearrange("p (t e) -> p t e", t=TILES),
                    wide(start[:, :], (P, TILES, E0), 1), ALU.add))
                own.then(nc.vector.tensor_tensor(place[:, :, :], place[:, :, :], one_hot[:, :, :], ALU.mult))
                own.then(nc.vector.tensor_reduce(slot[:, :], place[:, :, :], X_AXIS, ALU.add))
                nc.vector.tensor_copy(k.slot0[:, :], slot[:, :]).then_inc(slots_ready, 1)
                own.then(nc.vector.tensor_tensor(
                    over[:, :, :], wide(k.small["tile_no"], (P, SLOT_TILES0, E0), 2),
                    wide(tiles_of[:, :], (P, SLOT_TILES0, E0), 1), ALU.is_ge))
                own.then(nc.vector.tensor_reduce(expert[:, :], over[:, :, :], X_AXIS, ALU.add))
                nc.vector.tensor_scalar(k.expert0[:, :], expert[:, :], float(E0 - 1), None, ALU.min)\
                    .then_inc(experts_known, 1)
                unit_keys(0)
                unit_keys(1)
                sum_keys(2)
                sum_keys(3)
                unit_keys(2)
                for n in range(BATCH * IC):
                    if n == 2:
                        unit_keys(3)
                    dve.wait_ge(kvT_made, n + 1)
                    at_least(dve, m_made, n - 1)
                    nc.vector.tensor_tensor(kvT[:, n % 2, :], k.PS[:, PAIR_BANKS[n % 2], 0:P], k.small["pairmask"],
                                            ALU.mult).then_inc(kvT_ready, 1)


def attention1_stage(k):
    nc = k.nc
    k.stage_begins()
    with ExitStack() as own_memory:
        def sb(name, shape, dt=F32):
            return own_memory.enter_context(nc.sbuf_tensor(name, shape, dt))

        def sem(name):
            return k.stage_semaphore(name)

        wq, w1, w2 = sb("wq", [P, KC, INNER]), k.w1_sb, k.w2_sb
        squares = sb("squares", [P, D])
        router_rows = sb("router_rows", [P, D])
        x2 = sb("x2", [P, D])
        n_measured, x_kept, row_kept = sem("n_measured"), sem("x_kept"), sem("row_kept")
        qb_ready, qb_used = sem("qb_ready"), sem("qb_used")
        n_stats, n_mean, n_root, n_root2 = (sb(n, [P, width]) for n, width in (
            ("n_stats", 6), ("n_mean", 2), ("n_root", 1), ("n_root2", 1)))
        rT = sb("rT", [P, KC, P])
        n_summed, n_rooted, n_once, n_squared, n_summed2, n_rooted2, n_ready = (sem(n) for n in (
            "n_summed", "n_rooted", "n_once", "n_squared", "n_summed2", "n_rooted2", "n_ready"))
        r_turned, rT_ready, l_made, l_ready = (sem(n) for n in ("r_turned", "rT_ready", "l_made", "l_ready"))
        wq_in, w1_in, w2_in = sem("wq_in"), sem("w1_in"), sem("w2_in")
        fixed_high, fixed_ready = sem("fixed_high"), sem("fixed_ready")
        xhT_made, xhT_high, qnT_high, h_high, h_ready = (sem(n) for n in (
            "xhT_made", "xhT_high", "qnT_high", "h_high", "h_ready"))
        mean2 = sb("mean2", [P, TILES, 2])
        rstd2 = sb("rstd2", [P, TILES])
        xh = sb("xh", [P, D])
        xhT = sb("xhT", [P, KC, P])
        xhT_parts, qnT, hT_parts, wq_parts, w2_parts, kv_parts = (
            [sb(f"{name}_{part}", shape, F32R) for part in PARTS] for name, shape in (
                ("xhT", [P, KC, P]), ("qnT", [P, IC, P]), ("hT1", [P, FC, P]), ("wq1", [P, KC, INNER]),
                ("mw2", [P, FC, D]), ("keyval1", [P, BATCH, IC, D])))
        sq = sb("sq1", [P, INNER])
        ss = sb("ss1", [P, H1])
        rn = sb("rn1", [P, H1])
        qn = sb("qn", [P, INNER])
        qb = sb("qb", [P, 2, D])
        x1 = sb("x1", [P, 1, D])
        st1 = sb("st1", [P, 6])
        mv1 = sb("mv1", [P, 2])
        rs1 = sb("rs1", [P, 1])
        xh1 = sb("xh1", [P, D])
        xh1T = sb("xh1T", [P, KC, P])
        hT = sb("hT1", [P, FC, P])
        QT = TILES // 4
        made_in = [sem(f"made_in{q}") for q in range(4)]
        dve_own, x_whole = sem("dve_own"), sem("x_whole")
        sums, powers, sums2, powers2 = sem("sums"), sem("powers"), sem("sums2"), sem("powers2")
        xh_ready, xh_turned, xhT_ready = sem("xh_ready"), sem("xh_turned"), sem("xhT_ready")
        q_made, squared, q_summed, q_rooted, qn_ready = (sem(n) for n in (
            "q_made", "squared", "q_summed", "q_rooted", "qn_ready"))
        qn_turned, qnT_ready, o_made, x1_ready = (sem(n) for n in (
            "qn_turned", "qnT_ready", "o_made", "x1_ready"))
        x1_summed, x1_rooted, xh1_ready, xh1_turned, xh1T_ready = (sem(n) for n in (
            "x1_summed", "x1_rooted", "xh1_ready", "xh1_turned", "xh1T_ready"))
        upped, bent, downed, x_ready = (sem(n) for n in (
            "upped", "bent", "downed", "x_ready"))
        FIXED = {0: 1, 1: 2, 2: 3, TPB: 4}
        BANK_Q, BANK_QT, BANK_H, BANK_Y, BANK_T = 0, 2, 4, 6, 7

        def fixed(n, part):
            source, parts = ((wq[:, :, :], [w[:, :, :] for w in wq_parts]),
                             (k.keyval1[:, 0, :, :], [w[:, 0, :, :] for w in kv_parts]),
                             (w2[:, :, :], [w[:, :, :] for w in w2_parts]),
                             (k.keyval1[:, 1, :, :], [w[:, 1, :, :] for w in kv_parts]))[n]
            return source if part is None else parts[part]

        with nc.Block() as block:
            @block.sync
            def _(sp):
                for q in range(4):
                    sp.dma_start(k.XN[:, q * TILES // 4:(q + 1) * TILES // 4, :],
                                 k.made0[q * N // 4:(q + 1) * N // 4, :]
                                 .rearrange("(t p) d -> p t d", p=P)).then_inc(made_in[q], 16)
                    if q == 0:
                        sp.dma_start(wq[:, :, :], k.ap["wq1"]).then_inc(wq_in, 16)
                sp.dma_start(w1[:, :, :], k.ap["mw1"]).then_inc(w1_in, 16)
                sp.dma_start(w2[:, :, :], k.ap["mw2"]).then_inc(w2_in, 16)
                for a in range(0, 2 * N, ZM * P):
                    sp.dma_start(k.made1[a:a + ZM * P, :].rearrange("(p m) d -> p m d", m=ZM),
                                 k.zeros[:, :, 0:D]).then_inc(k.zeroed, 16)

            def turns(eng, one):
                one(0, "ba")
                one(1, "bcda")
                one(2, "becfdag")
                one(3, "becfdagn")
                one(4, "becrfldagn")
                with eng.Fori(5, TPB) as s:
                    one(s, "becrfldagn", 0)
                one(TPB, "becrfldagn", 0)
                with eng.Fori(TPB + 1, TILES - 1) as s:
                    one(s, "becrfldagn", 1)
                one(TILES - 1, "becrfldgn", 1)
                one(TILES, "ecrfldgn", 1)
                one(TILES + 1, "erflgn", 1)
                one(TILES + 2, "rln", 1)
                one(TILES + 3, "rl", 1)

            @block.tensor
            def _(pe):
                def a(t):
                    pe.wait_ge(xh_ready, t + 1)
                    if not isinstance(t, int) or t > 2:
                        pe.wait_ge(xh1T_ready, t - 2)
                    if not isinstance(t, int) or t > 4:
                        pe.wait_ge(l_ready, t - 4)
                    for c in range(KC):
                        last = nc.tensor.transpose(k.PS[:, BANK_T, c * P:(c + 1) * P], xh[:, c * P:(c + 1) * P],
                                                   k.ident)
                    last.then_inc(xh_turned, 1)

                def b(t):
                    pe.wait_ge(xhT_ready, t + 1)
                    at_least(pe, qn_ready, t)
                    for q in range(2):
                        for c in range(KC):
                            last = product(nc, k.PS[:, BANK_Q + q, :], lambda a: xhT_parts[a][:, c, :],
                                           lambda b: wq_parts[b][:, c, q * 512:(q + 1) * 512],
                                           c == 0, c == KC - 1)
                    last.then_inc(q_made, 1)

                def c(t):
                    pe.wait_ge(qn_ready, t + 1)
                    at_least(pe, qnT_ready, t)
                    for i in range(IC):
                        last = nc.tensor.transpose(k.PS[:, BANK_QT + i // 4, (i % 4) * P:(i % 4 + 1) * P],
                                                   qn[:, i * P:(i + 1) * P], k.ident)
                    last.then_inc(qn_turned, 1)

                def d(t, batch):
                    pe.wait_ge(qnT_ready, t + 1)
                    if not isinstance(t, int) or t > 0:
                        at_least(pe, x_ready, t - 1)
                    for i in range(IC):
                        last = product(nc, k.PS[:, BANK_Y, 0:D], lambda a: qnT[a][:, i, :],
                                       lambda b: kv_parts[b][:, batch, i, :], i == 0, i == IC - 1)
                    last.then_inc(o_made, 1)

                def e(t):
                    pe.wait_ge(xh1_ready, t + 1)
                    pe.wait_ge(xhT_ready, t + 3 if not isinstance(t, int) or t + 3 < TILES else TILES)
                    for c in range(KC):
                        last = nc.tensor.transpose(k.PS[:, BANK_T, c * P:(c + 1) * P],
                                                   xh1[:, c * P:(c + 1) * P], k.ident)
                    last.then_inc(xh1_turned, 1)

                def r(t, free):
                    pe.wait_ge(n_ready, t + 1)
                    pe.wait_ge(xh1T_ready, free)
                    if isinstance(t, int) and t >= TILES - 2:
                        pe.wait_ge(l_ready, t)
                    for c in range(KC):
                        last = nc.tensor.transpose(k.PS[:, BANK_T, c * P:(c + 1) * P],
                                                   router_rows[:, c * P:(c + 1) * P], k.ident)
                    last.then_inc(r_turned, 1)

                def l(t):
                    pe.wait_ge(rT_ready, t + 1)
                    for c in range(KC):
                        last = nc.tensor.matmul(k.PS[:, BANK_T, 0:E1], rT[:, c, :], k.small["wr1"][:, c, :],
                                                start=c == 0, stop=c == KC - 1)
                    last.then_inc(l_made, 1)

                def f(t):
                    pe.wait_ge(xh1T_ready, t + 1)
                    for q in range(2):
                        at_least(pe, bent, 2 * (t - 1) + q + 1)
                        for f in range(4 * q, 4 * q + 4):
                            for c in range(KC):
                                last = nc.tensor.matmul(k.PS[:, BANK_H + q, (f - 4 * q) * P:(f - 4 * q + 1) * P],
                                                        w1[:, c, f * P:(f + 1) * P], xh1T[:, c, :],
                                                        start=c == 0, stop=c == KC - 1)
                        last.then_inc(upped, 1)

                def g(t, last_x1):
                    pe.wait_ge(h_ready, 2 * t + 2)
                    pe.wait_ge(x1_ready, last_x1)
                    for f in range(FC):
                        last = product(nc, k.PS[:, BANK_Y, 0:D], lambda a: hT_parts[a][:, f, :],
                                       lambda b: w2_parts[b][:, f, :], f == 0, f == FC - 1)
                    last.then_inc(downed, 1)

                def turn(s, steps, batch=0):
                    if isinstance(s, int) and s in FIXED:
                        pe.wait_ge(fixed_ready, FIXED[s])
                        if s == 2:
                            pe.wait_ge(w1_in, 16)
                    for step in steps:
                        if step == "a":
                            a(s + 1)
                        elif step == "b":
                            b(s)
                        elif step == "c":
                            c(s - 1)
                        elif step == "d":
                            d(s - 1, batch)
                        elif step == "e":
                            e(s - 2)
                        elif step == "f":
                            f(s - 2)
                        elif step == "r":
                            r(s - 4, TILES if isinstance(s, int) and s > TILES + 1 else s - 1)
                        elif step == "l":
                            l(s - 4)
                        elif step == "g":
                            g(s - 2, TILES if isinstance(s, int) and s > TILES else s)

                a(0)
                turns(pe, turn)

            @block.scalar
            def _(act):
                def high_fixed(n):
                    if n in (0, 2):
                        act.wait_ge(w2_in if n else wq_in, 16)
                    nc.scalar.activation(fixed(n, 0), fixed(n, None), ACT.Copy).then_inc(fixed_high, 1)

                def high_xh(t):
                    act.wait_ge(xhT_made, t + 1)
                    at_least(act, q_made, t)
                    nc.scalar.activation(xhT_parts[0][:, :, :], xhT[:, :, :], ACT.Copy).then_inc(xhT_high, 1)

                def square(t):
                    act.wait_ge(q_made, t + 1)
                    at_least(act, q_summed, t)
                    nc.scalar.activation(sq[:, :], k.PS[:, BANK_Q:BANK_Q + 2, :], ACT.Square)\
                        .then_inc(squared, 1)

                def keep_x(t):
                    act.wait_ge(x_ready, t + 1)
                    nc.scalar.activation(k.X[:, t, :], x2[:, :], ACT.Copy).then_inc(x_kept, 1)

                def keep_row(t):
                    act.wait_ge(n_ready, t + 1)
                    nc.scalar.activation(k.XN[:, t, :], router_rows[:, :], ACT.Copy).then_inc(row_kept, 1)

                def square_n(t):
                    act.wait_ge(n_once, t + 1)
                    at_least(act, n_summed2, t)
                    nc.scalar.activation(squares[:, :], k.XN[:, t, :], ACT.Square).then_inc(n_squared, 1)

                def keep_r(t):
                    act.wait_ge(r_turned, t + 1)
                    at_least(act, l_made, t)
                    nc.scalar.activation(rT[:, :, :], k.PS[:, BANK_T, 0:D].rearrange("p (c q) -> p c q", c=KC),
                                         ACT.Copy).then_inc(rT_ready, 1)

                def keep_q(t):
                    act.wait_ge(qn_turned, t + 1)
                    at_least(act, o_made, t)
                    nc.scalar.activation(qnT[0][:, :, :], k.PS[:, BANK_QT:BANK_QT + 2, :]
                                         .rearrange("p b (c q) -> p (b c) q", c=4), ACT.Copy)\
                        .then_inc(qnT_high, 1)

                def bend(t):
                    at_least(act, downed, t)
                    for q in range(2):
                        act.wait_ge(upped, 2 * t + q + 1)
                        at_least(act, h_ready, 2 * (t - 1) + q + 1)
                        for f in range(4 * q, 4 * q + 4):
                            last = nc.scalar.activation(
                                hT[:, f, :], k.PS[:, BANK_H + q, (f - 4 * q) * P:(f - 4 * q + 1) * P],
                                ACT.Gelu, bias=k.small["mb1"][:, f:f + 1])
                        last.then_inc(bent, 1)
                        act.wait_ge(bent, 2 * t + q + 1)
                        part = slice(4 * q, 4 * q + 4)
                        nc.scalar.activation(hT_parts[0][:, part, :], hT[:, part, :], ACT.Copy)\
                            .then_inc(h_high, 1)

                def turn(s, steps, batch=0):
                    if "b" in steps:
                        square(s)
                    if "n" in steps:
                        keep_x(s - 3)
                    if "r" in steps:
                        keep_row(s - 4)
                    if "c" in steps:
                        keep_q(s - 1)
                    if "n" in steps:
                        square_n(s - 3)
                    if "r" in steps:
                        keep_r(s - 4)
                    if isinstance(s, int) and s < 2:
                        high_fixed(s + 2)
                    if "f" in steps:
                        bend(s - 2)
                    if "a" in steps:
                        high_xh(s + 1)

                high_fixed(0)
                high_fixed(1)
                high_xh(0)
                turns(act, turn)

            @block.gpsimd
            def _(pool):
                k.clear_spent()

                def add_made(q):
                    part = slice(q * QT, (q + 1) * QT)
                    pool.wait_ge(made_in[q], 16)
                    nc.gpsimd.tensor_tensor(k.X[:, part, :], k.X[:, part, :], k.XN[:, part, :], ALU.add)\
                        .then_inc(x_whole, 1)

                def prepare(q):
                    part = slice(q * QT, (q + 1) * QT)
                    pool.wait_ge(sums, q + 1)
                    nc.gpsimd.tensor_tensor(k.rstd[:, part], k.rstd[:, part], k.half_neg[:, 0:QT],
                                            ALU.pow).then_inc(powers, 1)
                    pool.wait_ge(sums2, q + 1)
                    nc.gpsimd.tensor_tensor(rstd2[:, part], rstd2[:, part], k.half_neg[:, 0:QT], ALU.pow)\
                        .then_inc(powers2, 1)

                def root_q(t):
                    pool.wait_ge(q_summed, t + 1)
                    at_least(pool, qn_ready, t)
                    nc.gpsimd.tensor_tensor(rn[:, :], ss[:, :], k.half_pos[:, 0:H1], ALU.pow)\
                        .then_inc(q_rooted, 1)

                def add_biases(t):
                    at_least(pool, qb_used, t)
                    nc.gpsimd.tensor_tensor(qb[:, 0, :], k.XN[:, t, :], k.small["bo1"], ALU.add)
                    nc.gpsimd.tensor_tensor(qb[:, 1, :], k.X[:, t, :], k.small["mb2"], ALU.add)\
                        .then_inc(qb_ready, 1)

                def root_n(t, of, summed, rooted):
                    pool.wait_ge(summed, t + 1)
                    nc.gpsimd.tensor_tensor(of[:, :], of[:, :], k.half_neg[:, 0:1], ALU.pow).then_inc(rooted, 1)

                def root_x1(t):
                    pool.wait_ge(x1_summed, t + 1)
                    nc.gpsimd.tensor_tensor(rs1[:, :], rs1[:, :], k.half_neg[:, 0:1], ALU.pow)\
                        .then_inc(x1_rooted, 1)

                def turn(s, steps, batch=0):
                    if "n" in steps:
                        root_n(s - 3, n_root, n_summed, n_rooted)
                    if "b" in steps:
                        root_q(s)
                    if "d" in steps:
                        add_biases(s - 1)
                    if "n" in steps:
                        root_n(s - 3, n_root2, n_summed2, n_rooted2)
                    if "d" in steps:
                        root_x1(s - 1)
                    if isinstance(s, int) and s < 3:
                        prepare(s + 1)
                        if s < 2:
                            add_made(s + 2)

                prepare(0)
                add_made(1)
                turns(pool, turn)

            @block.vector
            def _(dve):
                own = Own(dve, dve_own)

                def low(to, of, high):
                    return nc.vector.tensor_tensor(to, of, high.bitcast(F32), ALU.subtract)

                def low_fixed(n):
                    dve.wait_ge(fixed_high, n + 1)
                    low(fixed(n, 1), fixed(n, None), fixed(n, 0)).then_inc(fixed_ready, 1)

                def prepare(q):
                    tiles = range(q * QT, (q + 1) * QT)
                    part = slice(q * QT, (q + 1) * QT)
                    if q == 0:
                        dve.wait_ge(made_in[0], 16)
                        for t in tiles:
                            last = nc.vector.tensor_tensor(k.X[:, t, :], k.X[:, t, :], k.XN[:, t, :], ALU.add)
                        own.then(last)
                    else:
                        dve.wait_ge(x_whole, q)
                    for t in tiles:
                        last = nc.vector.bn_stats(k.stats[:, t, :], k.X[:, t, :])
                    own.then(last)
                    for t in tiles:
                        last = nc.vector.bn_aggr(k.mv[:, t, :], k.stats[:, t, :])
                    own.then(last)
                    nc.vector.tensor_scalar(k.rstd[:, part], k.mv[:, part, 1], EPS, None, ALU.add)\
                        .then_inc(sums, 1)
                    low_fixed(q)
                    dve.wait_ge(powers, q + 1)
                    for t in tiles:
                        last = apply_normalisation(k, t)
                    own.then(last)
                    for t in tiles:
                        last = nc.vector.bn_stats(k.stats[:, t, :], k.XN[:, t, :])
                    own.then(last)
                    for t in tiles:
                        last = nc.vector.bn_aggr(mean2[:, t, :], k.stats[:, t, :])
                    own.then(last)
                    nc.vector.tensor_scalar(rstd2[:, part], mean2[:, part, 1], EPS, None, ALU.add)\
                        .then_inc(sums2, 1)

                def normalise_again(t):
                    at_least(dve, xh_turned, t)
                    nc.vector.tensor_scalar(xh[:, :], k.XN[:, t, :], mean2[:, t, 0:1], rstd2[:, bass.ds(t, 1)],
                                            ALU.subtract, ALU.mult).then_inc(xh_ready, 1)

                def keep_xh(t):
                    dve.wait_ge(xh_turned, t + 1)
                    at_least(dve, xhT_high, t)
                    at_least(dve, q_made, t)
                    for c in range(KC):
                        last = nc.vector.tensor_scalar(xhT[:, c, :], k.PS[:, BANK_T, c * P:(c + 1) * P],
                                                       k.small["g1"][:, c:c + 1], k.small["be1"][:, c:c + 1],
                                                       ALU.mult, ALU.add)
                    last.then_inc(xhT_made, 1)

                def low_xh(t):
                    dve.wait_ge(xhT_high, t + 1)
                    low(xhT_parts[1][:, :, :], xhT[:, :, :], xhT_parts[0][:, :, :]).then_inc(xhT_ready, 1)

                def sum_q(t):
                    dve.wait_ge(squared, t + 1)
                    at_least(dve, q_rooted, t)
                    nc.vector.tensor_reduce(ss[:, :], sq[:, :].rearrange("p (h d) -> p h d", h=H1),
                                            X_AXIS, ALU.add).then_inc(q_summed, 1)

                def unit_q(t):
                    dve.wait_ge(q_rooted, t + 1)
                    own.then(nc.vector.tensor_scalar(rn[:, :], rn[:, :], 1e-12, None, ALU.max))
                    own.then(nc.vector.reciprocal(rn[:, :], rn[:, :]))
                    at_least(dve, qn_turned, t)
                    nc.vector.tensor_tensor(
                        qn[:, :].rearrange("p (h d) -> p h d", h=H1),
                        k.PS[:, BANK_Q:BANK_Q + 2, :].rearrange("p b (h d) -> p (b h) d", d=HD1),
                        wide(rn[:, :], (P, H1, HD1), 2), ALU.mult).then_inc(qn_ready, 1)

                def low_q(t):
                    dve.wait_ge(qnT_high, t + 1)
                    low(qnT[1][:, :, :], k.PS[:, BANK_QT:BANK_QT + 2, :].rearrange("p b (c q) -> p (b c) q", c=4),
                        qnT[0][:, :, :]).then_inc(qnT_ready, 1)

                def low_h(t, q):
                    part = slice(4 * q, 4 * q + 4)
                    dve.wait_ge(h_high, 2 * t + q + 1)
                    low(hT_parts[1][:, part, :], hT[:, part, :], hT_parts[0][:, part, :]).then_inc(h_ready, 1)

                def residual(t):
                    dve.wait_ge(qb_ready, t + 1)
                    dve.wait_ge(o_made, t + 1)
                    nc.vector.tensor_tensor(x1[:, 0, :], k.PS[:, BANK_Y, 0:D], qb[:, 0, :], ALU.add)\
                        .then_inc(x1_ready, 1)

                def measure_x1(t):
                    dve.wait_ge(x1_ready, t + 1)
                    own.then(nc.vector.bn_stats(st1[:, :], x1[:, 0, :]))
                    nc.vector.tensor_tensor(k.X[:, t, :], qb[:, 1, :], x1[:, 0, :], ALU.add).then_inc(qb_used, 1)
                    own.then(nc.vector.bn_aggr(mv1[:, :], st1[:, :]))
                    nc.vector.tensor_scalar(rs1[:, :], mv1[:, 1:2], EPS, None, ALU.add).then_inc(x1_summed, 1)

                def normalise_x1(t):
                    dve.wait_ge(x1_rooted, t + 1)
                    at_least(dve, xh1_turned, t)
                    nc.vector.tensor_scalar(xh1[:, :], x1[:, 0, :], mv1[:, 0:1], rs1[:, 0:1],
                                            ALU.subtract, ALU.mult).then_inc(xh1_ready, 1)

                def keep_xh1(t):
                    dve.wait_ge(xh1_turned, t + 1)
                    at_least(dve, upped, 2 * t)
                    for c in range(KC):
                        last = nc.vector.tensor_scalar(xh1T[:, c, :], k.PS[:, BANK_T, c * P:(c + 1) * P],
                                                       k.small["g2"][:, c:c + 1], k.small["be2"][:, c:c + 1],
                                                       ALU.mult, ALU.add)
                    last.then_inc(xh1T_ready, 1)

                def finish(t):
                    dve.wait_ge(downed, t + 1)
                    dve.wait_ge(qb_used, t + 1)
                    at_least(dve, x_kept, t)
                    nc.vector.tensor_tensor(x2[:, :], k.PS[:, BANK_Y, 0:D], k.X[:, t, :], ALU.add)\
                        .then_inc(x_ready, 1)
                    dve.wait_ge(x_ready, t + 1)
                    own.then(nc.vector.bn_stats(n_stats[:, :], x2[:, :]))

                def measure_n(t):
                    nc.vector.bn_aggr(n_mean[:, :], n_stats[:, :]).then_inc(n_measured, 1)
                    dve.wait_ge(n_measured, t + 1)
                    nc.vector.tensor_scalar(n_root[:, :], n_mean[:, 1:2], EPS, None, ALU.add).then_inc(n_summed, 1)

                def normalise_n(t):
                    dve.wait_ge(n_rooted, t + 1)
                    nc.vector.tensor_scalar(k.XN[:, t, :], x2[:, :], n_mean[:, 0:1], n_root[:, 0:1],
                                            ALU.subtract, ALU.mult).then_inc(n_once, 1)

                def sum_n(t):
                    dve.wait_ge(n_squared, t + 1)
                    own.then(nc.vector.tensor_reduce(n_root2[:, :], squares[:, :], X_AXIS, ALU.add))
                    nc.vector.tensor_scalar(n_root2[:, :], n_root2[:, :], 1.0 / D, EPS, ALU.mult, ALU.add)\
                        .then_inc(n_summed2, 1)

                def weigh_n(t):
                    dve.wait_ge(n_rooted2, t + 1)
                    at_least(dve, r_turned, t)
                    at_least(dve, row_kept, t)
                    nc.vector.scalar_tensor_tensor(router_rows[:, :], k.XN[:, t, :], n_root2[:, 0:1],
                                                   k.small["nw"], ALU.mult, ALU.mult).then_inc(n_ready, 1)

                def keep_logits(t):
                    dve.wait_ge(l_made, t + 1)
                    nc.vector.tensor_tensor(k.logits1[:, t, :], k.PS[:, BANK_T, 0:E1], k.small["br1"],
                                            ALU.add).then_inc(l_ready, 1)

                def turn(s, steps, batch=0):
                    if "e" in steps:
                        keep_xh1(s - 2)
                    if "n" in steps:
                        measure_n(s - 3)
                    if "b" in steps:
                        sum_q(s)
                    if "n" in steps:
                        normalise_n(s - 3)
                    if "a" in steps:
                        normalise_again(s + 1)
                    if "c" in steps:
                        low_q(s - 1)
                    if "f" in steps:
                        low_h(s - 2, 0)
                    if "l" in steps:
                        keep_logits(s - 4)
                    if "b" in steps:
                        unit_q(s)
                    if "f" in steps:
                        low_h(s - 2, 1)
                    if "d" in steps:
                        residual(s - 1)
                    if "a" in steps:
                        keep_xh(s + 1)
                    if "n" in steps:
                        sum_n(s - 3)
                    if "d" in steps:
                        measure_x1(s - 1)
                    if "a" in steps:
                        low_xh(s + 1)
                    if "d" in steps:
                        normalise_x1(s - 1)
                    if "n" in steps:
                        weigh_n(s - 3)
                    if "g" in steps:
                        finish(s - 2)

                def counted(s, steps, batch=0):
                    if isinstance(s, int):
                        turn(s, steps, batch)
                        if s < 3:
                            prepare(s + 1)
                            dve.wait_ge(powers2, s + 2)
                    else:
                        first, turns_ = (5, TPB - 5) if batch == 0 else (TPB + 1, TPB - 2)
                        own.enter(s, first, 6)
                        turn(s, steps, batch)
                        own.leave(turns_)

                prepare(0)
                dve.wait_ge(powers2, 1)
                normalise_again(0)
                keep_xh(0)
                low_xh(0)
                turns(dve, counted)


def route1_stage(k):
    nc = k.nc
    with ExitStack() as own_memory:
        def sb(name, shape, dt=F32):
            return own_memory.enter_context(nc.sbuf_tensor(name, shape, dt))

        def sem(name):
            return k.stage_semaphore(name)

        wide3 = [P, TILES, E1]
        logits = k.logits1
        probs, first, second, both = (sb(n, wide3) for n in ("probs1", "first", "second", "both"))
        rank, work = (sb(n, wide3) for n in ("rank1", "work1"))
        earlier = sb("earlier1", [P, TILES + 1, E1])
        top, total, kept, gate_sum = (sb(n, [P, TILES]) for n in ("top1", "total1", "kept1", "gate_sum"))
        gate = sb("gate", [P, 2, TILES])
        where = sb("where", [P, 2, TILES])
        drop = sb("drop", [P, 2, TILES])
        dve_own, raising, raised = sem("dve_own"), sem("raising"), sem("raised")
        chosen, ranked, rows_known = sem("chosen"), sem("ranked"), sem("rows_known")
        scattered = [sem(f"scattered{half}") for half in range(2)]
        numbers_set = sem("numbers_set")
        with nc.Block() as block:
            @block.sync
            def _(sp):
                load_w1(k, sp, "e1", 0)
                load_w2(k, sp, "e1", 0)

            @block.tensor
            def _(pe):
                pe.wait_ge(chosen, 1)
                nc.tensor.matmul(k.PS[:, 3, 0:TILES * E1], k.small["tri"][:, :], both[:, :, :],
                                 start=True, stop=False)
                nc.tensor.matmul(k.PS[:, 3, 0:TILES * E1], k.small["ones"][:, :], earlier[:, 0:TILES, :],
                                 start=False, stop=True).then_inc(ranked, 1)

            @block.scalar
            def _(act):
                act.wait_ge(raising, 1)
                nc.scalar.activation(probs[:, :, :], probs[:, :, :], ACT.Exp).then_inc(raised, 1)

            @block.gpsimd
            def _(pool):
                pool.wait_ge(k.zeroed, 16 * (SLOT_STORES + 2 * N // (ZM * P)))
                for n in range(2):
                    pool.wait_ge(rows_known, n + 1)
                    for t in range(TILES):
                        half = t // (TILES // 2)
                        if n and t % (TILES // 2) == 0:
                            part = k.rows_out[:, t:t + TILES // 2, D]
                            pool.wait_ge(scattered[half], 16 * TILES // 2)
                            nc.gpsimd.tensor_scalar(part, part, float(N), None, ALU.add).then_inc(numbers_set, 1)
                            pool.wait_ge(numbers_set, half + 1)
                        nc.gpsimd.indirect_dma_start(
                            out=k.slots1, out_offset=bass.IndirectOffsetOnAxis(ap=k.slot1[:, n, t:t + 1], axis=0),
                            in_=k.rows_out[:, t, :], in_offset=None, bounds_check=ROWS1 - 1,
                            oob_is_err=False).then_inc(scattered[half], 16)
                for half in range(2):
                    pool.wait_ge(scattered[half], 16 * TILES)

            @block.vector
            def _(dve):
                own = Own(dve, dve_own)
                own.then(nc.vector.tensor_reduce(top[:, :], logits[:, :, :], X_AXIS, ALU.max))
                nc.vector.tensor_tensor(probs[:, :, :], logits[:, :, :], wide(top[:, :], wide3, 2),
                                        ALU.subtract).then_inc(raising, 1)
                dve.wait_ge(raising, 1)
                order = k.small["order1"][:, :]
                first_of_largest(k, own, first[:, :, :], logits[:, :, :], top[:, :], order, E1)
                own.then(nc.vector.tensor_scalar(work[:, :, :], first[:, :, :], -3e38, None, ALU.mult))
                own.then(nc.vector.tensor_tensor(logits[:, :, :], logits[:, :, :], work[:, :, :], ALU.add))
                first_of_largest(k, own, second[:, :, :], logits[:, :, :], top[:, :], order, E1)
                own.then(nc.vector.tensor_tensor(both[:, :, :], first[:, :, :], second[:, :, :], ALU.add))
                own.then(nc.vector.memset(earlier[:, 0, :], 0.0))
                running_sum(k, own, both, work, earlier[:, 1:TILES + 1, :])
                dve.sem_inc(chosen, 1)
                dve.wait_ge(ranked, 1)
                ranks = k.PS[:, 3, 0:TILES * E1].rearrange("p (t e) -> p t e", t=TILES)
                own.then(nc.vector.tensor_scalar(work[:, :, :], ranks, float(CAP), float(SKIP),
                                                 ALU.is_ge, ALU.mult))
                own.then(nc.vector.tensor_tensor(rank[:, :, :], ranks, wide(k.small["base1"], wide3, 1), ALU.add))
                own.then(nc.vector.tensor_tensor(rank[:, :, :], rank[:, :, :], work[:, :, :], ALU.add))
                for n, one_hot in enumerate((first, second)):
                    own.then(nc.vector.tensor_tensor(work[:, :, :], rank[:, :, :], one_hot[:, :, :], ALU.mult))
                    own.then(nc.vector.tensor_reduce(where[:, n, :], work[:, :, :], X_AXIS, ALU.add))
                    nc.vector.tensor_copy(k.slot1[:, n, :], where[:, n, :]).then_inc(rows_known, 1)
                dve.wait_ge(raised, 1)
                own.then(nc.vector.tensor_reduce(total[:, :], probs[:, :, :], X_AXIS, ALU.add))
                own.then(nc.vector.reciprocal(total[:, :], total[:, :]))
                own.then(nc.vector.tensor_tensor(probs[:, :, :], probs[:, :, :], wide(total[:, :], wide3, 2),
                                                 ALU.mult))
                for n, one_hot in enumerate((first, second)):
                    own.then(nc.vector.tensor_tensor(work[:, :, :], probs[:, :, :], one_hot[:, :, :], ALU.mult))
                    own.then(nc.vector.tensor_reduce(gate[:, n, :], work[:, :, :], X_AXIS, ALU.add))
                own.then(nc.vector.tensor_scalar(drop[:, :, :], where[:, :, :], float(SKIP + CAP), None,
                                                 ALU.is_ge))
                own.then(nc.vector.tensor_scalar(drop[:, :, :], drop[:, :, :], -1.0, 1.0, ALU.mult, ALU.add))
                own.then(nc.vector.tensor_tensor(gate[:, :, :], gate[:, :, :], drop[:, :, :], ALU.mult))
                own.then(nc.vector.tensor_tensor(gate_sum[:, :], gate[:, 0, :], gate[:, 1, :], ALU.add))
                own.then(nc.vector.tensor_scalar(kept[:, :], gate_sum[:, :], 0.0, None, ALU.is_le))
                own.then(nc.vector.tensor_tensor(gate_sum[:, :], gate_sum[:, :], kept[:, :], ALU.add))
                own.then(nc.vector.reciprocal(gate_sum[:, :], gate_sum[:, :]))
                own.then(nc.vector.tensor_tensor(
                    gate[:, :, :], gate[:, :, :],
                    gate_sum[:, :].rearrange("p (a t) -> p a t", a=1).to_broadcast((P, 2, TILES)), ALU.mult))
                own.then(nc.vector.tensor_tensor(first[:, :, :], first[:, :, :], wide(gate[:, 0, :], wide3, 2),
                                                 ALU.mult))
                own.then(nc.vector.tensor_tensor(second[:, :, :], second[:, :, :], wide(gate[:, 1, :], wide3, 2),
                                                 ALU.mult))
                own.then(nc.vector.tensor_tensor(k.plain[:, :, :], first[:, :, 0:PLAIN], second[:, :, 0:PLAIN],
                                                 ALU.add))
                nc.vector.tensor_copy(k.gate1[:, :, :], gate[:, :, :])
                for t in range(TILES):
                    own.then(nc.vector.scalar_tensor_tensor(k.X[:, t, :], k.XN[:, t, :], k.plain[:, t, 1:2],
                                                            k.X[:, t, :], ALU.mult, ALU.add))
                    for c in range(2):
                        own.then(nc.vector.scalar_tensor_tensor(
                            k.X[:, t, :], k.small["cv"][:, c, :], k.plain[:, t, 2 + c:3 + c], k.X[:, t, :],
                            ALU.mult, ALU.add))


def combine_stage(k):
    nc = k.nc
    with ExitStack() as own_memory:
        def sem(name):
            return k.stage_semaphore(name)

        Y = own_memory.enter_context(nc.sbuf_tensor("Y", [P, 2, TILES, D], F32))
        PART = TILES // 4
        made_in = [sem(f"made_in{q}") for q in range(4)]
        own_sem, x_ready, stored = sem("dve_own"), sem("x_ready"), sem("stored")
        with nc.Block() as block:
            @block.scalar
            def _(act):
                for q in range(4):
                    for n in range(2):
                        act.dma_start(Y[:, n, q * PART:(q + 1) * PART, :],
                                      k.made1[n * N + q * PART * P:n * N + (q + 1) * PART * P, :]
                                      .rearrange("(t p) d -> p t d", p=P)).then_inc(made_in[q], 16)

            @block.vector
            def _(dve):
                own = Own(dve, own_sem)
                for t in range(TILES):
                    dve.wait_ge(made_in[t // PART], 16 * 2)
                    own.then(nc.vector.scalar_tensor_tensor(k.X[:, t, :], Y[:, 0, t, :], k.gate1[:, 0, t:t + 1],
                                                            k.X[:, t, :], ALU.mult, ALU.add))
                    nc.vector.scalar_tensor_tensor(k.X[:, t, :], Y[:, 1, t, :], k.gate1[:, 1, t:t + 1],
                                                   k.X[:, t, :], ALU.mult, ALU.add).then_inc(x_ready, 1)

            @block.sync
            def _(sp):
                for t in range(0, TILES, 2):
                    sp.wait_ge(x_ready, t + 2)
                    sp.dma_start(k.out[t * P:(t + 2) * P, :].rearrange("(t p) d -> p t d", p=P),
                                 k.X[:, t:t + 2, :]).then_inc(stored, 16)
                sp.wait_ge(stored, 16 * TILES // 2)


def build(nc, ap, out):
    with ExitStack() as ctx:
        def sb(name, shape, dt=F32):
            return ctx.enter_context(nc.sbuf_tensor(name, shape, dt))

        def sem(name):
            return ctx.enter_context(nc.semaphore(name))

        k = Core()
        k.nc, k.ap, k.out = nc, ap, out
        k.slots0 = nc.dram_tensor("slots0", [ROWS0, D + 1], F32, kind="Internal").ap()
        k.made0 = nc.dram_tensor("made0", [N, D], F32, kind="Internal").ap()
        k.slots1 = nc.dram_tensor("slots1", [ROWS1, D + 1], F32, kind="Internal").ap()
        k.heads0 = nc.dram_tensor("heads0", [BATCH, H0, CTX, HD0], F32, kind="Internal").ap()
        k.made1 = nc.dram_tensor("made1", [2 * N, D], F32, kind="Internal").ap()
        k.X = sb("X", [P, TILES, D])
        k.rows_out = sb("rows_out", [P, TILES, D + 1])
        k.XN = k.rows_out[:, :, 0:D]
        k.zeros = sb("zeros", [P, ZM, D + 1])
        k.zeroed = sem("zeroed")
        k.stats = sb("stats", [P, TILES, 6])
        k.mv = sb("mv", [P, TILES, 2])
        k.rstd = sb("rstd", [P, TILES])
        k.half_neg = sb("half_neg", [P, H1 * 4])
        k.half_pos = sb("half_pos", [P, H1 * 4])
        k.keyval1 = sb("keyval1", [P, BATCH, IC, D])
        k.plain_pack = sb("plain_pack", [P, PLAIN_WIDTH])
        k.spread_pack = sb("spread_pack", [P, SPREAD_WIDTH])
        k.small, at = {}, {True: 0, False: 0}
        for name, shape in SMALL:
            spread, width = name in BROADCAST, math.prod(shape[1:])
            part = (k.spread_pack if spread else k.plain_pack)[:, at[spread]:at[spread] + width]
            at[spread] += width
            k.small[name] = part if len(shape) == 2 else part.rearrange("p (a b) -> p a b", a=shape[1])
        k.ident = k.small["ident"]
        k.PS = ctx.enter_context(nc.psum_tensor("PS", [P, 8, 512], F32))
        k.w1_sb, k.w2_sb = sb("w1_sb", [P, KC, F]), sb("w2_sb", [P, FC, D])
        k.weights_in = {layer: (sem(f"{layer}_w1_in"), sem(f"{layer}_w2_in")) for layer in ("e0", "e1")}
        k.slot0 = sb("slot0", [P, TILES], U32)
        k.expert0 = sb("expert0", [P, SLOT_TILES0], I32)
        with ExitStack() as keyval:
            def sb_kv(name, shape):
                return keyval.enter_context(nc.sbuf_tensor(name, shape, F32))
            k.cnT = sb_kv("cnT", [P, KC, BATCH, CTX])
            k.wk1, k.wv1 = sb_kv("wk1", [P, KC, INNER]), sb_kv("wv1", [P, KC, INNER])
            k.wo1 = sb_kv("wo1", [P, IC, D])
            k.kv_w_in = keyval.enter_context(nc.semaphore("kv_w_in"))
            with ExitStack() as first:
                def sb1(name, shape):
                    return first.enter_context(nc.sbuf_tensor(name, shape, F32))
                k.keys0 = [first.enter_context(nc.sbuf_tensor(
                    f"keys0_{part}", [P, BATCH, HALVES, HALF_HEADS, CTX], F32R)) for part in PARTS]
                k.kT_parts = [first.enter_context(nc.sbuf_tensor(
                    f"kT_{part}", [P, BATCH, HALVES, CTX], F32R)) for part in PARTS]
                k.values0 = sb1("values0", [P, BATCH, HALVES, CHUNKS, 2, VW])
                k.probs = sb1("probs", [P, HALVES, PADDED])
                k.wq0 = sb1("wq0", [P, KC, D])
                k.wo0 = sb1("wo0", [P, KC, D])
                k.w0_in = sem("attention0_w_in")
                context_stage(k)
                attention0_stage(k)
            route0_stage(k)
        experts_stage(k, "e0", SLOT_TILES0, k.slots0, k.made0,
                      lambda eng, tile: expert_of_tile(k, eng, tile))
        k.logits1 = sb("logits1", [P, TILES, E1])
        attention1_stage(k)
        k.slot1 = sb("slot1", [P, 2, TILES], U32)
        k.gate1 = sb("gate1", [P, 2, TILES])
        k.plain = sb("plain", [P, TILES, PLAIN])
        route1_stage(k)
        experts_stage(k, "e1", MLPS, k.slots1, k.made1, lambda eng, tile: tile)
        combine_stage(k)


def kernel(**inputs):
    import numpy as np
    import concourse.bacc as bacc
    from concourse.bass_utils import run_bass_kernel_spmd

    laid = lay_out(inputs)
    nc = bacc.Bacc("TRN2", target_bir_lowering=False, num_devices=1)
    ap, arrays = {}, {}
    for name, a in laid.items():
        arrays[f"in_{name}"] = a
        ap[name] = nc.dram_tensor(f"in_{name}", a.shape, mybir.dt.from_np(a.dtype), kind="ExternalInput").ap()
    out = nc.dram_tensor("out_0", [N, D], F32, kind="ExternalOutput").ap()
    build(nc, ap, out)
    r = run_bass_kernel_spmd(nc, [arrays], core_ids=[0])
    return r.results[0]["out_0"].reshape(BATCH, SEQ, D)


def lay_out(inputs):
    import numpy as np
    g = {n: np.asarray(a) for n, a in inputs.items()}

    def rows(w):
        return np.ascontiguousarray(w.reshape(w.shape[0] // P, P, *w.shape[1:]).swapaxes(0, 1))

    def f32(a):
        return np.ascontiguousarray(a, dtype=np.float32)

    ctx = g["ctx_1024"]
    ctxT = ctx.transpose(2, 0, 1)
    pad = np.zeros((BATCH, 2 * P, D), ctx.dtype)
    pad[:, :CTX] = ctx
    row = np.arange(PADDED).reshape(CHUNKS, P).T
    head = np.where(row < ROWS, row // CTX, -1)
    part = np.arange(P)
    e8, e16 = np.arange(E0), np.arange(E1)
    laid = {
        "x": g["x"].reshape(N, D),
        "ctx": pad.reshape(BATCH, 2, P, D).transpose(2, 0, 1, 3),
        "ctxT": rows(ctxT),
        "wq0": rows(g["L0_xattn_Wq"]), "wk0": rows(g["L0_xattn_Wk"]), "wo0": rows(g["L0_xattn_Wo"]),
        "wv0": rows(g["L0_xattn_Wv"]),
        "bq0": g["L0_xattn_bq"].reshape(KC, P).T, "bk0": g["L0_xattn_bk"].reshape(KC, P).T,
        "bv0": g["L0_xattn_bv"].reshape(1, D), "bo0": g["L0_xattn_bo"].reshape(1, D),
        "vmask": f32(head[:, :, None] == np.array(PAIR0)[None, :, None] + np.arange(2)),
        "headmask": f32(part[:, None] // HD0 == np.arange(HALF_HEADS)),
        "pairmask": f32(part[:, None] // HD1 == part[None, :] // HD1),
        "wk1": rows(g["L1_xattn_wk"]), "wv1": rows(g["L1_xattn_wv"]), "wq1": rows(g["L1_xattn_wq"]),
        "wo1": rows(g["L1_xattn_wo"]),
        "g1": g["L1_xattn_ln1_g"].reshape(KC, P).T, "be1": g["L1_xattn_ln1_b"].reshape(KC, P).T,
        "g2": g["L1_xattn_ln2_g"].reshape(KC, P).T, "be2": g["L1_xattn_ln2_b"].reshape(KC, P).T,
        "bo1": g["L1_xattn_bo"].reshape(1, D), "mb2": g["L1_xattn_b2"].reshape(1, D),
        "mb1": g["L1_xattn_b1"].reshape(FC, P).T,
        "mw1": rows(g["L1_xattn_w1"]), "mw2": rows(g["L1_xattn_w2"]),
        "wr0": rows(g["L0_ffn_wr"]), "br0": g["L0_ffn_br"].reshape(1, E0),
        "wr1": rows(g["L1_ffn_router_weight"].T), "br1": g["L1_ffn_router_bias"].reshape(1, E1),
        "nw": g["L1_ffn_norm_weight"].reshape(1, D), "cv": g["L1_ffn_constant_vectors"].reshape(1, 2 * D),
        "e0w1": g["L0_ffn_w1"].reshape(E0, KC, P, F).transpose(0, 2, 1, 3),
        "e0w2": g["L0_ffn_w2"].reshape(E0, FC, P, D).transpose(0, 2, 1, 3),
        "e0b1": g["L0_ffn_b1"].reshape(E0, FC, P).transpose(0, 2, 1), "e0b2": g["L0_ffn_b2"],
        "e1w1": g["L1_ffn_fc1_weight"].transpose(0, 2, 1).reshape(MLPS, KC, P, F).transpose(0, 2, 1, 3),
        "e1w2": g["L1_ffn_fc2_weight"].transpose(0, 2, 1).reshape(MLPS, FC, P, D).transpose(0, 2, 1, 3),
        "e1b1": g["L1_ffn_fc1_bias"].reshape(MLPS, FC, P).transpose(0, 2, 1), "e1b2": g["L1_ffn_fc2_bias"],
        "tri": f32(part[:, None] < part[None, :]), "ones": np.ones((P, P), np.float32),
        "ident": np.eye(P, dtype=np.float32),
        "token_no": f32(part[:, None] + P * np.arange(TILES)),
        "order0": f32(E0 - e8)[None], "order1": f32(E1 - e16)[None],
        "thresh0": f32(W * np.arange(N // W))[None],
        "before0": f32(e8[None, :] < e8[:, None]).reshape(1, -1),
        "tile_no": f32(np.arange(SLOT_TILES0))[None],
        "base1": f32(np.where(e16 < PLAIN, SKIP, (e16 - PLAIN) * CAP))[None],
    }
    small = {name: laid.pop(name) for name, _ in SMALL}
    laid["plain_pack"] = np.concatenate([a.reshape(P, -1) for n, a in small.items() if n not in BROADCAST], 1)
    laid["spread_pack"] = np.concatenate([a.reshape(1, -1) for n, a in small.items() if n in BROADCAST], 1)
    return {name: np.ascontiguousarray(a) for name, a in laid.items()}
```
